# Optimizing a Trainium2 kernel written in Bass

```python
import numpy as np
import jax
import jax.numpy as jnp

def _softmax(x, axis=-1):
    return jax.nn.softmax(x, axis=axis)

def _gelu(x):
    return jax.nn.gelu(x, approximate=True)

def _silu(x):
    return jax.nn.silu(x)

def _sigmoid(x):
    return jax.nn.sigmoid(x)

def _layernorm(x, axis=-1, eps=1e-05):
    m = jnp.mean(x, axis=axis, keepdims=True)
    v = jnp.var(x, axis=axis, keepdims=True)
    return (x - m) / jnp.sqrt(v + eps)

def _scatter_add(tgt, idx, src, axis=0):
    return tgt.at[idx].add(src)

def _segment_sum(src, seg, n):
    return jax.ops.segment_sum(src, seg, n)
kernel_name = 'mk_prb_d2_jaxref_r4_c920f0'

def setup_inputs(seed: int=0):
    np.random.seed(seed)
    _w = jnp.asarray

    def _L0_attn_setup():
        import jax, jax.numpy as jnp
        import numpy as np
        from jax import lax
        D_MODEL = 256
        D_STATE = 16
        D_CONV = 4
        EXPAND = 2
        D_INNER = D_MODEL * EXPAND
        DT_RANK = (D_MODEL + 15) // 16
        B_SZ, L_SEQ = (4, 512)
        key = jax.random.key(seed)
        ks = jax.random.split(key, 8)
        s = 0.02
        x = jax.random.normal(ks[0], (B_SZ, L_SEQ, D_MODEL), jnp.float32)
        W_in = jax.random.normal(ks[1], (2 * D_INNER, D_MODEL), jnp.float32) * s
        conv_w = jax.random.normal(ks[2], (D_INNER, 1, D_CONV), jnp.float32) * 0.2
        conv_b = jax.random.normal(ks[3], (D_INNER,), jnp.float32) * 0.01
        W_xproj = jax.random.normal(ks[4], (DT_RANK + 2 * D_STATE, D_INNER), jnp.float32) * s
        W_dt = jax.random.normal(ks[5], (D_INNER, DT_RANK), jnp.float32) * s
        b_dt = jax.random.normal(ks[6], (D_INNER,), jnp.float32) * 0.01
        A_log = jnp.log(jnp.broadcast_to(jnp.arange(1, D_STATE + 1, dtype=jnp.float32), (D_INNER, D_STATE)))
        D_param = jnp.ones((D_INNER,), jnp.float32)
        W_out = jax.random.normal(ks[7], (D_MODEL, D_INNER), jnp.float32) * s
        return {'x': x, 'W_in': W_in, 'conv_w': conv_w, 'conv_b': conv_b, 'W_xproj': W_xproj, 'W_dt': W_dt, 'b_dt': b_dt, 'A_log': A_log, 'D_param': D_param, 'W_out': W_out}
    _L0_attn_in = _L0_attn_setup()

    def _L0_ffn_setup():
        import jax, jax.numpy as jnp
        import numpy as np
        BLOCK = 16
        _GRID = jnp.array([0.0, 0.5, 1.0, 1.5, 2.0, 3.0, 4.0, 6.0], dtype=jnp.float32)
        _MID = jnp.array([0.25, 0.75, 1.25, 1.75, 2.5, 3.5, 5.0], dtype=jnp.float32)

        def fp4_quant_dequant(x):
            shape = x.shape
            xb = x.reshape(shape[:-1] + (shape[-1] // BLOCK, BLOCK))
            scale = jnp.max(jnp.abs(xb), axis=-1, keepdims=True) / 6.0
            scale = jnp.maximum(scale, jnp.float32(1e-12))
            xn = xb / scale
            idx = jnp.searchsorted(_MID, jnp.abs(xn))
            q = _GRID[idx] * jnp.sign(xn) * scale
            return q.reshape(shape)

        def fp4_linear(x, w):
            xq = fp4_quant_dequant(x)
            wq = fp4_quant_dequant(w)
            return jnp.einsum('bsk,nk->bsn', xq, wq)
        key = jax.random.key(seed)
        k1, k2, k3, k4 = jax.random.split(key, 4)
        H, I = (256, 704)
        x = jax.random.normal(k1, (4, 1024, H), dtype=jnp.float32)
        w_gate = jax.random.normal(k2, (I, H), dtype=jnp.float32) * 0.02
        w_up = jax.random.normal(k3, (I, H), dtype=jnp.float32) * 0.02
        w_down = jax.random.normal(k4, (H, I), dtype=jnp.float32) * 0.02
        return {'x': x, 'w_gate': w_gate, 'w_up': w_up, 'w_down': w_down}
    _L0_ffn_in = _L0_ffn_setup()

    def _L1_attn_setup():
        import jax, jax.numpy as jnp
        import numpy as np
        EMBED_DIM = 256
        NUM_HEADS = 16
        BLOCK_SIZE = 128
        GLOBAL_EVERY = 24

        def make_block_sparse_mask(seq_len):
            bi = jnp.arange(seq_len) // BLOCK_SIZE
            is_global = bi % GLOBAL_EVERY == 0
            allowed = (bi[:, None] == bi[None, :]) | is_global[:, None] | is_global[None, :]
            return jnp.where(allowed, 0.0, -jnp.inf).astype(jnp.float32)
        key = jax.random.key(seed)
        k_x, k_w, k_wo = jax.random.split(key, 3)
        B, L, D = (1, 1024, EMBED_DIM)
        x = jax.random.normal(k_x, (B, L, D), dtype=jnp.float32)
        w_qkv = jax.random.normal(k_w, (3 * D, D), dtype=jnp.float32) * 0.02
        b_qkv = jnp.zeros((3 * D,), dtype=jnp.float32)
        w_out = jax.random.normal(k_wo, (D, D), dtype=jnp.float32) * 0.02
        b_out = jnp.zeros((D,), dtype=jnp.float32)
        return {'x': x, 'w_qkv': w_qkv, 'b_qkv': b_qkv, 'w_out': w_out, 'b_out': b_out}
    _L1_attn_in = _L1_attn_setup()

    def _L1_ffn_setup():
        import jax, jax.numpy as jnp
        import numpy as np
        DIM = 256
        DEPTH = 2
        HEADS = 8
        DIM_HEAD = 64
        WINDOW = 128
        INNER = HEADS * DIM_HEAD
        HID = int(DIM * 4 * 2 / 3)
        B, N = (2, 2048)
        QK_SCALE = 8.0

        def shift_token(t):
            t1, t2 = jnp.split(t, 2, axis=-1)
            t2 = jnp.pad(t2, ((0, 0), (1, 0), (0, 0)))[:, :-1]
            return jnp.concatenate([t1, t2], axis=-1)

        def l2norm(t):
            return t / jnp.clip(jnp.linalg.norm(t, axis=-1, keepdims=True), 1e-12)

        def rotate_half(x):
            x1, x2 = jnp.split(x, 2, axis=-1)
            return jnp.concatenate([-x2, x1], axis=-1)

        def rotary_xpos(q, k):
            n = q.shape[-2]
            half_idx = jnp.arange(0, DIM_HEAD, 2, dtype=jnp.float32)
            inv_freq = 1.0 / 10000.0 ** (half_idx / DIM_HEAD)
            t = jnp.arange(n, dtype=jnp.float32)
            freqs = t[:, None] * inv_freq[None, :]
            freqs = jnp.concatenate([freqs, freqs], axis=-1)
            base = (half_idx + 0.4 * DIM_HEAD) / (1.4 * DIM_HEAD)
            power = (t - n // 2) / float(WINDOW // 2)
            scale = base[None, :] ** power[:, None]
            scale = jnp.concatenate([scale, scale], axis=-1)
            cos, sin = (jnp.cos(freqs), jnp.sin(freqs))
            q = q * cos * scale + rotate_half(q) * sin * scale
            k = k * cos / scale + rotate_half(k) * sin / scale
            return (q, k)

        def local_attention(q, k, v):
            b, h, n, d = q.shape
            w = n // WINDOW
            bq = q.reshape(b, h, w, WINDOW, d) * QK_SCALE
            bk = k.reshape(b, h, w, WINDOW, d)
            bv = v.reshape(b, h, w, WINDOW, d)

            def look_around(t):
                p = jnp.pad(t, ((0, 0), (0, 0), (1, 0), (0, 0), (0, 0)))
                return jnp.concatenate([p[:, :, :w], p[:, :, 1:]], axis=3)
            bk, bv = (look_around(bk), look_around(bv))
            bt = jnp.arange(n).reshape(w, WINDOW)
            btp = jnp.pad(bt, ((1, 0), (0, 0)), constant_values=-1)
            btk = jnp.concatenate([btp[:w], btp[1:]], axis=1)
            sim = jnp.einsum('bhwid,bhwjd->bhwij', bq, bk)
            i = bt[:, :, None]
            j = btk[:, None, :]
            mask = (i < j) | (i > j + WINDOW) | (j == -1)
            sim = jnp.where(mask, -jnp.finfo(sim.dtype).max, sim)
            attn = jax.nn.softmax(sim, axis=-1)
            out = jnp.einsum('bhwij,bhwjd->bhwid', attn, bv)
            return out.reshape(b, h, n, d)

        def _layer(x, wqkv, qs, ksc, wo, lg, lb, w1, b1, w2, b2):
            b, n, _ = x.shape
            h = shift_token(x)
            qkv = h @ wqkv
            q, k, v = jnp.split(qkv, 3, axis=-1)
            to_heads = lambda t: t.reshape(b, n, HEADS, DIM_HEAD).transpose(0, 2, 1, 3)
            q, k, v = (to_heads(q), to_heads(k), to_heads(v))
            q = l2norm(q) * qs
            k = l2norm(k) * ksc
            q, k = rotary_xpos(q, k)
            o = local_attention(q, k, v)
            o = o.transpose(0, 2, 1, 3).reshape(b, n, INNER)
            x = x + o @ wo
            h = shift_token(x)
            mu = h.mean(-1, keepdims=True)
            var = h.var(-1, keepdims=True)
            h = (h - mu) / jnp.sqrt(var + 1e-05) * lg + lb
            h = h @ w1 + b1
            a, g = jnp.split(h, 2, axis=-1)
            h = a * jax.nn.gelu(g, approximate=False)
            x = x + h @ w2 + b2
            return x
        key = jax.random.key(seed)
        ks = jax.random.split(key, 6)
        return {'x': jax.random.normal(ks[0], (B, N, DIM), jnp.float32), 'wqkv': jax.random.normal(ks[1], (DEPTH, DIM, 3 * INNER), jnp.float32) * 0.02, 'q_scale': jnp.ones((DEPTH, DIM_HEAD), jnp.float32), 'k_scale': jnp.ones((DEPTH, DIM_HEAD), jnp.float32), 'wo': jax.random.normal(ks[2], (DEPTH, INNER, DIM), jnp.float32) * 0.02, 'ln_g': jnp.ones((DEPTH, DIM), jnp.float32), 'ln_b': jnp.zeros((DEPTH, DIM), jnp.float32), 'w1': jax.random.normal(ks[3], (DEPTH, DIM, 2 * HID), jnp.float32) * 0.02, 'b1': jnp.zeros((DEPTH, 2 * HID), jnp.float32), 'w2': jax.random.normal(ks[4], (DEPTH, HID, DIM), jnp.float32) * 0.02, 'b2': jnp.zeros((DEPTH, DIM), jnp.float32)}
    _L1_ffn_in = _L1_ffn_setup()
    _d = {'L0_attn_x': _L0_attn_in['x'], 'L0_attn_W_in': _L0_attn_in['W_in'], 'L0_attn_conv_w': _L0_attn_in['conv_w'], 'L0_attn_conv_b': _L0_attn_in['conv_b'], 'L0_attn_W_xproj': _L0_attn_in['W_xproj'], 'L0_attn_W_dt': _L0_attn_in['W_dt'], 'L0_attn_b_dt': _L0_attn_in['b_dt'], 'L0_attn_A_log': _L0_attn_in['A_log'], 'L0_attn_D_param': _L0_attn_in['D_param'], 'L0_attn_W_out': _L0_attn_in['W_out'], 'L0_ffn_w_gate': _L0_ffn_in['w_gate'], 'L0_ffn_w_up': _L0_ffn_in['w_up'], 'L0_ffn_w_down': _L0_ffn_in['w_down'], 'L1_attn_w_qkv': _L1_attn_in['w_qkv'], 'L1_attn_b_qkv': _L1_attn_in['b_qkv'], 'L1_attn_w_out': _L1_attn_in['w_out'], 'L1_attn_b_out': _L1_attn_in['b_out'], 'L1_ffn_wqkv': _L1_ffn_in['wqkv'], 'L1_ffn_q_scale': _L1_ffn_in['q_scale'], 'L1_ffn_k_scale': _L1_ffn_in['k_scale'], 'L1_ffn_wo': _L1_ffn_in['wo'], 'L1_ffn_ln_g': _L1_ffn_in['ln_g'], 'L1_ffn_ln_b': _L1_ffn_in['ln_b'], 'L1_ffn_w1': _L1_ffn_in['w1'], 'L1_ffn_b1': _L1_ffn_in['b1'], 'L1_ffn_w2': _L1_ffn_in['w2'], 'L1_ffn_b2': _L1_ffn_in['b2']}
    _x0 = _d['L0_attn_x']
    _d['L0_attn_x'] = jax.random.normal(jax.random.fold_in(jax.random.key(seed), 1), (8, 512, 256), dtype=_x0.dtype)
    del _x0
    return _d

def reference(L0_attn_x, L0_attn_W_in, L0_attn_conv_w, L0_attn_conv_b, L0_attn_W_xproj, L0_attn_W_dt, L0_attn_b_dt, L0_attn_A_log, L0_attn_D_param, L0_attn_W_out, L0_ffn_w_gate, L0_ffn_w_up, L0_ffn_w_down, L1_attn_w_qkv, L1_attn_b_qkv, L1_attn_w_out, L1_attn_b_out, L1_ffn_wqkv, L1_ffn_q_scale, L1_ffn_k_scale, L1_ffn_wo, L1_ffn_ln_g, L1_ffn_ln_b, L1_ffn_w1, L1_ffn_b1, L1_ffn_w2, L1_ffn_b2):

    def _L0_attn_ref(x, W_in, conv_w, conv_b, W_xproj, W_dt, b_dt, A_log, D_param, W_out):
        import jax, jax.numpy as jnp
        import numpy as np
        from jax import lax
        D_MODEL = 256
        D_STATE = 16
        D_CONV = 4
        EXPAND = 2
        D_INNER = D_MODEL * EXPAND
        DT_RANK = (D_MODEL + 15) // 16
        B_SZ, L_SEQ = (4, 512)
        B, L, _ = x.shape
        d_inner, d_state = A_log.shape
        dt_rank = W_dt.shape[1]
        k = conv_w.shape[-1]
        xz = jnp.einsum('bld,ed->ble', x, W_in)
        x_in, z = (xz[..., :d_inner], xz[..., d_inner:])
        xt = x_in.transpose(0, 2, 1)
        xc = lax.conv_general_dilated(xt, conv_w, (1,), [(k - 1, 0)], feature_group_count=d_inner)
        xc = xc + conv_b[None, :, None]
        xc = jax.nn.silu(xc)
        u = xc.transpose(0, 2, 1)
        x_dbl = jnp.einsum('bld,ed->ble', u, W_xproj)
        delta_raw = x_dbl[..., :dt_rank]
        B_ssm = x_dbl[..., dt_rank:dt_rank + d_state]
        C_ssm = x_dbl[..., dt_rank + d_state:]
        delta = jax.nn.softplus(jnp.einsum('blr,dr->bld', delta_raw, W_dt) + b_dt)
        A = -jnp.exp(A_log)

        def step(h, inp):
            d_t, u_t, B_t, C_t = inp
            dA = jnp.exp(d_t[:, :, None] * A[None])
            h = dA * h + (d_t * u_t)[:, :, None] * B_t[:, None, :]
            y_t = jnp.einsum('bdn,bn->bd', h, C_t)
            return (h, y_t)
        h0 = jnp.zeros((B, d_inner, d_state), x.dtype)
        xs = (delta.transpose(1, 0, 2), u.transpose(1, 0, 2), B_ssm.transpose(1, 0, 2), C_ssm.transpose(1, 0, 2))
        _, ys = lax.scan(step, h0, xs)
        y = ys.transpose(1, 0, 2) + D_param * u
        y = y * jax.nn.silu(z)
        return jnp.einsum('bld,ed->ble', y, W_out)

    def _L0_ffn_ref(x, w_gate, w_up, w_down):
        import jax, jax.numpy as jnp
        import numpy as np
        BLOCK = 16
        _GRID = jnp.array([0.0, 0.5, 1.0, 1.5, 2.0, 3.0, 4.0, 6.0], dtype=jnp.float32)
        _MID = jnp.array([0.25, 0.75, 1.25, 1.75, 2.5, 3.5, 5.0], dtype=jnp.float32)

        def fp4_quant_dequant(x):
            shape = x.shape
            xb = x.reshape(shape[:-1] + (shape[-1] // BLOCK, BLOCK))
            scale = jnp.max(jnp.abs(xb), axis=-1, keepdims=True) / 6.0
            scale = jnp.maximum(scale, jnp.float32(1e-12))
            xn = xb / scale
            idx = jnp.searchsorted(_MID, jnp.abs(xn))
            q = _GRID[idx] * jnp.sign(xn) * scale
            return q.reshape(shape)

        def fp4_linear(x, w):
            xq = fp4_quant_dequant(x)
            wq = fp4_quant_dequant(w)
            return jnp.einsum('bsk,nk->bsn', xq, wq)
        gate = fp4_linear(x, w_gate)
        y = fp4_linear(x, w_up)
        h = jax.nn.silu(gate) * y
        return fp4_linear(h, w_down)

    def _L1_attn_ref(x, w_qkv, b_qkv, w_out, b_out):
        import jax, jax.numpy as jnp
        import numpy as np
        EMBED_DIM = 256
        NUM_HEADS = 16
        BLOCK_SIZE = 128
        GLOBAL_EVERY = 24

        def make_block_sparse_mask(seq_len):
            bi = jnp.arange(seq_len) // BLOCK_SIZE
            is_global = bi % GLOBAL_EVERY == 0
            allowed = (bi[:, None] == bi[None, :]) | is_global[:, None] | is_global[None, :]
            return jnp.where(allowed, 0.0, -jnp.inf).astype(jnp.float32)
        B, L, D = x.shape
        H = NUM_HEADS
        hd = D // H
        mask = make_block_sparse_mask(L)
        qkv = x @ w_qkv.T + b_qkv
        q, k, v = jnp.split(qkv, 3, axis=-1)
        q = q.reshape(B, L, H, hd).transpose(0, 2, 1, 3)
        k = k.reshape(B, L, H, hd).transpose(0, 2, 1, 3)
        v = v.reshape(B, L, H, hd).transpose(0, 2, 1, 3)
        scale = 1.0 / jnp.sqrt(jnp.asarray(hd, dtype=x.dtype))
        scores = jnp.einsum('bhqd,bhkd->bhqk', q * scale, k) + mask
        attn = jax.nn.softmax(scores, axis=-1)
        out = jnp.einsum('bhqk,bhkd->bhqd', attn, v)
        out = out.transpose(0, 2, 1, 3).reshape(B, L, D)
        return out @ w_out.T + b_out

    def _L1_ffn_ref(x, wqkv, q_scale, k_scale, wo, ln_g, ln_b, w1, b1, w2, b2):
        import jax, jax.numpy as jnp
        import numpy as np
        DIM = 256
        DEPTH = 2
        HEADS = 8
        DIM_HEAD = 64
        WINDOW = 128
        INNER = HEADS * DIM_HEAD
        HID = int(DIM * 4 * 2 / 3)
        B, N = (2, 2048)
        QK_SCALE = 8.0

        def shift_token(t):
            t1, t2 = jnp.split(t, 2, axis=-1)
            t2 = jnp.pad(t2, ((0, 0), (1, 0), (0, 0)))[:, :-1]
            return jnp.concatenate([t1, t2], axis=-1)

        def l2norm(t):
            return t / jnp.clip(jnp.linalg.norm(t, axis=-1, keepdims=True), 1e-12)

        def rotate_half(x):
            x1, x2 = jnp.split(x, 2, axis=-1)
            return jnp.concatenate([-x2, x1], axis=-1)

        def rotary_xpos(q, k):
            n = q.shape[-2]
            half_idx = jnp.arange(0, DIM_HEAD, 2, dtype=jnp.float32)
            inv_freq = 1.0 / 10000.0 ** (half_idx / DIM_HEAD)
            t = jnp.arange(n, dtype=jnp.float32)
            freqs = t[:, None] * inv_freq[None, :]
            freqs = jnp.concatenate([freqs, freqs], axis=-1)
            base = (half_idx + 0.4 * DIM_HEAD) / (1.4 * DIM_HEAD)
            power = (t - n // 2) / float(WINDOW // 2)
            scale = base[None, :] ** power[:, None]
            scale = jnp.concatenate([scale, scale], axis=-1)
            cos, sin = (jnp.cos(freqs), jnp.sin(freqs))
            q = q * cos * scale + rotate_half(q) * sin * scale
            k = k * cos / scale + rotate_half(k) * sin / scale
            return (q, k)

        def local_attention(q, k, v):
            b, h, n, d = q.shape
            w = n // WINDOW
            bq = q.reshape(b, h, w, WINDOW, d) * QK_SCALE
            bk = k.reshape(b, h, w, WINDOW, d)
            bv = v.reshape(b, h, w, WINDOW, d)

            def look_around(t):
                p = jnp.pad(t, ((0, 0), (0, 0), (1, 0), (0, 0), (0, 0)))
                return jnp.concatenate([p[:, :, :w], p[:, :, 1:]], axis=3)
            bk, bv = (look_around(bk), look_around(bv))
            bt = jnp.arange(n).reshape(w, WINDOW)
            btp = jnp.pad(bt, ((1, 0), (0, 0)), constant_values=-1)
            btk = jnp.concatenate([btp[:w], btp[1:]], axis=1)
            sim = jnp.einsum('bhwid,bhwjd->bhwij', bq, bk)
            i = bt[:, :, None]
            j = btk[:, None, :]
            mask = (i < j) | (i > j + WINDOW) | (j == -1)
            sim = jnp.where(mask, -jnp.finfo(sim.dtype).max, sim)
            attn = jax.nn.softmax(sim, axis=-1)
            out = jnp.einsum('bhwij,bhwjd->bhwid', attn, bv)
            return out.reshape(b, h, n, d)

        def _layer(x, wqkv, qs, ksc, wo, lg, lb, w1, b1, w2, b2):
            b, n, _ = x.shape
            h = shift_token(x)
            qkv = h @ wqkv
            q, k, v = jnp.split(qkv, 3, axis=-1)
            to_heads = lambda t: t.reshape(b, n, HEADS, DIM_HEAD).transpose(0, 2, 1, 3)
            q, k, v = (to_heads(q), to_heads(k), to_heads(v))
            q = l2norm(q) * qs
            k = l2norm(k) * ksc
            q, k = rotary_xpos(q, k)
            o = local_attention(q, k, v)
            o = o.transpose(0, 2, 1, 3).reshape(b, n, INNER)
            x = x + o @ wo
            h = shift_token(x)
            mu = h.mean(-1, keepdims=True)
            var = h.var(-1, keepdims=True)
            h = (h - mu) / jnp.sqrt(var + 1e-05) * lg + lb
            h = h @ w1 + b1
            a, g = jnp.split(h, 2, axis=-1)
            h = a * jax.nn.gelu(g, approximate=False)
            x = x + h @ w2 + b2
            return x
        for l in range(DEPTH):
            x = _layer(x, wqkv[l], q_scale[l], k_scale[l], wo[l], ln_g[l], ln_b[l], w1[l], b1[l], w2[l], b2[l])
        return x
    x = L0_attn_x
    xn = _layernorm(x, axis=-1)
    x = x + _L0_attn_ref(xn, L0_attn_W_in, L0_attn_conv_w, L0_attn_conv_b, L0_attn_W_xproj, L0_attn_W_dt, L0_attn_b_dt, L0_attn_A_log, L0_attn_D_param, L0_attn_W_out) + _L0_ffn_ref(xn, L0_ffn_w_gate, L0_ffn_w_up, L0_ffn_w_down)
    xn = _layernorm(x, axis=-1)
    x = x + _L1_attn_ref(xn, L1_attn_w_qkv, L1_attn_b_qkv, L1_attn_w_out, L1_attn_b_out) + _L1_ffn_ref(xn, L1_ffn_wqkv, L1_ffn_q_scale, L1_ffn_k_scale, L1_ffn_wo, L1_ffn_ln_g, L1_ffn_ln_b, L1_ffn_w1, L1_ffn_b1, L1_ffn_w2, L1_ffn_b2)
    return x

_drawn_inputs = setup_inputs


def setup_inputs(seed=0):
    import zlib

    import numpy as np

    out = dict(_drawn_inputs(seed))
    spreads = {'L0_attn_D_param': (1.0, 0.2),
     'L1_attn_b_qkv': (0.0, 0.1),
     'L1_attn_b_out': (0.0, 0.1),
     'L1_ffn_q_scale': (1.0, 0.2),
     'L1_ffn_k_scale': (1.0, 0.2),
     'L1_ffn_ln_g': (1.0, 0.2),
     'L1_ffn_ln_b': (0.0, 0.1),
     'L1_ffn_b1': (0.0, 0.1),
     'L1_ffn_b2': (0.0, 0.1)}
    factors = {}
    for name, (base, spread) in spreads.items():
        noise = np.random.default_rng([zlib.crc32(name.encode()), seed]).standard_normal(out[name].shape)
        drawn = base * np.exp(spread * noise) if base else spread * noise
        out[name] = jnp.asarray(drawn.astype(out[name].dtype))
    for name, factor in factors.items():
        out[name] = (out[name] * factor).astype(out[name].dtype)
    return out
```

```python
from contextlib import ExitStack

import numpy as np

import concourse.bass as bass
from concourse import mybir

ALU = mybir.AluOpType
ACT = mybir.ActivationFunctionType
F32 = mybir.dt.float32
BF16 = mybir.dt.bfloat16
U32 = mybir.dt.uint32
AX = mybir.AxisListType

P = 128
SIGN_BIT = 0x80000000
LN_EPS = 1e-5


class Sem:

    def __init__(self, ctx, nc, name, per):
        self.s = ctx.enter_context(nc.semaphore(name))
        self.per = per

    def at(self, it, k):
        assert 0 <= k <= self.per, (k, self.per)
        return it * self.per + k + 1


def seed(nc, sems):
    with nc.Block() as block:
        @block.gpsimd
        def _(pool):
            for sem in sems:
                pool.sem_inc(sem.s, 1)


class Steps:

    def __init__(self, sem, eng):
        self.sem, self.s, self.eng, self.it, self.k = sem, sem.s, eng, 0, 0

    def turn(self, it):
        self.it, self.k = it, 0

    def at(self, k):
        return self.sem.at(self.it, k)

    def done(self, ins):
        ins.then_inc(self.s, 1)
        self.k += 1
        return self.k

    def link(self, ins):
        self.eng.wait_ge(self.s, self.at(self.done(ins)))

    def end(self):
        assert self.k == self.sem.per, (self.s, self.k, self.sem.per)


def bc(ap, shape):
    return ap.broadcast_to(shape)


def fp4_steps(dve, st, src, out, blk, work, p, n):
    g = n // 16
    amax, scale, inv = blk[0:p, 0, 0:g], blk[0:p, 1, 0:g], blk[0:p, 2, 0:g]
    a, s, w = work[0:p, 0, 0:n], work[0:p, 1, 0:n], work[0:p, 2, 0:n]

    def blocks(ap):
        return ap.rearrange("p (g e) -> p g e", e=16)

    st.link(dve.tensor_reduce(amax, blocks(src), AX.X, ALU.max, apply_absolute_value=True))
    st.link(dve.tensor_scalar(scale, amax, 1.0 / 6.0, 1e-12, ALU.mult, ALU.max))
    st.link(dve.reciprocal(inv, scale))
    st.link(dve.tensor_tensor(blocks(a), blocks(src), bc(inv.unsqueeze(2), [p, g, 16]), ALU.mult))
    st.link(dve.tensor_scalar(a.bitcast(U32), a.bitcast(U32), SIGN_BIT - 1, None, ALU.bitwise_and))
    s1 = st.done(dve.tensor_scalar(s, a, 0.25, None, ALU.is_gt))
    w1 = st.done(dve.tensor_scalar(w, a, 5.0, 2.0, ALU.is_gt, ALU.mult))
    dve.wait_ge(st.s, st.at(s1))
    s1 = st.done(dve.scalar_tensor_tensor(s, a, 0.75, s, ALU.is_gt, ALU.add))
    dve.wait_ge(st.s, st.at(w1))
    w1 = st.done(dve.scalar_tensor_tensor(w, a, 2.5, w, ALU.is_gt, ALU.add))
    dve.wait_ge(st.s, st.at(s1))
    s1 = st.done(dve.scalar_tensor_tensor(s, a, 1.25, s, ALU.is_gt, ALU.add))
    dve.wait_ge(st.s, st.at(w1))
    w1 = st.done(dve.scalar_tensor_tensor(w, a, 3.5, w, ALU.is_gt, ALU.add))
    dve.wait_ge(st.s, st.at(s1))
    s1 = st.done(dve.scalar_tensor_tensor(s, a, 1.75, s, ALU.is_gt, ALU.add))
    dve.wait_ge(st.s, st.at(s1))
    dve.wait_ge(st.s, st.at(w1))
    st.link(dve.scalar_tensor_tensor(s, s, 0.5, w, ALU.mult, ALU.add))
    st.link(dve.tensor_tensor(blocks(s), blocks(s), bc(scale.unsqueeze(2), [p, g, 16]), ALU.mult))
    return dve.scalar_tensor_tensor(out.bitcast(U32), src.bitcast(U32), SIGN_BIT, s.bitcast(U32),
                                    ALU.bitwise_and, ALU.bitwise_or)


FP4_STEPS = 14


def prepare_fp4_weights(nc, io, W):
    RT, NT = 88, 8
    H, I = 256, 704
    with ExitStack() as ctx:
        sb = lambda n, s, d=F32: ctx.enter_context(nc.sbuf_tensor(n, s, d))
        sem = lambda n: ctx.enter_context(nc.semaphore(n))
        up_raw = sb("up_raw", [RT, 2, NT * H])
        down_raw = sb("down_raw", [P, 2 * I])
        up_q = sb("up_q", [RT, 2, NT * H])
        down_q = sb("down_q", [P, 2 * I])
        blk = sb("w_blk", [P, 3, NT * H // 16])
        work = sb("w_work", [P, 3, NT * H])
        turned = ctx.enter_context(nc.psum_tensor("w_turned", [P, 4, 512], F32))
        loaded, quant, turned_ready, copied, ident0 = map(sem, ("w_loaded", "w_quant", "w_turned_s", "w_copied", "w_ident0"))
        ident_ready = sem("ident_ready")
        steps_sem = Sem(ctx, nc, "w_steps", 3 * FP4_STEPS)
        seed(nc, [steps_sem])
        block = ctx.enter_context(nc.Block())

        @block.sync
        def _(sp):
            for n, w in enumerate((io["L0_ffn_w_gate"], io["L0_ffn_w_up"])):
                sp.dma_start(up_raw[:, n, :].rearrange("p (t k) -> p t k", t=NT),
                             w.rearrange("(t p) k -> p t k", p=RT)).then_inc(loaded, 16)
                sp.wait_ge(loaded, 16 * (n + 1))
            sp.dma_start(down_raw[:, :].rearrange("p (t k) -> p t k", t=2),
                         io["L0_ffn_w_down"].rearrange("(t p) k -> p t k", p=P)).then_inc(loaded, 16)

        @block.gpsimd
        def _(pool):
            pool.memset(W["ident"][:, :], 0.0).then_inc(ident0, 1)
            pool.wait_ge(ident0, 1)
            pool.affine_select(out=W["ident"][:, :], in_=W["ident"][:, :], compare_op=ALU.not_equal, fill=1.0,
                               base=0, pattern=[[-1, P]], channel_multiplier=1).then_inc(ident_ready, 1)

        @block.vector
        def _(dve):
            st = Steps(steps_sem, dve)
            for n in range(2):
                dve.wait_ge(loaded, 16 * (n + 1))
                if n:
                    dve.wait_ge(quant, n)
                fp4_steps(dve, st, up_raw[:, n, :], up_q[:, n, :], blk, work, RT, NT * H).then_inc(quant, 1)
            dve.wait_ge(loaded, 48)
            dve.wait_ge(quant, 2)
            fp4_steps(dve, st, down_raw[:, :], down_q[:, :], blk, work, P, 2 * I).then_inc(quant, 1)
            st.end()

        moves = []
        for n, name in enumerate(("gateT", "upT")):
            for k in range(2):
                for t in range(NT):
                    moves.append((n, up_q[:, n, t * H + k * P:t * H + (k + 1) * P],
                                  W[name][:, k, t * RT:(t + 1) * RT], P, RT))
        for t in range(2):
            for k in range(6):
                kk = min(P, I - k * P)
                moves.append((2, down_q[:, t * I + k * P:t * I + k * P + kk],
                              W["downT"][0:kk, k, t * P:(t + 1) * P], kk, P))

        @block.tensor
        def _(pe):
            pe.wait_ge(ident_ready, 1)
            for i, (n, src, dst, rows, cols) in enumerate(moves):
                pe.wait_ge(quant, n + 1)
                if i >= 4:
                    pe.wait_ge(copied, i - 3)
                pe.transpose(turned[0:rows, i % 4, 0:cols], src, W["ident"][0:cols, 0:cols]).then_inc(turned_ready, 1)

        @block.scalar
        def _(act):
            for i, (n, src, dst, rows, cols) in enumerate(moves):
                act.wait_ge(turned_ready, i + 1)
                act.activation(dst, turned[0:rows, i % 4, 0:cols], ACT.Copy).then_inc(copied, 1)


def mamba_and_fp4_ffn(nc, io, W, x1_dram, bc_dram, NB):
    T, D, DI, NS, R, I = 512, 256, 512, 16, 16, 704
    TT, DC, IC = T // P, D // P, DI // P
    KC = 6
    HALF = I // 2
    NG = 2
    GROUPS = NS // NG
    SCANS = GROUPS * IC
    RING = 4

    with ExitStack() as ctx:
        sb = lambda n, s, d=F32: ctx.enter_context(nc.sbuf_tensor(n, s, d))
        sems = []

        def S(name, per):
            sems.append(Sem(ctx, nc, name, per))
            return sems[-1]

        w_in = sb("w_in", [P, DC, 2 * DI])
        w_xp = sb("w_xp", [P, IC, R + 2 * NS])
        w_dt = sb("w_dt", [64, DI])
        w_out = sb("w_out", [P, IC, D])
        conv_w = sb("conv_w", [P, IC, 4])
        cols = sb("cols", [P, 3, IC])
        a_neg = sb("a_neg", [P, IC, NS])
        a_log = sb("a_log", [P, IC, NS])
        mhalf = sb("mhalf", [P, TT])
        eps = sb("eps", [P, TT])
        tick = sb("tick", [P, 1])

        x_sb = sb("x_sb", [P, TT, D])
        stats = sb("stats", [P, TT, 6])
        mv = sb("mv", [P, TT, 2])
        rstd = sb("rstd", [P, TT])
        veps = sb("veps", [P, TT])
        xn = sb("xn", [P, TT, D])
        xq = sb("xq", [P, TT, D])
        xnT = sb("xnT", [P, DC, T])
        xqT = sb("xqT", [P, DC, T])
        xin = sb("xin", [P, IC, T + 3])
        cv = sb("cv", [P, IC, T])
        u = sb("u", [P, IC, T])
        sz = sb("sz", [P, IC, T])
        xd = sb("xd", [64, T])
        sp_t = sb("sp_t", [P, IC, T])
        delta = sb("delta", [P, IC, T])
        du = sb("du", [P, IC, T])
        y = sb("y", [P, IC, T])
        bcB = sb("bcB", [P, 2, NG, T])
        bcC = sb("bcC", [P, 2, NG, T])
        dA = sb("dA", [P, 2, NG, T])
        hb = sb("hb", [P, RING, NG, T])
        blk = sb("blk", [P, 3, TT * D // 16])
        work = sb("work", [P, 3, TT * D])
        sg = sb("sg", [P, I])
        h = sb("h", [P, I])
        hq = sb("hq", [P, I])
        hqT = sb("hqT", [P, KC, T])

        ps_t = ctx.enter_context(nc.psum_tensor("ps_t", [P, 2, 512], F32))
        ps_p = ctx.enter_context(nc.psum_tensor("ps_p", [P, 2, 512], F32))
        ps_f = ctx.enter_context(nc.psum_tensor("ps_f", [P, 4, 512], F32))
        ps_o = ps_f[:, 0:2, :].rearrange("p a (b d) -> p (a b) d", b=2)

        s_w = ctx.enter_context(nc.semaphore("a_weights"))
        s_zero = ctx.enter_context(nc.semaphore("a_zeroed"))
        s_aneg = ctx.enter_context(nc.semaphore("a_negA"))
        x_in = S("a_x_in", 16)
        v_steps = S("a_v_steps", TT + (1 + TT) * FP4_STEPS + 3 * IC + SCANS)
        ticks = S("a_ticks", 1)
        mv_ready = S("a_mv", TT)
        g_steps = S("a_g_steps", 1)
        rstd_ready = S("a_rstd", 1)
        xn_ready = S("a_xn", TT)
        xq_ready = S("a_xq", 1)
        turned = S("a_turned", 4 + 2 * TT)
        taken = S("a_taken", 4 + 2 * TT)
        taken_k4 = S("a_taken_k4", TT)
        proj = S("a_proj", 2 * IC + 1 + IC)
        xin_ready = S("a_xin", IC)
        z_ready = S("a_z", IC)
        cv_ready = S("a_cv", IC)
        u_ready = S("a_u", IC)
        xd_ready = S("a_xd", 1)
        bc_out = S("a_bc_out", 16)
        bc_in = [S(f"a_bc_in{i}", 32 * GROUPS // 2) for i in range(2)]
        sp_abs = S("a_sp_abs", IC)
        sp_relu = S("a_sp_relu", IC)
        sp_exp = S("a_sp_exp", IC)
        sp_ln = S("a_sp_ln", IC)
        delta_ready = S("a_delta", IC)
        du_ready = S("a_du", IC)
        dA_ready = S("a_dA", SCANS)
        dA_half = S("a_dA_half", SCANS * (NG - 1))
        dBu_ready = S("a_dBu", SCANS)
        scanned = S("a_scanned", SCANS)
        weighed = S("a_weighed", SCANS)
        added = S("a_added", SCANS)
        y0_ready = S("a_y0", IC)
        y_ready = S("a_y", IC)
        gu = S("a_gate_up", TT)
        sg_ready = S("a_sg", TT)
        h_ready = S("a_h", TT)
        hq_ready = S("a_hq", TT)
        out_ready = S("a_out", 1)
        x1_ready = S("a_x1", 1)
        stored = S("a_stored", 16)
        seed(nc, sems)
        block = ctx.enter_context(nc.Block())

        def kk(k):
            return min(P, I - k * P)

        @block.sync
        def _(sp):
            n = 0

            def load(dst, src):
                sp.dma_start(dst, src).then_inc(s_w, 16)

            load(w_in[:, :, :], io["W_inT"].rearrange("(c p) n -> p c n", p=P))
            load(w_xp[:, :, :], io["W_xprojT"].rearrange("(c p) n -> p c n", p=P))
            load(w_out[:, :, :], io["W_outT"].rearrange("(c p) n -> p c n", p=P))
            load(conv_w[:, :, :], io["L0_attn_conv_w"].rearrange("(c p) o k -> p c (o k)", p=P))
            load(a_log[:, :, :], io["L0_attn_A_log"].rearrange("(c p) n -> p c n", p=P))
            load(cols[:, :, :], io["mamba_cols"])
            sp.wait_ge(s_zero, 1)
            load(w_dt[0:R, :], io["W_dtT"])
            with sp.Fori(0, NB) as b:
                sp.wait_ge(stored.s, stored.at(b, 0))
                sp.dma_start(x_sb[:, :, :], io["x"][b].rearrange("(t p) d -> p t d", p=P)).then_inc(x_in.s, 16)
                sp.wait_ge(xd_ready.s, xd_ready.at(b, 1))
                sp.dma_start(bc_dram[b], xd[R:R + 2 * NS, :]).then_inc(bc_out.s, 16)
                sp.wait_ge(bc_out.s, bc_out.at(b, 16))
                for g in range(GROUPS):
                    if g >= 2:
                        sp.wait_ge(weighed.s, weighed.at(b, (g - 1) * IC))
                    sp.dma_start(bcB[:, g % 2, :, :],
                                 bc_dram[b, g * NG:(g + 1) * NG, :].unsqueeze(0).broadcast_to([P, NG, T]))\
                        .then_inc(bc_in[g % 2].s, 16)
                    sp.dma_start(bcC[:, g % 2, :, :],
                                 bc_dram[b, NS + g * NG:NS + (g + 1) * NG, :].unsqueeze(0).broadcast_to([P, NG, T]))\
                        .then_inc(bc_in[g % 2].s, 16)
                sp.wait_ge(x1_ready.s, x1_ready.at(b, 1))
                sp.dma_start(x1_dram[b].rearrange("(t p) d -> p t d", p=P), x_sb[:, :, :]).then_inc(stored.s, 16)
            sp.wait_ge(stored.s, stored.at(NB, 0))

        @block.gpsimd
        def _(pool):
            pool.memset(w_dt[:, :], 0.0).then_inc(s_zero, 1)
            pool.memset(mhalf[:, :], -0.5).then_inc(s_zero, 1)
            pool.memset(xd[:, :], 0.0).then_inc(s_zero, 1)
            pool.memset(eps[:, :], LN_EPS).then_inc(s_zero, 1)
            pool.memset(xin[:, :, 0:3], 0.0).then_inc(s_zero, 1)
            pool.memset(dA[:, :, :, 0:1], 0.0).then_inc(s_zero, 1)
            pool.wait_ge(s_zero, 6)
            with pool.Fori(0, NB) as b:
                pool.wait_ge(mv_ready.s, mv_ready.at(b, TT))
                pool.wait_ge(xn_ready.s, xn_ready.at(b, 0))
                pool.tensor_tensor(veps[:, :], mv[:, :, 1], eps[:, :], ALU.add).then_inc(g_steps.s, 1)
                pool.wait_ge(g_steps.s, g_steps.at(b, 1))
                pool.tensor_tensor(rstd[:, :], veps[:, :], mhalf[:, :], ALU.pow).then_inc(rstd_ready.s, 1)
                for c in range(IC):
                    pool.wait_ge(delta_ready.s, delta_ready.at(b, c + 1))
                    pool.tensor_tensor(du[:, c, :], delta[:, c, :], u[:, c, :], ALU.mult).then_inc(du_ready.s, 1)
                for s in range(SCANS):
                    g, c = divmod(s, IC)
                    pool.wait_ge(bc_in[g % 2].s, bc_in[g % 2].at(b, 32 * (g // 2 + 1)))
                    pool.wait_ge(du_ready.s, du_ready.at(b, c + 1))
                    if s >= RING:
                        pool.wait_ge(added.s, added.at(b, s - RING + 1))
                    else:
                        pool.wait_ge(added.s, added.at(b, 0))
                    pool.tensor_tensor(hb[:, s % RING, :, :], bcB[:, g % 2, :, :],
                                       bc(du[:, c, :].unsqueeze(1), [P, NG, T]), ALU.mult)\
                        .then_inc(dBu_ready.s, 1)

        @block.vector
        def _(dve):
            st = Steps(v_steps, dve)
            dve.wait_ge(s_w, 16 * 7)
            dve.wait_ge(s_zero, 6)
            dve.wait_ge(s_aneg, 1)
            dve.tensor_scalar(a_neg[:, :, :], a_neg[:, :, :], -1.0, None, ALU.mult).then_inc(s_aneg, 1)
            with dve.Fori(0, NB) as b:
                st.turn(b)
                dve.wait_ge(x_in.s, x_in.at(b, 16))
                dve.wait_ge(rstd_ready.s, rstd_ready.at(b, 0))
                for t in range(TT):
                    st.done(dve.bn_stats(stats[:, t, :], x_sb[:, t, :]))
                for t in range(TT):
                    if t == 0:
                        dve.wait_ge(st.s, st.at(TT))
                        dve.memset(tick[:, :], 0.0).then_inc(ticks.s, 1)
                    dve.bn_aggr(mv[:, t, :], stats[:, t, :]).then_inc(mv_ready.s, 1)
                dve.wait_ge(rstd_ready.s, rstd_ready.at(b, 1))
                dve.wait_ge(turned.s, turned.at(b, 0))
                for t in range(TT):
                    dve.tensor_scalar(xn[:, t, :], x_sb[:, t, :], mv[:, t, 0:1], rstd[:, t:t + 1],
                                      ALU.subtract, ALU.mult).then_inc(xn_ready.s, 1)
                dve.wait_ge(xn_ready.s, xn_ready.at(b, TT))
                fp4_steps(dve, st, xn[:, :, :].rearrange("p t d -> p (t d)"),
                          xq[:, :, :].rearrange("p t d -> p (t d)"), blk, work, P, TT * D).then_inc(xq_ready.s, 1)
                dve.wait_ge(xq_ready.s, xq_ready.at(b, 1))
                marks = [0] * IC
                for c in range(IC):
                    dve.wait_ge(xin_ready.s, xin_ready.at(b, c + 1))
                    marks[c] = st.done(dve.tensor_scalar(cv[:, c, :], xin[:, c, 0:T], conv_w[:, c, 0:1], None, ALU.mult))
                for j in range(1, 4):
                    for c in range(IC):
                        dve.wait_ge(st.s, st.at(marks[c]))
                        ins = dve.scalar_tensor_tensor(cv[:, c, :], xin[:, c, j:j + T], conv_w[:, c, j:j + 1],
                                                       cv[:, c, :], ALU.mult, ALU.add)
                        if j < 3:
                            marks[c] = st.done(ins)
                        else:
                            ins.then_inc(cv_ready.s, 1)

                def ffn_hidden(t):
                    dve.wait_ge(sg_ready.s, sg_ready.at(b, t + 1))
                    if t:
                        dve.wait_ge(hq_ready.s, hq_ready.at(b, t))
                    dve.tensor_tensor(h[:, :].rearrange("p (a n) -> p a n", a=2), ps_f[:, 2:4, 0:HALF],
                                      sg[:, :].rearrange("p (a n) -> p a n", a=2), ALU.mult).then_inc(h_ready.s, 1)
                    dve.wait_ge(h_ready.s, h_ready.at(b, t + 1))
                    if t:
                        dve.wait_ge(turned.s, turned.at(b, 4 + 2 * t))
                    fp4_steps(dve, st, h[:, :], hq[:, :], blk, work, P, I).then_inc(hq_ready.s, 1)

                ffn_hidden(0)
                for c in range(IC):
                    dve.wait_ge(sp_abs.s, sp_abs.at(b, c + 1))
                    dve.tensor_scalar(delta[:, c, :], ps_p[:, (1 + c) % 2, :], cols[:, 1, c:c + 1], 0.0,
                                      ALU.add, ALU.max).then_inc(sp_relu.s, 1)
                ffn_hidden(1)
                for c in range(IC):
                    dve.wait_ge(sp_ln.s, sp_ln.at(b, c + 1))
                    dve.wait_ge(sp_relu.s, sp_relu.at(b, c + 1))
                    dve.tensor_tensor(delta[:, c, :], delta[:, c, :], sp_t[:, c, :], ALU.add)\
                        .then_inc(delta_ready.s, 1)
                ffn_hidden(2)
                ffn_hidden(3)
                for c in range(IC):
                    dve.tensor_scalar(y[:, c, :], u[:, c, :], cols[:, 2, c:c + 1], None, ALU.mult)\
                        .then_inc(y0_ready.s, 1)
                flat = lambda ap: ap.rearrange("p n t -> p (n t)")
                for s in range(SCANS + 2):
                    if s < SCANS:
                        dve.wait_ge(dA_ready.s, dA_ready.at(b, s + 1))
                        dve.wait_ge(dBu_ready.s, dBu_ready.at(b, s + 1))
                        tile = flat(hb[:, s % RING, :, :])
                        dve.tensor_tensor_scan(tile, flat(dA[:, s % 2, :, :]), tile, 0.0, ALU.mult, ALU.add)\
                            .then_inc(scanned.s, 1)
                    if s >= 2:
                        r = s - 2
                        c = r % IC
                        dve.wait_ge(st.s, st.at(pair))
                        if r >= IC:
                            dve.wait_ge(added.s, added.at(b, r - IC + 1))
                        else:
                            dve.wait_ge(y0_ready.s, y0_ready.at(b, c + 1))
                        dve.tensor_tensor(y[:, c, :], y[:, c, :], hb[:, r % RING, 0, :], ALU.add)\
                            .then_inc(added.s, 1)
                    if 1 <= s <= SCANS:
                        r = s - 1
                        dve.wait_ge(scanned.s, scanned.at(b, r + 1))
                        tile = hb[:, r % RING, :, :]
                        dve.tensor_tensor(tile, tile, bcC[:, (r // IC) % 2, :, :], ALU.mult)\
                            .then_inc(weighed.s, 1)
                        dve.wait_ge(weighed.s, weighed.at(b, r + 1))
                        pair = st.done(dve.tensor_tensor(tile[:, 0, :], tile[:, 0, :], tile[:, 1, :], ALU.add))
                for c in range(IC):
                    dve.wait_ge(added.s, added.at(b, SCANS - IC + c + 1))
                    dve.tensor_tensor(y[:, c, :], y[:, c, :], sz[:, c, :], ALU.mult).then_inc(y_ready.s, 1)
                dve.wait_ge(out_ready.s, out_ready.at(b, 1))
                dve.tensor_tensor(x_sb[:, :, :], ps_o, x_sb[:, :, :], ALU.add).then_inc(x1_ready.s, 1)
                st.end()

        @block.scalar
        def _(act):
            act.wait_ge(s_w, 16 * 7)
            act.activation(a_neg[:, :, :], a_log[:, :, :], ACT.Exp).then_inc(s_aneg, 1)
            act.wait_ge(s_aneg, 2)
            act.wait_ge(s_zero, 6)
            with act.Fori(0, NB) as b:
                for k in range(DC):
                    act.wait_ge(turned.s, turned.at(b, k + 1))
                    act.activation(xnT[:, k, :], ps_t[:, k, :], ACT.Copy).then_inc(taken.s, 1)
                for c in range(IC):
                    act.wait_ge(proj.s, proj.at(b, c + 1))
                    if c == 0:
                        act.wait_ge(cv_ready.s, cv_ready.at(b, 0))
                    act.activation(xin[:, c, 3:], ps_p[:, c % 2, :], ACT.Copy).then_inc(xin_ready.s, 1)
                for c in range(IC):
                    act.wait_ge(proj.s, proj.at(b, IC + c + 1))
                    if c == 0:
                        act.wait_ge(y_ready.s, y_ready.at(b, 0))
                    act.activation(sz[:, c, :], ps_p[:, c % 2, :], ACT.Silu).then_inc(z_ready.s, 1)
                for k in range(DC):
                    act.wait_ge(turned.s, turned.at(b, 2 + k + 1))
                    act.activation(xqT[:, k, :], ps_t[:, k, :], ACT.Copy).then_inc(taken.s, 1)
                for c in range(IC):
                    act.wait_ge(cv_ready.s, cv_ready.at(b, c + 1))
                    if c == 0:
                        act.wait_ge(du_ready.s, du_ready.at(b, 0))
                    act.activation(u[:, c, :], cv[:, c, :], ACT.Silu, bias=cols[:, 0, c:c + 1]).then_inc(u_ready.s, 1)

                def silu_gate(t):
                    act.wait_ge(gu.s, gu.at(b, t + 1))
                    if t:
                        act.wait_ge(h_ready.s, h_ready.at(b, t))
                    act.activation(sg[:, :].rearrange("p (a n) -> p a n", a=2), ps_f[:, 0:2, 0:HALF], ACT.Silu)\
                        .then_inc(sg_ready.s, 1)

                def take_h(t):
                    act.wait_ge(turned.s, turned.at(b, 4 + 2 * t + 1))
                    act.activation(hqT[:, 0:4, t * P:(t + 1) * P], ps_t[:, 0, :].rearrange("p (k n) -> p k n", k=4),
                                   ACT.Copy).then_inc(taken.s, 1)
                    act.wait_ge(turned.s, turned.at(b, 4 + 2 * t + 2))
                    act.activation(hqT[:, 4, t * P:(t + 1) * P], ps_t[:, 1, 0:P], ACT.Copy).then_inc(taken_k4.s, 1)
                    act.activation(hqT[0:64, 5, t * P:(t + 1) * P], ps_t[0:64, 1, P:2 * P], ACT.Copy)\
                        .then_inc(taken.s, 1)

                silu_gate(0)
                act.wait_ge(proj.s, proj.at(b, 2 * IC + 1))
                act.activation(xd[0:R + 2 * NS, :], ps_p[0:R + 2 * NS, 0, :], ACT.Copy).then_inc(xd_ready.s, 1)
                for c in range(IC):
                    act.wait_ge(proj.s, proj.at(b, 2 * IC + 1 + c + 1))
                    act.activation(sp_t[:, c, :], ps_p[:, (1 + c) % 2, :], ACT.Abs, bias=cols[:, 1, c:c + 1])\
                        .then_inc(sp_abs.s, 1)
                for c in range(IC):
                    act.wait_ge(sp_abs.s, sp_abs.at(b, c + 1))
                    act.activation(sp_t[:, c, :], sp_t[:, c, :], ACT.Exp, scale=-1.0).then_inc(sp_exp.s, 1)
                for c in range(IC):
                    act.wait_ge(sp_exp.s, sp_exp.at(b, c + 1))
                    act.activation(sp_t[:, c, :], sp_t[:, c, :], ACT.Ln, bias=1.0).then_inc(sp_ln.s, 1)
                take_h(0)
                silu_gate(1)
                take_h(1)
                silu_gate(2)
                take_h(2)
                silu_gate(3)
                take_h(3)
                for s in range(SCANS):
                    g, c = divmod(s, IC)
                    act.wait_ge(delta_ready.s, delta_ready.at(b, c + 1))
                    if s >= 2:
                        act.wait_ge(scanned.s, scanned.at(b, s - 1))
                    for n in range(NG):
                        ins = act.activation(dA[:, s % 2, n, 1:], delta[:, c, 1:], ACT.Exp,
                                             scale=a_neg[:, c, g * NG + n:g * NG + n + 1])
                        ins.then_inc((dA_half if n + 1 < NG else dA_ready).s, 1)

        @block.tensor
        def _(pe):
            pe.wait_ge(s_w, 16 * 7)
            pe.wait_ge(s_zero, 6)
            with pe.Fori(0, NB) as b:
                def turn_x(src, k, n):
                    for t in range(TT):
                        last = pe.transpose(ps_t[:, k, t * P:(t + 1) * P], src[:, t, k * P:(k + 1) * P], W["ident"][:, :])
                    last.then_inc(turned.s, 1)

                pe.wait_ge(taken.s, taken.at(b, 0))
                pe.wait_ge(xn_ready.s, xn_ready.at(b, TT))
                for k in range(DC):
                    turn_x(xn, k, k)
                for c in range(2 * IC):
                    if c < DC:
                        pe.wait_ge(taken.s, taken.at(b, DC))
                    if c >= 2:
                        read = xin_ready if c - 2 < IC else z_ready
                        pe.wait_ge(read.s, read.at(b, (c - 2) % IC + 1))
                    else:
                        pe.wait_ge(sp_abs.s, sp_abs.at(b, 0))
                        pe.wait_ge(sp_relu.s, sp_relu.at(b, 0))
                    for k in range(DC):
                        last = pe.matmul(ps_p[:, c % 2, :], w_in[:, k, c * P:(c + 1) * P], xnT[:, k, :],
                                         start=(k == 0), stop=(k == DC - 1))
                    last.then_inc(proj.s, 1)
                pe.wait_ge(xq_ready.s, xq_ready.at(b, 1))
                for k in range(DC):
                    turn_x(xq, k, 2 + k)

                def gate_up(t):
                    if t == 0:
                        pe.wait_ge(taken.s, taken.at(b, 4))
                        pe.wait_ge(x1_ready.s, x1_ready.at(b, 0))
                    else:
                        pe.wait_ge(h_ready.s, h_ready.at(b, t))
                    for n in range(4):
                        w = W["gateT"] if n < 2 else W["upT"]
                        for k in range(DC):
                            last = pe.matmul(ps_f[:, n, 0:HALF], xqT[:, k, t * P:(t + 1) * P],
                                             w[:, k, (n % 2) * HALF:(n % 2 + 1) * HALF],
                                             start=(k == 0), stop=(k == DC - 1))
                    last.then_inc(gu.s, 1)

                def turn_h(t):
                    pe.wait_ge(hq_ready.s, hq_ready.at(b, t + 1))
                    pe.wait_ge(taken.s, taken.at(b, 4 + 2 * t))
                    for k in range(KC):
                        last = pe.transpose(ps_t[0:kk(k), k // 4, (k % 4) * P:(k % 4 + 1) * P],
                                            hq[:, k * P:k * P + kk(k)], W["ident"][:, :])
                        if k in (3, KC - 1):
                            last.then_inc(turned.s, 1)

                gate_up(0)
                pe.wait_ge(u_ready.s, u_ready.at(b, IC))
                pe.wait_ge(z_ready.s, z_ready.at(b, IC))
                for k in range(IC):
                    last = pe.matmul(ps_p[0:R + 2 * NS, 0, :], w_xp[:, k, :], u[:, k, :],
                                     start=(k == 0), stop=(k == IC - 1))
                last.then_inc(proj.s, 1)
                pe.wait_ge(xd_ready.s, xd_ready.at(b, 1))
                for c in range(IC):
                    if c >= 2:
                        pe.wait_ge(sp_abs.s, sp_abs.at(b, c - 1))
                        pe.wait_ge(sp_relu.s, sp_relu.at(b, c - 1))
                    pe.matmul(ps_p[:, (1 + c) % 2, :], w_dt[:, c * P:(c + 1) * P], xd[:, :],
                              start=True, stop=True).then_inc(proj.s, 1)
                turn_h(0)
                for t in range(1, TT):
                    gate_up(t)
                    turn_h(t)
                pe.wait_ge(taken.s, taken.at(b, 4 + 2 * TT))
                pe.wait_ge(y_ready.s, y_ready.at(b, IC))
                pe.wait_ge(h_ready.s, h_ready.at(b, TT))
                for t in range(TT):
                    for k in range(KC):
                        pe.matmul(ps_o[:, t, :], hqT[0:kk(k), k, t * P:(t + 1) * P], W["downT"][0:kk(k), k, :],
                                  start=(k == 0), stop=False)
                    for k in range(IC):
                        last = pe.matmul(ps_o[:, t, :], y[:, k, t * P:(t + 1) * P], w_out[:, k, :],
                                         start=False, stop=(k == IC - 1))
                last.then_inc(out_ready.s, 1)


def block_sparse_attention(nc, io, W, x1_dram, xn_dram, base_dram, NB):
    T, D, NH, HD = 512, 256, 16, 16
    TT, DC = T // P, D // P
    UNITS = TT * NH // 2
    KEYS = [[0, 1, 2, 3], [0, 1], [0, 2], [0, 3]]

    with ExitStack() as ctx:
        sb = lambda n, s, d=F32: ctx.enter_context(nc.sbuf_tensor(n, s, d))
        sems = []

        def S(name, per):
            sems.append(Sem(ctx, nc, name, per))
            return sems[-1]

        w_qkv = sb("b_w_qkv", [P, DC, 3 * D])
        w_o = sb("b_w_o", [P, DC, D])
        qk_bias = sb("b_qk_bias", [P, 4])
        head_mask = sb("b_head_mask", [P, 4])
        v_bias = sb("b_v_bias", [P, D])
        o_bias = sb("b_o_bias", [P, D])
        mhalf = sb("b_mhalf", [P, TT])
        eps = sb("b_eps", [P, TT])
        tick = sb("b_tick", [P, 1])
        x_sb = sb("b_x", [P, TT, D])
        xb = sb("b_xb", [P, TT, D])
        res = sb("b_res", [P, TT, D])
        stats = sb("b_stats", [P, TT, 6])
        mv = sb("b_mv", [P, TT, 2])
        rstd = sb("b_rstd", [P, TT])
        veps = sb("b_veps", [P, TT])
        xn = sb("b_xn", [P, TT, D])
        xT = sb("b_xT", [P, DC, T])
        qm = sb("b_qm", [P, DC, 4, T])
        kf = sb("b_kf", [P, DC, T])
        v = sb("b_v", [P, TT, NH, HD + 1])
        negmax = sb("b_negmax", [P, UNITS, 2])
        pr = sb("b_pr", [P, 2, 2, 512])
        pt = sb("b_pt", [P, 2, 1024])
        inv = sb("b_inv", [P, NH])
        o = sb("b_o", [P, TT, D])
        oT = sb("b_oT", [P, DC, T])

        ps_s = ctx.enter_context(nc.psum_tensor("b_ps_s", [P, 4, 512], F32))
        ps_t = ctx.enter_context(nc.psum_tensor("b_ps_t", [P, 2, 512], F32))
        ps_o = ctx.enter_context(nc.psum_tensor("b_ps_o", [P, 512], F32))
        ps_v = ps_t[:, :, :].rearrange("p a (b d) -> p (a b) d", b=2)
        ps_oh = ps_o[:, 0:NH * (HD + 1)].rearrange("p (h e) -> p h e", h=NH)

        s_w = ctx.enter_context(nc.semaphore("b_weights"))
        s_const = ctx.enter_context(nc.semaphore("b_const"))
        x_in = S("b_x_in", 16)
        v_steps = S("b_v_steps", TT)
        ticks = S("b_ticks", 1)
        mv_ready = S("b_mv", TT)
        g_steps = S("b_g_steps", 1)
        rstd_ready = S("b_rstd", 1)
        xn_ready = S("b_xn", TT)
        xb_ready = S("b_xb", 1)
        xT_turned = S("b_xT_turned", DC)
        xT_ready = S("b_xT", DC)
        qk_proj = S("b_qk_proj", 4)
        q_ready = S("b_q", 8)
        k_ready = S("b_k", 2)
        v_proj = S("b_v_proj", TT)
        v_ready = S("b_v", TT)
        scores = S("b_scores", UNITS)
        max_ready = S("b_max", UNITS)
        exp_half = S("b_exp_half", UNITS)
        exp_ready = S("b_exp", UNITS)
        p_turned = S("b_p_turned", UNITS)
        pt_ready = S("b_pt_ready", UNITS)
        pv_done = S("b_pv", UNITS)
        inv_ready = S("b_inv_ready", TT)
        o_ready = S("b_o_ready", TT)
        o_turned = S("b_o_turned", DC)
        oT_ready = S("b_oT_ready", DC)
        out_done = S("b_out", 1)
        res_ready = S("b_res_ready", 1)
        stored = S("b_stored", 32)
        seed(nc, sems)
        block = ctx.enter_context(nc.Block())

        def nk(u):
            return len(KEYS[u // 8])

        def slot(u):
            return 2 * (u % 2)

        def normalise(t, dve, b):
            dve.wait_ge(pv_done.s, pv_done.at(b, 8 * (t + 1)))
            dve.reciprocal(inv[:, :], ps_oh[:, :, HD]).then_inc(inv_ready.s, 1)
            dve.wait_ge(inv_ready.s, inv_ready.at(b, t + 1))
            dve.tensor_tensor(o[:, t, :].rearrange("p (h e) -> p h e", h=NH), ps_oh[:, :, 0:HD],
                              bc(inv[:, :].unsqueeze(2), [P, NH, HD]), ALU.mult).then_inc(o_ready.s, 1)

        @block.sync
        def _(sp):
            for dst, src in ((w_qkv[:, :, :], io["L1_w_qkvT"].rearrange("(c p) n -> p c n", p=P)),
                             (w_o[:, :, :], io["L1_w_outT"].rearrange("(c p) n -> p c n", p=P)),
                             (qk_bias[:, :], io["qk_bias_cols"]),
                             (head_mask[:, :], io["head_mask"]),
                             (v_bias[:, :], io["L1_attn_b_qkv"][2 * D:3 * D].unsqueeze(0).broadcast_to([P, D])),
                             (o_bias[:, :], io["L1_attn_b_out"].unsqueeze(0).broadcast_to([P, D]))):
                sp.dma_start(dst, src).then_inc(s_w, 16)
            with sp.Fori(0, NB) as b:
                sp.wait_ge(xb_ready.s, xb_ready.at(b, 0))
                sp.dma_start(x_sb[:, :, :], x1_dram[b].rearrange("(t p) d -> p t d", p=P)).then_inc(x_in.s, 16)
                sp.wait_ge(xn_ready.s, xn_ready.at(b, TT))
                sp.dma_start(xn_dram[b].rearrange("(t p) d -> p t d", p=P), xn[:, :, :]).then_inc(stored.s, 16)
                sp.wait_ge(res_ready.s, res_ready.at(b, 1))
                sp.dma_start(base_dram[b].rearrange("(t p) d -> p t d", p=P), res[:, :, :]).then_inc(stored.s, 16)
            sp.wait_ge(stored.s, stored.at(NB, 0))

        @block.gpsimd
        def _(pool):
            pool.memset(mhalf[:, :], -0.5).then_inc(s_const, 1)
            pool.memset(eps[:, :], LN_EPS).then_inc(s_const, 1)
            pool.memset(v[:, :, :, HD:HD + 1], 1.0).then_inc(s_const, 1)
            pool.wait_ge(s_const, 3)
            pool.wait_ge(s_w, 16 * 6)
            with pool.Fori(0, NB) as b:
                pool.wait_ge(mv_ready.s, mv_ready.at(b, TT))
                pool.tensor_tensor(veps[:, :], mv[:, :, 1], eps[:, :], ALU.add).then_inc(g_steps.s, 1)
                pool.wait_ge(g_steps.s, g_steps.at(b, 1))
                pool.tensor_tensor(rstd[:, :], veps[:, :], mhalf[:, :], ALU.pow).then_inc(rstd_ready.s, 1)
                pool.wait_ge(res_ready.s, res_ready.at(b, 0))
                pool.tensor_tensor(xb[:, :, :], x_sb[:, :, :], bc(o_bias[:, :].unsqueeze(1), [P, TT, D]), ALU.add)\
                    .then_inc(xb_ready.s, 1)

        @block.vector
        def _(dve):
            st = Steps(v_steps, dve)
            dve.wait_ge(s_w, 16 * 6)
            dve.wait_ge(s_const, 3)
            with dve.Fori(0, NB) as b:
                st.turn(b)
                dve.wait_ge(x_in.s, x_in.at(b, 16))
                dve.wait_ge(rstd_ready.s, rstd_ready.at(b, 0))
                for t in range(TT):
                    st.done(dve.bn_stats(stats[:, t, :], x_sb[:, t, :]))
                dve.wait_ge(st.s, st.at(TT))
                dve.memset(tick[:, :], 0.0).then_inc(ticks.s, 1)
                for t in range(TT):
                    dve.bn_aggr(mv[:, t, :], stats[:, t, :]).then_inc(mv_ready.s, 1)
                dve.wait_ge(rstd_ready.s, rstd_ready.at(b, 1))
                dve.wait_ge(stored.s, stored.at(b, 0))
                for t in range(TT):
                    dve.tensor_scalar(xn[:, t, :], x_sb[:, t, :], mv[:, t, 0:1], rstd[:, t:t + 1],
                                      ALU.subtract, ALU.mult).then_inc(xn_ready.s, 1)
                for m in range(DC):
                    dve.wait_ge(qk_proj.s, qk_proj.at(b, m + 1))
                    for j in range(4):
                        dve.tensor_scalar(qm[:, m, j, :], ps_s[:, m, :], qk_bias[:, m:m + 1], head_mask[:, j:j + 1],
                                          ALU.add, ALU.mult).then_inc(q_ready.s, 1)
                for t in range(TT):
                    dve.wait_ge(v_proj.s, v_proj.at(b, 2 * (t // 2) + 2))
                    dve.tensor_tensor(v[:, t, :, 0:HD], ps_v[:, t, :].rearrange("p (h e) -> p h e", h=NH),
                                      v_bias[:, :].rearrange("p (h e) -> p h e", h=NH), ALU.add).then_inc(v_ready.s, 1)
                for u in range(UNITS + 1):
                    if u < UNITS:
                        dve.wait_ge(scores.s, scores.at(b, u + 1))
                        dve.tensor_reduce(negmax[:, u, :], ps_s[:, slot(u):slot(u) + 2, 0:P * nk(u)], AX.X, ALU.max,
                                          negate=True).then_inc(max_ready.s, 1)
                    if u:
                        r = u - 1
                        dve.wait_ge(p_turned.s, p_turned.at(b, r + 1))
                        if r >= 2:
                            dve.wait_ge(pv_done.s, pv_done.at(b, r - 1))
                        n = 2 * nk(r)
                        if n == 8:
                            dst, src = pt[:, r % 2, :].rearrange("p (a n) -> p a n", a=2), ps_t[:, :, :]
                        else:
                            dst, src = pt[:, r % 2, 0:512], ps_t[:, r % 2, :]
                        dve.tensor_copy(dst, src).then_inc(pt_ready.s, 1)
                    if u >= 10 and (u - 2) % 8 == 0:
                        normalise((u - 2) // 8 - 1, dve, b)
                normalise(TT - 1, dve, b)
                dve.wait_ge(out_done.s, out_done.at(b, 1))
                dve.wait_ge(xb_ready.s, xb_ready.at(b, 1))
                dve.wait_ge(stored.s, stored.at(b, 16))
                dve.tensor_tensor(res[:, :, :], ps_v, xb[:, :, :], ALU.add).then_inc(res_ready.s, 1)
                st.end()

        @block.scalar
        def _(act):
            act.wait_ge(s_w, 16 * 6)
            with act.Fori(0, NB) as b:
                for k in range(DC):
                    act.wait_ge(xT_turned.s, xT_turned.at(b, k + 1))
                    act.activation(xT[:, k, :], ps_t[:, k, :], ACT.Copy).then_inc(xT_ready.s, 1)
                for m in range(DC):
                    act.wait_ge(qk_proj.s, qk_proj.at(b, 2 + m + 1))
                    act.activation(kf[:, m, :], ps_s[:, 2 + m, :], ACT.Identity, bias=qk_bias[:, 2 + m:3 + m])\
                        .then_inc(k_ready.s, 1)
                for u in range(UNITS):
                    act.wait_ge(max_ready.s, max_ready.at(b, u + 1))
                    if u >= 2:
                        act.wait_ge(p_turned.s, p_turned.at(b, u - 1))
                    for i in range(2):
                        act.activation(pr[:, u % 2, i, 0:P * nk(u)], ps_s[:, slot(u) + i, 0:P * nk(u)], ACT.Exp,
                                       bias=negmax[:, u, i:i + 1]).then_inc((exp_ready if i else exp_half).s, 1)
                for k in range(DC):
                    act.wait_ge(o_turned.s, o_turned.at(b, k + 1))
                    act.activation(oT[:, k, :], ps_s[:, k, :], ACT.Copy).then_inc(oT_ready.s, 1)

        @block.tensor
        def _(pe):
            pe.wait_ge(s_w, 16 * 6)
            pe.wait_ge(s_const, 3)
            with pe.Fori(0, NB) as b:
                def turn(dst, src, ready):
                    for k in range(DC):
                        for t in range(TT):
                            last = pe.transpose(dst[:, k, t * P:(t + 1) * P], src[:, t, k * P:(k + 1) * P],
                                                W["ident"][:, :])
                        last.then_inc(ready.s, 1)

                pe.wait_ge(xn_ready.s, xn_ready.at(b, TT))
                pe.wait_ge(res_ready.s, res_ready.at(b, 0))
                turn(ps_t, xn, xT_turned)
                pe.wait_ge(xT_ready.s, xT_ready.at(b, DC))
                for m in range(4):
                    for k in range(DC):
                        last = pe.matmul(ps_s[:, m, :], w_qkv[:, k, m * P:(m + 1) * P], xT[:, k, :],
                                         start=(k == 0), stop=(k == DC - 1))
                    last.then_inc(qk_proj.s, 1)
                for t in range(TT):
                    for k in range(DC):
                        last = pe.matmul(ps_v[:, t, :], xT[:, k, t * P:(t + 1) * P], w_qkv[:, k, 2 * D:3 * D],
                                         start=(k == 0), stop=(k == DC - 1))
                    last.then_inc(v_proj.s, 1)
                pe.wait_ge(q_ready.s, q_ready.at(b, 8))
                pe.wait_ge(k_ready.s, k_ready.at(b, 2))
                pe.wait_ge(v_ready.s, v_ready.at(b, TT))
                for u in range(UNITS + 2):
                    if u < UNITS:
                        qt = u // 8
                        if u >= 2:
                            pe.wait_ge(exp_ready.s, exp_ready.at(b, u - 1))
                        for i in range(2):
                            h = 2 * (u % 8) + i
                            m, half, j = h // 8, h % 8 // 4, h % 4
                            rows = slice(64 * half, 64 * half + 64)
                            runs = [(0, 0, 512)] if qt == 0 else [(0, 0, 256)] if qt == 1 else \
                                [(0, 0, P), (P, qt * P, P)]
                            for at, key, n in runs:
                                last = pe.matmul(ps_s[:, slot(u) + i, at:at + n], qm[rows, m, j, qt * P:(qt + 1) * P],
                                                 kf[rows, m, key:key + n], start=True, stop=True)
                        last.then_inc(scores.s, 1)
                    if 1 <= u <= UNITS:
                        r = u - 1
                        pe.wait_ge(exp_ready.s, exp_ready.at(b, r + 1))
                        if r:
                            pe.wait_ge(pt_ready.s, pt_ready.at(b, r - 1 if nk(r) == 2 and nk(max(r - 1, 0)) == 2 else r))
                        for i in range(2):
                            for n in range(nk(r)):
                                at = i * nk(r) + n
                                bank = at // 4 if nk(r) == 4 else r % 2
                                last = pe.transpose(ps_t[:, bank, (at % 4) * P:(at % 4 + 1) * P],
                                                    pr[:, r % 2, i, n * P:(n + 1) * P], W["ident"][:, :])
                        last.then_inc(p_turned.s, 1)
                    if u >= 2:
                        r = u - 2
                        qt = r // 8
                        pe.wait_ge(pt_ready.s, pt_ready.at(b, r + 1))
                        if r % 8 == 0 and qt:
                            pe.wait_ge(o_ready.s, o_ready.at(b, qt))
                        for i in range(2):
                            h = 2 * (r % 8) + i
                            for n, key in enumerate(KEYS[qt]):
                                at = i * nk(r) + n
                                last = pe.matmul(ps_oh[:, h, :], pt[:, r % 2, at * P:(at + 1) * P], v[:, key, h, :],
                                                 start=(n == 0), stop=(n == nk(r) - 1))
                        last.then_inc(pv_done.s, 1)
                pe.wait_ge(o_ready.s, o_ready.at(b, TT))
                turn(ps_s, o, o_turned)
                pe.wait_ge(oT_ready.s, oT_ready.at(b, DC))
                pe.wait_ge(pt_ready.s, pt_ready.at(b, UNITS))
                for t in range(TT):
                    for k in range(DC):
                        last = pe.matmul(ps_v[:, t, :], oT[:, k, t * P:(t + 1) * P], w_o[:, k, :],
                                         start=(k == 0), stop=(k == DC - 1))
                last.then_inc(out_done.s, 1)


def local_attention_layers(nc, io, W, stream, NB):
    L, T, D, NH, HD, HID = 2, 512, 256, 8, 64, 682
    TT, DC, IC = T // P, D // P, NH * HD // P
    INNER = NH * HD
    JC = 6
    HPU = 4
    UNITS = TT * NH // HPU
    E1 = HD + 1

    with ExitStack() as ctx:
        sb = lambda n, s, d=F32: ctx.enter_context(nc.sbuf_tensor(n, s, d))
        sems = []

        def S(name, per):
            sems.append(Sem(ctx, nc, name, per))
            return sems[-1]

        w_qkv = sb("c_w_qkv", [P, DC, 3 * INNER])
        w_o = sb("c_w_o", [P, IC, D])
        w_1 = sb("c_w_1", [P, DC, 2 * HID])
        w_2 = sb("c_w_2", [P, JC, D])
        ln_cols = sb("c_ln_cols", [P, DC, 2])
        b1_cols = sb("c_b1_cols", [P, 2, JC])
        b2_row = sb("c_b2_row", [P, D])
        qk_scale = sb("c_qk_scale", [P, 2, HD])
        rot_c0 = sb("c_rot_c0", [P, TT, 2, HD])
        rot_s0 = sb("c_rot_s0", [P, TT, 2, HD])
        rot_c = sb("c_rot_c", [P, TT, 2, HD])
        rot_s = sb("c_rot_s", [P, TT, 2, HD])
        mask32 = sb("c_mask32", [P, 2 * P])
        mask = sb("c_mask", [P, 2 * P], BF16)
        identb = sb("c_identb", [P, P], BF16)
        mhalf = sb("c_mhalf", [P, 2 * NH])
        eps = sb("c_eps", [P, TT])
        tick = sb("c_tick", [P, 1])

        x_sb = sb("c_x", [P, TT, D])
        xT = sb("c_xT", [P, DC, T + 1])
        sq = sb("c_sq", [P, 2, INNER])
        ss = sb("c_ss", [P, 2, NH])
        ssc = sb("c_ssc", [P, 2, NH])
        rn = sb("c_rn", [P, 2, NH])
        qn = sb("c_qn", [P, 2, INNER])
        q_cos = sb("c_q_cos", [P, 2, INNER])
        q_sin = sb("c_q_sin", [P, 2, INNER])
        qr = sb("c_qr", [P, 2, INNER])
        v = sb("c_v", [P, TT, NH, E1])
        qT = sb("c_qT", [P, IC, T])
        kT = sb("c_kT", [P, IC, T])
        negmax = sb("c_negmax", [P, UNITS, HPU])
        pr = sb("c_pr", [P, 2, HPU, 2 * P])
        pt = sb("c_pt", [P, 2, 1024])
        inv = sb("c_inv", [P, 2, HPU])
        o = sb("c_o", [P, TT, INNER])
        oT = sb("c_oT", [P, IC, T])
        xa = sb("c_xa", [P, TT, D])
        xsh = sb("c_xsh", [P, TT, P])
        xa2 = sb("c_xa2", [P, TT, D])
        stats = sb("c_stats", [P, TT, 12])
        mv = sb("c_mv", [P, TT, 2])
        rstd = sb("c_rstd", [P, TT])
        veps = sb("c_veps", [P, TT])
        hn = sb("c_hn", [P, TT, D])
        hT = sb("c_hT", [P, DC, T])
        gl = sb("c_gl", [P, 2, T])
        hid = sb("c_hid", [P, JC, T])
        xo = sb("c_xo", [P, TT, D])

        ps_s = ctx.enter_context(nc.psum_tensor("c_ps_s", [P, 4, 512], F32))
        ps_t = ctx.enter_context(nc.psum_tensor("c_ps_t", [P, 2, 512], F32))
        ps_o = ctx.enter_context(nc.psum_tensor("c_ps_o", [P, 2, 512], F32))
        ps_x = ps_s[:, 0:2, :].rearrange("p a (b d) -> p (a b) d", b=2)
        ps_y = ps_t[:, :, :].rearrange("p a (b d) -> p (a b) d", b=2)

        s_c = ctx.enter_context(nc.semaphore("c_const"))
        s_t = ctx.enter_context(nc.semaphore("c_tables"))
        w_in = S("c_w_in", 16 * 10)
        rot_ready = S("c_rot_ready", 3)
        x_in = S("c_x_in", 16)
        x_turned = S("c_x_turned", DC)
        xT_ready = S("c_xT_ready", DC)
        q_proj = S("c_q_proj", TT)
        v_proj = S("c_v_proj", TT)
        sq_half = S("c_sq_half", TT)
        sq_ready = S("c_sq_ready", TT)
        v_ready = S("c_v_ready", TT)
        ss_raw = S("c_ss_raw", TT)
        ss_ready = S("c_ss", TT)
        rn_ready = S("c_rn", TT)
        qn_half = S("c_qn_half", TT)
        qn_ready = S("c_qn", TT)
        cos_half = S("c_cos_half", TT)
        cos_ready = S("c_cos", TT)
        sin_part = S("c_sin_part", 3 * TT)
        sin_ready = S("c_sin", TT)
        qr_ready = S("c_qr_ready", TT)
        q_turned = S("c_q_turned", TT)
        k_turned = S("c_k_turned", TT)
        qT_ready = S("c_qT_ready", TT)
        kT_ready = S("c_kT_ready", TT)
        scores = S("c_scores", UNITS)
        max_ready = S("c_max", UNITS)
        exp_part = S("c_exp_part", UNITS * (HPU - 1))
        exp_ready = S("c_exp", UNITS)
        p_turned = S("c_p_turned", UNITS)
        pt_ready = S("c_pt_ready", UNITS)
        pv_done = S("c_pv", UNITS)
        inv_ready = S("c_inv_ready", UNITS)
        o_ready = S("c_o_ready", UNITS)
        o_turned = S("c_o_turned", IC)
        oT_ready = S("c_oT_ready", IC)
        wo_done = S("c_wo_done", 1)
        xa_ready = S("c_xa", 1)
        shifted = S("c_shifted", 32)
        v_steps = S("c_v_steps", 2 * TT)
        ticks = S("c_ticks", 1)
        mv_ready = S("c_mv", TT)
        g_steps = S("c_g_steps", 1)
        rstd_ready = S("c_rstd_ready", 1)
        xa2_ready = S("c_xa2", 1)
        hn_ready = S("c_hn", 2 * TT)
        h_turned = S("c_h_turned", DC)
        hT_ready = S("c_hT_ready", DC)
        ag_proj = S("c_ag_proj", JC)
        gl_ready = S("c_gl", JC)
        hid_ready = S("c_hid", JC)
        y_done = S("c_y_done", 1)
        xo_ready = S("c_xo", 1)
        stored = S("c_stored", 16)
        seed(nc, sems)
        block = ctx.enter_context(nc.Block())

        def jj(j):
            return min(P, HID - j * P)

        def nk(u):
            return 1 if u < 2 else 2

        def slot(u):
            return 2 * (u % 2)

        def head(i):
            return i % 2 * 2 + i // 2

        def turns(eng, body, layer=None):
            with eng.Fori(0, L) as l:
                if layer:
                    layer(l)
                with eng.Fori(0, NB) as b:
                    body(l, b, l * NB + b)

        @block.sync
        def _(sp):
            for dst, src in ((rot_c0[:, :, :, :], io["rot_cos"].rearrange("(t p) a d -> p t a d", p=P)),
                             (rot_s0[:, :, :, :], io["rot_sin"].rearrange("(t p) a d -> p t a d", p=P)),
                             (mask32[:, :], io["window_mask"])):
                sp.dma_start(dst, src).then_inc(s_t, 16)

            def layer(l):
                sp.wait_ge(xo_ready.s, xo_ready.at(l * NB, 0))
                for dst, src in ((w_qkv[:, :, :], io["L1_ffn_wqkv"][l].rearrange("(c p) n -> p c n", p=P)),
                                 (w_o[:, :, :], io["L1_ffn_wo"][l].rearrange("(c p) n -> p c n", p=P)),
                                 (w_1[:, :, :], io["L1_ffn_w1"][l].rearrange("(c p) n -> p c n", p=P)),
                                 (w_2[:, 0:JC - 1, :], io["L1_ffn_w2"][l, 0:(JC - 1) * P, :].rearrange("(c p) n -> p c n", p=P)),
                                 (w_2[0:jj(JC - 1), JC - 1, :], io["L1_ffn_w2"][l, (JC - 1) * P:, :]),
                                 (ln_cols[:, :, :], io["ln_cols"][l]),
                                 (b1_cols[:, :, :], io["b1_cols"][l]),
                                 (b2_row[:, :], io["L1_ffn_b2"][l].unsqueeze(0).broadcast_to([P, D])),
                                 (qk_scale[:, 0, :], io["L1_ffn_q_scale"][l].unsqueeze(0).broadcast_to([P, HD])),
                                 (qk_scale[:, 1, :], io["L1_ffn_k_scale"][l].unsqueeze(0).broadcast_to([P, HD]))):
                    sp.dma_start(dst, src).then_inc(w_in.s, 16)

            def body(l, b, it):
                sp.wait_ge(stored.s, stored.at(it, 0))
                sp.dma_start(x_sb[:, :, :], stream[l, b].rearrange("(t p) d -> p t d", p=P)).then_inc(x_in.s, 16)
                sp.wait_ge(xa_ready.s, xa_ready.at(it, 1))
                sp.dma_start(xsh[1:P, :, :], xa[0:P - 1, :, P:D]).then_inc(shifted.s, 16)
                sp.dma_start(xsh[0:1, 1:TT, :], xa[P - 1:P, 0:TT - 1, P:D]).then_inc(shifted.s, 16)
                sp.wait_ge(xo_ready.s, xo_ready.at(it, 1))
                sp.dma_start(stream[l + 1, b].rearrange("(t p) d -> p t d", p=P), xo[:, :, :]).then_inc(stored.s, 16)

            turns(sp, body, layer)
            sp.wait_ge(stored.s, stored.at(L * NB, 0))

        @block.gpsimd
        def _(pool):
            pool.memset(mhalf[:, :], -0.5).then_inc(s_c, 1)
            pool.memset(eps[:, :], LN_EPS).then_inc(s_c, 1)
            pool.memset(v[:, :, :, HD:E1], 1.0).then_inc(s_c, 1)
            pool.memset(xT[:, 1, 0:1], 0.0).then_inc(s_c, 1)
            pool.memset(xsh[0:1, 0, :], 0.0).then_inc(s_c, 1)
            pool.tensor_copy(identb[:, :], W["ident"][:, :]).then_inc(s_c, 1)
            pool.wait_ge(s_t, 48)
            pool.tensor_copy(mask[:, :], mask32[:, :]).then_inc(s_c, 1)
            pool.wait_ge(s_c, 7)

            def body(l, b, it):
                for t in range(TT):
                    pool.wait_ge(ss_ready.s, ss_ready.at(it, t + 1))
                    if t:
                        pool.wait_ge(qn_ready.s, qn_ready.at(it, t))
                    pool.tensor_tensor(rn[:, :, :].rearrange("p a h -> p (a h)"), ssc[:, :, :].rearrange("p a h -> p (a h)"),
                                       mhalf[:, :], ALU.pow).then_inc(rn_ready.s, 1)
                    pool.wait_ge(qn_ready.s, qn_ready.at(it, t + 1))
                    if t == 0:
                        pool.wait_ge(w_in.s, w_in.at(l + 1, 0))
                        pool.wait_ge(rot_ready.s, rot_ready.at(l + 1, 0))
                    heads = lambda ap: ap.rearrange("p a (h d) -> p a h d", h=NH)
                    for a in range(2):
                        ins = pool.tensor_tensor(heads(q_cos[:, :, :])[:, a], heads(qn[:, :, :])[:, a],
                                                 bc(rot_c[:, t, a, :].unsqueeze(1), [P, NH, HD]), ALU.mult)
                        ins.then_inc((cos_ready if a else cos_half).s, 1)
                    pool.wait_ge(sin_ready.s, sin_ready.at(it, t + 1))
                    pool.wait_ge(cos_ready.s, cos_ready.at(it, t + 1))
                    if t:
                        pool.wait_ge(k_turned.s, k_turned.at(it, t))
                    pool.tensor_tensor(qr[:, :, :], q_cos[:, :, :], q_sin[:, :, :], ALU.add).then_inc(qr_ready.s, 1)
                pool.wait_ge(xa_ready.s, xa_ready.at(it, 1))
                pool.wait_ge(xo_ready.s, xo_ready.at(it, 0))
                pool.tensor_tensor(xa2[:, :, :], xa[:, :, :], bc(b2_row[:, :].unsqueeze(1), [P, TT, D]), ALU.add)\
                    .then_inc(xa2_ready.s, 1)
                pool.wait_ge(mv_ready.s, mv_ready.at(it, TT))
                pool.tensor_tensor(veps[:, :], mv[:, :, 1], eps[:, :], ALU.add).then_inc(g_steps.s, 1)
                pool.wait_ge(g_steps.s, g_steps.at(it, 1))
                pool.tensor_tensor(rstd[:, :], veps[:, :], mhalf[:, 0:TT], ALU.pow).then_inc(rstd_ready.s, 1)

            turns(pool, body)

        def normalise(dve, it, u):
            qt, g = u // 2, u % 2
            ps = ps_o[:, g, 0:HPU * E1].rearrange("p (h e) -> p h e", h=HPU)
            dve.wait_ge(pv_done.s, pv_done.at(it, u + 1))
            dve.reciprocal(inv[:, g, :], ps[:, :, HD]).then_inc(inv_ready.s, 1)
            dve.wait_ge(inv_ready.s, inv_ready.at(it, u + 1))
            dve.tensor_tensor(o[:, qt, g * HPU * HD:(g + 1) * HPU * HD].rearrange("p (h e) -> p h e", h=HPU), ps[:, :, 0:HD],
                              bc(inv[:, g, :].unsqueeze(2), [P, HPU, HD]), ALU.mult).then_inc(o_ready.s, 1)

        @block.vector
        def _(dve):
            dve.wait_ge(s_c, 7)
            dve.wait_ge(s_t, 48)
            st = Steps(v_steps, dve)

            def take_k(it, t):
                dve.wait_ge(k_turned.s, k_turned.at(it, t + 1))
                dve.tensor_copy(kT[:, :, t * P:(t + 1) * P], ps_t[:, 1, :].rearrange("p (c n) -> p c n", c=IC))\
                    .then_inc(kT_ready.s, 1)

            def layer(l):
                dve.wait_ge(w_in.s, w_in.at(l + 1, 0))
                dve.wait_ge(xo_ready.s, xo_ready.at(l * NB, 0))
                H2 = HD // 2
                every = lambda ap: bc(ap.unsqueeze(1), [P, TT, 2, ap.shape[2]])
                dve.tensor_tensor(rot_c[:, :, :, :], rot_c0[:, :, :, :], every(qk_scale[:, :, :]), ALU.mult).then_inc(rot_ready.s, 1)
                dve.tensor_tensor(rot_s[:, :, :, 0:H2], rot_s0[:, :, :, 0:H2], every(qk_scale[:, :, H2:HD]), ALU.mult)\
                    .then_inc(rot_ready.s, 1)
                dve.tensor_tensor(rot_s[:, :, :, H2:HD], rot_s0[:, :, :, H2:HD], every(qk_scale[:, :, 0:H2]), ALU.mult)\
                    .then_inc(rot_ready.s, 1)

            def body(l, b, it):
                st.turn(it)
                H2 = HD // 2
                for t in range(TT):
                    bank = slot(t)
                    dve.wait_ge(sq_ready.s, sq_ready.at(it, t + 1))
                    dve.tensor_reduce(ss[:, :, :], sq[:, :, :].rearrange("p a (h d) -> p a h d", h=NH), AX.X, ALU.add)\
                        .then_inc(ss_raw.s, 1)
                    dve.wait_ge(ss_raw.s, ss_raw.at(it, t + 1))
                    dve.tensor_scalar(ssc[:, :, :], ss[:, :, :], 1e-24, None, ALU.max).then_inc(ss_ready.s, 1)
                    dve.wait_ge(rn_ready.s, rn_ready.at(it, t + 1))
                    if t:
                        dve.wait_ge(cos_ready.s, cos_ready.at(it, t))
                        dve.wait_ge(qr_ready.s, qr_ready.at(it, t))
                    for a in range(2):
                        ins = dve.tensor_tensor(qn[:, a, :].rearrange("p (h d) -> p h d", h=NH),
                                                ps_s[:, bank + a, :].rearrange("p (h d) -> p h d", h=NH),
                                                bc(rn[:, a, :].unsqueeze(2), [P, NH, HD]), ALU.mult)
                        ins.then_inc((qn_ready if a else qn_half).s, 1)
                    dve.wait_ge(qn_half.s, qn_half.at(it, t + 1))
                    dve.wait_ge(qn_ready.s, qn_ready.at(it, t + 1))
                    if t == 0:
                        dve.wait_ge(rot_ready.s, rot_ready.at(l + 1, 0))
                    heads = lambda ap: ap.rearrange("p a (h d) -> p a h d", h=NH)
                    for n in range(2):
                        for a in range(2):
                            to, of = slice(n * H2, n * H2 + H2), slice(H2 - n * H2, HD - n * H2)
                            ins = dve.tensor_tensor(heads(q_sin[:, :, :])[:, a, :, to], heads(qn[:, :, :])[:, a, :, of],
                                                    bc(rot_s[:, t, a, to].unsqueeze(1), [P, NH, H2]), ALU.mult)
                            ins.then_inc((sin_ready if n and a else sin_part).s, 1)
                    if t:
                        take_k(it, t - 1)
                take_k(it, TT - 1)
                for u in range(UNITS + 1):
                    if u < UNITS:
                        dve.wait_ge(scores.s, scores.at(it, u + 1))
                        src = ps_s[:, slot(u):slot(u) + 2, :].rearrange("p a (h n) -> p (a h) n", h=2)
                        dve.tensor_reduce(negmax[:, u, :], src[:, :, 0:P * nk(u)], AX.X, ALU.max, negate=True)\
                            .then_inc(max_ready.s, 1)
                    if u:
                        r = u - 1
                        dve.wait_ge(p_turned.s, p_turned.at(it, r + 1))
                        if r >= 2:
                            dve.wait_ge(pv_done.s, pv_done.at(it, r - 1))
                        if nk(r) == 2:
                            dve.tensor_copy(pt[:, r % 2, :].rearrange("p (a n) -> p a n", a=2), ps_t[:, :, :])\
                                .then_inc(pt_ready.s, 1)
                        else:
                            dve.tensor_copy(pt[:, r % 2, 0:512], ps_t[:, r, :]).then_inc(pt_ready.s, 1)
                    if u >= 2:
                        normalise(dve, it, u - 2)
                normalise(dve, it, UNITS - 1)
                dve.wait_ge(wo_done.s, wo_done.at(it, 1))
                dve.wait_ge(xa2_ready.s, xa2_ready.at(it, 0))
                dve.wait_ge(hn_ready.s, hn_ready.at(it, 0))
                dve.tensor_tensor(xa[:, :, :], ps_x, x_sb[:, :, :], ALU.add).then_inc(xa_ready.s, 1)
                dve.wait_ge(xa_ready.s, xa_ready.at(it, 1))
                for t in range(TT):
                    st.done(dve.bn_stats(stats[:, t, 0:6], xa[:, t, 0:P]))
                dve.wait_ge(shifted.s, shifted.at(it, 32))
                for t in range(TT):
                    st.done(dve.bn_stats(stats[:, t, 6:12], xsh[:, t, :]))
                dve.wait_ge(st.s, st.at(2 * TT))
                dve.memset(tick[:, :], 0.0).then_inc(ticks.s, 1)
                for t in range(TT):
                    dve.bn_aggr(mv[:, t, :], stats[:, t, :]).then_inc(mv_ready.s, 1)
                dve.wait_ge(rstd_ready.s, rstd_ready.at(it, 1))
                for t in range(TT):
                    for half, src in enumerate((xa[:, t, 0:P], xsh[:, t, :])):
                        dve.tensor_scalar(hn[:, t, half * P:(half + 1) * P], src, mv[:, t, 0:1], rstd[:, t:t + 1],
                                          ALU.subtract, ALU.mult).then_inc(hn_ready.s, 1)
                for j in range(JC):
                    m = jj(j)
                    dve.wait_ge(gl_ready.s, gl_ready.at(it, j + 1))
                    dve.scalar_tensor_tensor(hid[0:m, j, :], ps_s[0:m, slot(j), :], b1_cols[0:m, 0, j:j + 1],
                                             gl[0:m, j % 2, :], ALU.add, ALU.mult).then_inc(hid_ready.s, 1)
                dve.wait_ge(y_done.s, y_done.at(it, 1))
                dve.wait_ge(xa2_ready.s, xa2_ready.at(it, 1))
                dve.wait_ge(stored.s, stored.at(it, 0))
                dve.tensor_tensor(xo[:, :, :], ps_y, xa2[:, :, :], ALU.add).then_inc(xo_ready.s, 1)
                st.end()

            turns(dve, body, layer)

        @block.scalar
        def _(act):
            act.wait_ge(s_c, 7)

            def take_q(it, t):
                act.wait_ge(q_turned.s, q_turned.at(it, t + 1))
                act.activation(qT[:, :, t * P:(t + 1) * P], ps_t[:, 0, :].rearrange("p (c n) -> p c n", c=IC), ACT.Copy)\
                    .then_inc(qT_ready.s, 1)

            def body(l, b, it):
                act.wait_ge(w_in.s, w_in.at(l + 1, 0))
                for k in range(DC):
                    act.wait_ge(x_turned.s, x_turned.at(it, k + 1))
                    act.activation(xT[:, k, k:k + T], ps_t[:, k, :], ACT.Copy).then_inc(xT_ready.s, 1)
                for t in range(TT):
                    act.wait_ge(q_proj.s, q_proj.at(it, t + 1))
                    if t:
                        act.wait_ge(ss_raw.s, ss_raw.at(it, t))
                    for a in range(2):
                        act.activation(sq[:, a, :], ps_s[:, slot(t) + a, :], ACT.Square)\
                            .then_inc((sq_ready if a else sq_half).s, 1)
                    act.wait_ge(v_proj.s, v_proj.at(it, t + 1))
                    act.activation(v[:, t, :, 0:HD], ps_o[:, t % 2, :].rearrange("p (h d) -> p h d", h=NH), ACT.Copy)\
                        .then_inc(v_ready.s, 1)
                    if t:
                        take_q(it, t - 1)
                take_q(it, TT - 1)
                for u in range(UNITS):
                    act.wait_ge(max_ready.s, max_ready.at(it, u + 1))
                    if u >= 2:
                        act.wait_ge(p_turned.s, p_turned.at(it, u - 1))
                    src = ps_s[:, slot(u):slot(u) + 2, :].rearrange("p a (h n) -> p (a h) n", h=2)
                    for i in range(HPU):
                        act.activation(pr[:, u % 2, i, 0:P * nk(u)], src[:, i, 0:P * nk(u)], ACT.Exp,
                                       bias=negmax[:, u, i:i + 1]).then_inc((exp_ready if i == HPU - 1 else exp_part).s, 1)
                for c in range(IC):
                    act.wait_ge(o_turned.s, o_turned.at(it, c + 1))
                    act.activation(oT[:, c, :], ps_t[:, c % 2, :], ACT.Copy).then_inc(oT_ready.s, 1)
                for k in range(DC):
                    act.wait_ge(h_turned.s, h_turned.at(it, k + 1))
                    act.activation(hT[:, k, :], ps_t[:, k, :], ACT.Identity, bias=ln_cols[:, k, 1:2],
                                   scale=ln_cols[:, k, 0:1]).then_inc(hT_ready.s, 1)
                for j in range(JC):
                    m = jj(j)
                    act.wait_ge(ag_proj.s, ag_proj.at(it, j + 1))
                    if j >= 2:
                        act.wait_ge(hid_ready.s, hid_ready.at(it, j - 1))
                    act.activation(gl[0:m, j % 2, :], ps_s[0:m, slot(j) + 1, :], ACT.Gelu, bias=b1_cols[0:m, 1, j:j + 1])\
                        .then_inc(gl_ready.s, 1)

            turns(act, body)

        @block.tensor
        def _(pe):
            pe.wait_ge(s_c, 7)

            def body(l, b, it):
                pe.wait_ge(w_in.s, w_in.at(l + 1, 0))
                pe.wait_ge(x_in.s, x_in.at(it, 16))
                pe.wait_ge(xo_ready.s, xo_ready.at(it, 0))
                for k in range(DC):
                    for t in range(TT):
                        last = pe.transpose(ps_t[:, k, t * P:(t + 1) * P], x_sb[:, t, k * P:(k + 1) * P], W["ident"][:, :])
                    last.then_inc(x_turned.s, 1)
                pe.wait_ge(xT_ready.s, xT_ready.at(it, DC))

                def turn_qk(t):
                    pe.wait_ge(qr_ready.s, qr_ready.at(it, t + 1))
                    if t:
                        pe.wait_ge(qT_ready.s, qT_ready.at(it, t))
                        pe.wait_ge(kT_ready.s, kT_ready.at(it, t))
                    for a in range(2):
                        for c in range(IC):
                            last = pe.transpose(ps_t[:, a, c * P:(c + 1) * P], qr[:, a, c * P:(c + 1) * P], W["ident"][:, :])
                        last.then_inc((k_turned if a else q_turned).s, 1)

                for t in range(TT + 2):
                    if t < TT:
                        if t >= 2:
                            pe.wait_ge(qn_ready.s, qn_ready.at(it, t - 1))
                            pe.wait_ge(v_ready.s, v_ready.at(it, t - 1))
                        else:
                            pe.wait_ge(o_ready.s, o_ready.at(it, 0))
                        for a in range(3):
                            dst = ps_o[:, t % 2, :] if a == 2 else ps_s[:, slot(t) + a, :]
                            for k in range(DC):
                                last = pe.matmul(dst, xT[:, k, t * P:(t + 1) * P], w_qkv[:, k, a * INNER:(a + 1) * INNER],
                                                 start=(k == 0), stop=(k == DC - 1))
                            if a:
                                last.then_inc((q_proj if a == 1 else v_proj).s, 1)
                    if t >= 2:
                        turn_qk(t - 2)
                pe.wait_ge(qT_ready.s, qT_ready.at(it, TT))
                pe.wait_ge(kT_ready.s, kT_ready.at(it, TT))
                pe.wait_ge(v_ready.s, v_ready.at(it, TT))
                for u in range(UNITS + 2):
                    if u < UNITS:
                        qt = u // 2
                        if u >= 2:
                            pe.wait_ge(exp_ready.s, exp_ready.at(it, u - 1))
                        for i in range(HPU):
                            h = u % 2 * HPU + head(i)
                            rows = slice(64 * (h % 2), 64 * (h % 2) + 64)
                            n = P * nk(u)
                            dst = ps_s[:, slot(u) + i // 2, i % 2 * 2 * P:i % 2 * 2 * P + n]
                            pe.matmul(dst, identb[:, :], mask[:, 2 * P - n:2 * P], start=True, stop=False)
                            last = pe.matmul(dst, qT[rows, h // 2, qt * P:(qt + 1) * P],
                                             kT[rows, h // 2, (qt + 1) * P - n:(qt + 1) * P], start=False, stop=True)
                        last.then_inc(scores.s, 1)
                    if 1 <= u <= UNITS:
                        r = u - 1
                        pe.wait_ge(exp_ready.s, exp_ready.at(it, r + 1))
                        if r >= 2:
                            pe.wait_ge(pt_ready.s, pt_ready.at(it, r))
                        for i in range(HPU):
                            for n in range(nk(r)):
                                at = i * nk(r) + n
                                bank = at // 4 if nk(r) == 2 else r
                                last = pe.transpose(ps_t[:, bank, at % 4 * P:(at % 4 + 1) * P],
                                                    pr[:, r % 2, i, n * P:(n + 1) * P], W["ident"][:, :])
                        last.then_inc(p_turned.s, 1)
                    if u >= 2:
                        r = u - 2
                        qt = r // 2
                        pe.wait_ge(pt_ready.s, pt_ready.at(it, r + 1))
                        if r >= 2:
                            pe.wait_ge(o_ready.s, o_ready.at(it, r - 1))
                        for i in range(HPU):
                            for n in range(nk(r)):
                                at = i * nk(r) + n
                                last = pe.matmul(ps_o[:, r % 2, head(i) * E1:(head(i) + 1) * E1], pt[:, r % 2, at * P:(at + 1) * P],
                                                 v[:, qt - nk(r) + 1 + n, r % 2 * HPU + head(i), :],
                                                 start=(n == 0), stop=(n == nk(r) - 1))
                        last.then_inc(pv_done.s, 1)
                pe.wait_ge(o_ready.s, o_ready.at(it, UNITS))
                for c in range(IC):
                    if c >= 2:
                        pe.wait_ge(oT_ready.s, oT_ready.at(it, c - 1))
                    for t in range(TT):
                        last = pe.transpose(ps_t[:, c % 2, t * P:(t + 1) * P], o[:, t, c * P:(c + 1) * P], W["ident"][:, :])
                    last.then_inc(o_turned.s, 1)
                pe.wait_ge(oT_ready.s, oT_ready.at(it, IC))
                for t in range(TT):
                    for c in range(IC):
                        last = pe.matmul(ps_x[:, t, :], oT[:, c, t * P:(t + 1) * P], w_o[:, c, :],
                                         start=(c == 0), stop=(c == IC - 1))
                last.then_inc(wo_done.s, 1)
                pe.wait_ge(hn_ready.s, hn_ready.at(it, 2 * TT))
                for k in range(DC):
                    for t in range(TT):
                        last = pe.transpose(ps_t[:, k, t * P:(t + 1) * P], hn[:, t, k * P:(k + 1) * P], W["ident"][:, :])
                    last.then_inc(h_turned.s, 1)
                pe.wait_ge(hT_ready.s, hT_ready.at(it, DC))
                pe.wait_ge(xa_ready.s, xa_ready.at(it, 1))
                for j in range(JC):
                    m = jj(j)
                    if j >= 2:
                        pe.wait_ge(hid_ready.s, hid_ready.at(it, j - 1))
                    for a in range(2):
                        for k in range(DC):
                            last = pe.matmul(ps_s[0:m, slot(j) + a, :], w_1[:, k, a * HID + j * P:a * HID + j * P + m],
                                             hT[:, k, :], start=(k == 0), stop=(k == DC - 1))
                    last.then_inc(ag_proj.s, 1)
                pe.wait_ge(hid_ready.s, hid_ready.at(it, JC))
                for t in range(TT):
                    for j in range(JC):
                        m = jj(j)
                        last = pe.matmul(ps_y[:, t, :], hid[0:m, j, t * P:(t + 1) * P], w_2[0:m, j, :],
                                         start=(j == 0), stop=(j == JC - 1))
                last.then_inc(y_done.s, 1)

            turns(pe, body)


def add_streams(nc, base_dram, last_dram, out, NB):
    T, D = 512, 256
    TT = T // P
    with ExitStack() as ctx:
        sems = []

        def S(name, per):
            sems.append(Sem(ctx, nc, name, per))
            return sems[-1]

        one = ctx.enter_context(nc.sbuf_tensor("d_one", [P, 2, TT, D], F32))
        two = ctx.enter_context(nc.sbuf_tensor("d_two", [P, 2, TT, D], F32))
        loaded = [S(f"d_loaded{i}", 32) for i in range(2)]
        added = [S(f"d_added{i}", 1) for i in range(2)]
        stored = [S(f"d_stored{i}", 16) for i in range(2)]
        seed(nc, sems)
        tiles = lambda ap: ap.rearrange("(t p) d -> p t d", p=P)
        with nc.Block() as block:
            @block.sync
            def _(sp):
                with sp.Fori(0, NB // 2) as n:
                    for i in range(2):
                        sp.wait_ge(stored[i].s, stored[i].at(n, 0))
                        sp.dma_start(one[:, i, :, :], tiles(base_dram[n * 2 + i])).then_inc(loaded[i].s, 16)
                        sp.dma_start(two[:, i, :, :], tiles(last_dram[n * 2 + i])).then_inc(loaded[i].s, 16)

            @block.vector
            def _(dve):
                with dve.Fori(0, NB // 2) as n:
                    for i in range(2):
                        dve.wait_ge(loaded[i].s, loaded[i].at(n, 32))
                        dve.tensor_tensor(one[:, i, :, :], one[:, i, :, :], two[:, i, :, :], ALU.add).then_inc(added[i].s, 1)

            @block.scalar
            def _(act):
                with act.Fori(0, NB // 2) as n:
                    for i in range(2):
                        act.wait_ge(added[i].s, added[i].at(n, 1))
                        act.dma_start(tiles(out[n * 2 + i]), one[:, i, :, :]).then_inc(stored[i].s, 16)
                for i in range(2):
                    act.wait_ge(stored[i].s, stored[i].at(NB // 2, 0))


def build(nc, io, out, NB):
    x1_dram = nc.dram_tensor("x1_scratch", [NB, 512, 256], F32).ap()
    bc_dram = nc.dram_tensor("bc_scratch", [NB, 32, 512], F32).ap()
    base_dram = nc.dram_tensor("base_scratch", [NB, 512, 256], F32).ap()
    stream = nc.dram_tensor("stream_scratch", [3, NB, 512, 256], F32).ap()
    with ExitStack() as ctx:
        W = {"ident": ctx.enter_context(nc.sbuf_tensor("ident", [P, P], F32))}
        with ExitStack() as first:
            for name, shape in (("gateT", [P, 2, 704]), ("upT", [P, 2, 704]), ("downT", [P, 6, 256])):
                W[name] = first.enter_context(nc.sbuf_tensor(name, shape, F32))
            prepare_fp4_weights(nc, io, W)
            mamba_and_fp4_ffn(nc, io, W, x1_dram, bc_dram, NB)
        block_sparse_attention(nc, io, W, x1_dram, stream[0], base_dram, NB)
        local_attention_layers(nc, io, W, stream, NB)
        add_streams(nc, base_dram, stream[2], out, NB)


_PLAIN = ['L0_attn_conv_w', 'L0_attn_A_log', 'L0_ffn_w_gate', 'L0_ffn_w_up', 'L0_ffn_w_down',
          'L1_attn_b_qkv', 'L1_attn_b_out', 'L1_ffn_wqkv', 'L1_ffn_wo', 'L1_ffn_w1', 'L1_ffn_w2',
          'L1_ffn_q_scale', 'L1_ffn_k_scale', 'L1_ffn_b2']
_TURNED = {'W_inT': 'L0_attn_W_in', 'W_xprojT': 'L0_attn_W_xproj', 'W_dtT': 'L0_attn_W_dt', 'W_outT': 'L0_attn_W_out',
           'L1_w_qkvT': 'L1_attn_w_qkv', 'L1_w_outT': 'L1_attn_w_out'}


def _columns(v):
    return np.asarray(v).reshape(-1, P).T


def _layouts(inputs):
    a = {name: np.asarray(inputs[name]) for name in _PLAIN}
    a.update({name: np.asarray(inputs[src]).T for name, src in _TURNED.items()})
    a["mamba_cols"] = np.stack([_columns(inputs[n]) for n in ('L0_attn_conv_b', 'L0_attn_b_dt', 'L0_attn_D_param')],
                               axis=1)
    a["qk_bias_cols"] = _columns(np.asarray(inputs["L1_attn_b_qkv"])[:512])
    a["head_mask"] = np.where(np.arange(P)[:, None] % 64 // 16 == np.arange(4)[None, :], 0.25, 0.0).astype(np.float32)
    a["ln_cols"] = np.stack([np.stack([_columns(v) for v in np.asarray(inputs[n])])
                             for n in ('L1_ffn_ln_g', 'L1_ffn_ln_b')], axis=3)
    b1 = np.zeros((2, 2, 768), np.float32)
    b1[:, :, :682] = np.asarray(inputs['L1_ffn_b1']).reshape(2, 2, 682)
    a["b1_cols"] = b1.reshape(2, 2, 6, P).transpose(0, 3, 1, 2)
    a.update(_rotary_tables())
    return a


def _rotary_tables():
    n, d, window = 512, 64, 128
    f = np.float32
    half = np.arange(0, d, 2, dtype=f)
    freqs = np.arange(n, dtype=f)[:, None] * (f(1.0) / f(10000.0) ** (half / f(d)))[None, :]
    base = (half + f(0.4 * d)) / f(1.4 * d)
    scale = base[None, :] ** ((np.arange(n, dtype=f) - n // 2) / f(window // 2))[:, None]
    freqs, scale = (np.concatenate([t, t], axis=1).astype(f) for t in (freqs, scale))
    cos, sin = np.cos(freqs), np.sin(freqs)
    sin[:, :d // 2] *= -1
    qk = lambda t: np.stack([t * scale * f(8.0), t / scale], axis=1).astype(f)
    i, j = np.arange(P)[:, None], np.arange(P)[None, :]
    mask = np.concatenate([np.where(j >= i, 0.0, -1e30), np.where(j <= i, 0.0, -1e30)], axis=1).astype(f)
    return {"rot_cos": qk(cos), "rot_sin": qk(sin), "window_mask": mask}


def kernel(**inputs):
    import numpy as _np
    import concourse.bacc as _bacc
    from concourse import mybir as _mybir
    from concourse.bass_utils import run_bass_kernel_spmd as _run

    nc = _bacc.Bacc("TRN2", target_bir_lowering=False, num_devices=1)
    arrays, io = {}, {}
    named = _layouts(inputs)
    named["x"] = _np.asarray(inputs["L0_attn_x"])
    for name, a in named.items():
        a = _np.ascontiguousarray(a)
        arrays[f"in_{name}_dram"] = a
        io[name] = nc.dram_tensor(f"in_{name}_dram", a.shape, _mybir.dt.from_np(a.dtype), kind="ExternalInput").ap()
    NB = io["x"].shape[0]
    out = nc.dram_tensor("out_0_dram", (NB, 512, 256), F32, kind="ExternalOutput").ap()
    build(nc, io, out, NB)
    r = _run(nc, [arrays], core_ids=[0])
    return r.results[0]["out_0_dram"]
```

```python
from contextlib import ExitStack

import numpy as np

import concourse.bass as bass
from concourse import mybir

ALU = mybir.AluOpType
ACT = mybir.ActivationFunctionType
F32 = mybir.dt.float32
BF16 = mybir.dt.bfloat16
U32 = mybir.dt.uint32
AX = mybir.AxisListType

P = 128
SIGN_BIT = 0x80000000
LN_EPS = 1e-5


class Sem:

    def __init__(self, ctx, nc, name, per):
        self.s = ctx.enter_context(nc.semaphore(name))
        self.per = per

    def at(self, it, k):
        assert 0 <= k <= self.per, (k, self.per)
        return it * self.per + k + 1


def seed(nc, sems):
    with nc.Block() as block:
        @block.gpsimd
        def _(pool):
            for sem in sems:
                pool.sem_inc(sem.s, 1)


class Steps:

    def __init__(self, sem, eng):
        self.sem, self.s, self.eng, self.it, self.k = sem, sem.s, eng, 0, 0

    def turn(self, it):
        self.it, self.k = it, 0

    def at(self, k):
        return self.sem.at(self.it, k)

    def done(self, ins):
        ins.then_inc(self.s, 1)
        self.k += 1
        return self.k

    def link(self, ins):
        self.eng.wait_ge(self.s, self.at(self.done(ins)))

    def end(self):
        assert self.k == self.sem.per, (self.s, self.k, self.sem.per)


def bc(ap, shape):
    return ap.broadcast_to(shape)


def fp4_steps(dve, st, src, out, blk, work, p, n):
    g = n // 16
    amax, scale, inv = blk[0:p, 0, 0:g], blk[0:p, 1, 0:g], blk[0:p, 2, 0:g]
    a, s, w = work[0:p, 0, 0:n], work[0:p, 1, 0:n], work[0:p, 2, 0:n]

    def blocks(ap):
        return ap.rearrange("p (g e) -> p g e", e=16)

    st.link(dve.tensor_reduce(amax, blocks(src), AX.X, ALU.max, apply_absolute_value=True))
    st.link(dve.tensor_scalar(scale, amax, 1.0 / 6.0, 1e-12, ALU.mult, ALU.max))
    st.link(dve.reciprocal(inv, scale))
    st.link(dve.tensor_tensor(blocks(a), blocks(src), bc(inv.unsqueeze(2), [p, g, 16]), ALU.mult))
    st.link(dve.tensor_scalar(a.bitcast(U32), a.bitcast(U32), SIGN_BIT - 1, None, ALU.bitwise_and))
    s1 = st.done(dve.tensor_scalar(s, a, 0.25, None, ALU.is_gt))
    w1 = st.done(dve.tensor_scalar(w, a, 5.0, 2.0, ALU.is_gt, ALU.mult))
    dve.wait_ge(st.s, st.at(s1))
    s1 = st.done(dve.scalar_tensor_tensor(s, a, 0.75, s, ALU.is_gt, ALU.add))
    dve.wait_ge(st.s, st.at(w1))
    w1 = st.done(dve.scalar_tensor_tensor(w, a, 2.5, w, ALU.is_gt, ALU.add))
    dve.wait_ge(st.s, st.at(s1))
    s1 = st.done(dve.scalar_tensor_tensor(s, a, 1.25, s, ALU.is_gt, ALU.add))
    dve.wait_ge(st.s, st.at(w1))
    w1 = st.done(dve.scalar_tensor_tensor(w, a, 3.5, w, ALU.is_gt, ALU.add))
    dve.wait_ge(st.s, st.at(s1))
    s1 = st.done(dve.scalar_tensor_tensor(s, a, 1.75, s, ALU.is_gt, ALU.add))
    dve.wait_ge(st.s, st.at(s1))
    dve.wait_ge(st.s, st.at(w1))
    st.link(dve.scalar_tensor_tensor(s, s, 0.5, w, ALU.mult, ALU.add))
    st.link(dve.tensor_tensor(blocks(s), blocks(s), bc(scale.unsqueeze(2), [p, g, 16]), ALU.mult))
    return dve.scalar_tensor_tensor(out.bitcast(U32), src.bitcast(U32), SIGN_BIT, s.bitcast(U32),
                                    ALU.bitwise_and, ALU.bitwise_or)


FP4_STEPS = 14


def prepare_fp4_weights(nc, io, W):
    RT, NT = 88, 8
    H, I = 256, 704
    with ExitStack() as ctx:
        sb = lambda n, s, d=F32: ctx.enter_context(nc.sbuf_tensor(n, s, d))
        sem = lambda n: ctx.enter_context(nc.semaphore(n))
        up_raw = sb("up_raw", [RT, 2, NT * H])
        down_raw = sb("down_raw", [P, 2 * I])
        up_q = sb("up_q", [RT, 2, NT * H])
        down_q = sb("down_q", [P, 2 * I])
        blk = sb("w_blk", [P, 3, NT * H // 16])
        work = sb("w_work", [P, 3, NT * H])
        turned = ctx.enter_context(nc.psum_tensor("w_turned", [P, 4, 512], F32))
        loaded, quant, turned_ready, copied, ident0 = map(sem, ("w_loaded", "w_quant", "w_turned_s", "w_copied", "w_ident0"))
        ident_ready = sem("ident_ready")
        steps_sem = Sem(ctx, nc, "w_steps", 3 * FP4_STEPS)
        seed(nc, [steps_sem])
        block = ctx.enter_context(nc.Block())

        @block.sync
        def _(sp):
            for n, w in enumerate((io["L0_ffn_w_gate"], io["L0_ffn_w_up"])):
                sp.dma_start(up_raw[:, n, :].rearrange("p (t k) -> p t k", t=NT),
                             w.rearrange("(t p) k -> p t k", p=RT)).then_inc(loaded, 16)
                sp.wait_ge(loaded, 16 * (n + 1))
            sp.dma_start(down_raw[:, :].rearrange("p (t k) -> p t k", t=2),
                         io["L0_ffn_w_down"].rearrange("(t p) k -> p t k", p=P)).then_inc(loaded, 16)

        @block.gpsimd
        def _(pool):
            pool.memset(W["ident"][:, :], 0.0).then_inc(ident0, 1)
            pool.wait_ge(ident0, 1)
            pool.affine_select(out=W["ident"][:, :], in_=W["ident"][:, :], compare_op=ALU.not_equal, fill=1.0,
                               base=0, pattern=[[-1, P]], channel_multiplier=1).then_inc(ident_ready, 1)

        @block.vector
        def _(dve):
            st = Steps(steps_sem, dve)
            for n in range(2):
                dve.wait_ge(loaded, 16 * (n + 1))
                if n:
                    dve.wait_ge(quant, n)
                fp4_steps(dve, st, up_raw[:, n, :], up_q[:, n, :], blk, work, RT, NT * H).then_inc(quant, 1)
            dve.wait_ge(loaded, 48)
            dve.wait_ge(quant, 2)
            fp4_steps(dve, st, down_raw[:, :], down_q[:, :], blk, work, P, 2 * I).then_inc(quant, 1)
            st.end()

        moves = []
        for n, name in enumerate(("gateT", "upT")):
            for k in range(2):
                for t in range(NT):
                    moves.append((n, up_q[:, n, t * H + k * P:t * H + (k + 1) * P],
                                  W[name][:, k, t * RT:(t + 1) * RT], P, RT))
        for t in range(2):
            for k in range(6):
                kk = min(P, I - k * P)
                moves.append((2, down_q[:, t * I + k * P:t * I + k * P + kk],
                              W["downT"][0:kk, k, t * P:(t + 1) * P], kk, P))

        @block.tensor
        def _(pe):
            pe.wait_ge(ident_ready, 1)
            for i, (n, src, dst, rows, cols) in enumerate(moves):
                pe.wait_ge(quant, n + 1)
                if i >= 4:
                    pe.wait_ge(copied, i - 3)
                pe.transpose(turned[0:rows, i % 4, 0:cols], src, W["ident"][0:cols, 0:cols]).then_inc(turned_ready, 1)

        @block.scalar
        def _(act):
            for i, (n, src, dst, rows, cols) in enumerate(moves):
                act.wait_ge(turned_ready, i + 1)
                act.activation(dst, turned[0:rows, i % 4, 0:cols], ACT.Copy).then_inc(copied, 1)


def mamba_and_fp4_ffn(nc, io, W, x1_dram, bc_dram, NB):
    T, D, DI, NS, R, I = 512, 256, 512, 16, 16, 704
    TT, DC, IC = T // P, D // P, DI // P
    KC = 6
    HALF = I // 2
    NG = 2
    GROUPS = NS // NG
    SCANS = GROUPS * IC
    RING = 4

    with ExitStack() as ctx:
        sb = lambda n, s, d=F32: ctx.enter_context(nc.sbuf_tensor(n, s, d))
        sems = []

        def S(name, per):
            sems.append(Sem(ctx, nc, name, per))
            return sems[-1]

        w_in = sb("w_in", [P, DC, 2 * DI])
        w_xp = sb("w_xp", [P, IC, R + 2 * NS])
        w_dt = sb("w_dt", [64, DI])
        w_out = sb("w_out", [P, IC, D])
        conv_w = sb("conv_w", [P, IC, 4])
        cols = sb("cols", [P, 3, IC])
        a_neg = sb("a_neg", [P, IC, NS])
        a_log = sb("a_log", [P, IC, NS])
        mhalf = sb("mhalf", [P, TT])
        eps = sb("eps", [P, TT])
        tick = sb("tick", [P, 1])

        x_sb = sb("x_sb", [P, TT, D])
        stats = sb("stats", [P, TT, 6])
        mv = sb("mv", [P, TT, 2])
        rstd = sb("rstd", [P, TT])
        veps = sb("veps", [P, TT])
        xn = sb("xn", [P, TT, D])
        xq = sb("xq", [P, TT, D])
        xnT = sb("xnT", [P, DC, T])
        xqT = sb("xqT", [P, DC, T])
        xin = sb("xin", [P, IC, T + 3])
        cv = sb("cv", [P, IC, T])
        u = sb("u", [P, IC, T])
        sz = sb("sz", [P, IC, T])
        xd = sb("xd", [64, T])
        sp_t = sb("sp_t", [P, IC, T])
        delta = sb("delta", [P, IC, T])
        du = sb("du", [P, IC, T])
        y = sb("y", [P, IC, T])
        bcB = sb("bcB", [P, 2, NG, T])
        bcC = sb("bcC", [P, 2, NG, T])
        dA = sb("dA", [P, 2, NG, T])
        hb = sb("hb", [P, RING, NG, T])
        blk = sb("blk", [P, 3, TT * D // 16])
        work = sb("work", [P, 3, TT * D])
        sg = sb("sg", [P, I])
        h = sb("h", [P, I])
        hq = sb("hq", [P, I])
        hqT = sb("hqT", [P, KC, T])

        ps_t = ctx.enter_context(nc.psum_tensor("ps_t", [P, 2, 512], F32))
        ps_p = ctx.enter_context(nc.psum_tensor("ps_p", [P, 2, 512], F32))
        ps_f = ctx.enter_context(nc.psum_tensor("ps_f", [P, 4, 512], F32))
        ps_o = ps_f[:, 0:2, :].rearrange("p a (b d) -> p (a b) d", b=2)

        s_w = ctx.enter_context(nc.semaphore("a_weights"))
        s_zero = ctx.enter_context(nc.semaphore("a_zeroed"))
        s_aneg = ctx.enter_context(nc.semaphore("a_negA"))
        x_in = S("a_x_in", 16)
        v_steps = S("a_v_steps", TT + (1 + TT) * FP4_STEPS + 3 * IC + SCANS)
        ticks = S("a_ticks", 1)
        mv_ready = S("a_mv", TT)
        g_steps = S("a_g_steps", 1)
        rstd_ready = S("a_rstd", 1)
        xn_ready = S("a_xn", TT)
        xq_ready = S("a_xq", 1)
        turned = S("a_turned", 4 + 2 * TT)
        taken = S("a_taken", 4 + 2 * TT)
        taken_k4 = S("a_taken_k4", TT)
        proj = S("a_proj", 2 * IC + 1 + IC)
        xin_ready = S("a_xin", IC)
        z_ready = S("a_z", IC)
        cv_ready = S("a_cv", IC)
        u_ready = S("a_u", IC)
        xd_ready = S("a_xd", 1)
        bc_out = S("a_bc_out", 16)
        bc_in = [S(f"a_bc_in{i}", 32 * GROUPS // 2) for i in range(2)]
        sp_abs = S("a_sp_abs", IC)
        sp_relu = S("a_sp_relu", IC)
        sp_exp = S("a_sp_exp", IC)
        sp_ln = S("a_sp_ln", IC)
        delta_ready = S("a_delta", IC)
        du_ready = S("a_du", IC)
        dA_ready = S("a_dA", SCANS)
        dA_half = S("a_dA_half", SCANS * (NG - 1))
        dBu_ready = S("a_dBu", SCANS)
        scanned = S("a_scanned", SCANS)
        weighed = S("a_weighed", SCANS)
        added = S("a_added", SCANS)
        y0_ready = S("a_y0", IC)
        y_ready = S("a_y", IC)
        gu = S("a_gate_up", TT)
        sg_ready = S("a_sg", TT)
        h_ready = S("a_h", TT)
        hq_ready = S("a_hq", TT)
        out_ready = S("a_out", 1)
        x1_ready = S("a_x1", 1)
        stored = S("a_stored", 16)
        seed(nc, sems)
        block = ctx.enter_context(nc.Block())

        def kk(k):
            return min(P, I - k * P)

        @block.sync
        def _(sp):
            n = 0

            def load(dst, src):
                sp.dma_start(dst, src).then_inc(s_w, 16)

            load(w_in[:, :, :], io["W_inT"].rearrange("(c p) n -> p c n", p=P))
            load(w_xp[:, :, :], io["W_xprojT"].rearrange("(c p) n -> p c n", p=P))
            load(w_out[:, :, :], io["W_outT"].rearrange("(c p) n -> p c n", p=P))
            load(conv_w[:, :, :], io["L0_attn_conv_w"].rearrange("(c p) o k -> p c (o k)", p=P))
            load(a_log[:, :, :], io["L0_attn_A_log"].rearrange("(c p) n -> p c n", p=P))
            load(cols[:, :, :], io["mamba_cols"])
            sp.wait_ge(s_zero, 1)
            load(w_dt[0:R, :], io["W_dtT"])
            with sp.Fori(0, NB) as b:
                sp.wait_ge(stored.s, stored.at(b, 0))
                sp.dma_start(x_sb[:, :, :], io["x"][b].rearrange("(t p) d -> p t d", p=P)).then_inc(x_in.s, 16)
                sp.wait_ge(xd_ready.s, xd_ready.at(b, 1))
                sp.dma_start(bc_dram[b], xd[R:R + 2 * NS, :]).then_inc(bc_out.s, 16)
                sp.wait_ge(bc_out.s, bc_out.at(b, 16))
                for g in range(GROUPS):
                    if g >= 2:
                        sp.wait_ge(weighed.s, weighed.at(b, (g - 1) * IC))
                    sp.dma_start(bcB[:, g % 2, :, :],
                                 bc_dram[b, g * NG:(g + 1) * NG, :].unsqueeze(0).broadcast_to([P, NG, T]))\
                        .then_inc(bc_in[g % 2].s, 16)
                    sp.dma_start(bcC[:, g % 2, :, :],
                                 bc_dram[b, NS + g * NG:NS + (g + 1) * NG, :].unsqueeze(0).broadcast_to([P, NG, T]))\
                        .then_inc(bc_in[g % 2].s, 16)
                sp.wait_ge(x1_ready.s, x1_ready.at(b, 1))
                sp.dma_start(x1_dram[b].rearrange("(t p) d -> p t d", p=P), x_sb[:, :, :]).then_inc(stored.s, 16)
            sp.wait_ge(stored.s, stored.at(NB, 0))

        @block.gpsimd
        def _(pool):
            pool.memset(w_dt[:, :], 0.0).then_inc(s_zero, 1)
            pool.memset(mhalf[:, :], -0.5).then_inc(s_zero, 1)
            pool.memset(xd[:, :], 0.0).then_inc(s_zero, 1)
            pool.memset(eps[:, :], LN_EPS).then_inc(s_zero, 1)
            pool.memset(xin[:, :, 0:3], 0.0).then_inc(s_zero, 1)
            pool.memset(dA[:, :, :, 0:1], 0.0).then_inc(s_zero, 1)
            pool.wait_ge(s_zero, 6)
            with pool.Fori(0, NB) as b:
                pool.wait_ge(mv_ready.s, mv_ready.at(b, TT))
                pool.wait_ge(xn_ready.s, xn_ready.at(b, 0))
                pool.tensor_tensor(veps[:, :], mv[:, :, 1], eps[:, :], ALU.add).then_inc(g_steps.s, 1)
                pool.wait_ge(g_steps.s, g_steps.at(b, 1))
                pool.tensor_tensor(rstd[:, :], veps[:, :], mhalf[:, :], ALU.pow).then_inc(rstd_ready.s, 1)
                for c in range(IC):
                    pool.wait_ge(delta_ready.s, delta_ready.at(b, c + 1))
                    pool.tensor_tensor(du[:, c, :], delta[:, c, :], u[:, c, :], ALU.mult).then_inc(du_ready.s, 1)
                for s in range(SCANS):
                    g, c = divmod(s, IC)
                    pool.wait_ge(bc_in[g % 2].s, bc_in[g % 2].at(b, 32 * (g // 2 + 1)))
                    pool.wait_ge(du_ready.s, du_ready.at(b, c + 1))
                    if s >= RING:
                        pool.wait_ge(added.s, added.at(b, s - RING + 1))
                    else:
                        pool.wait_ge(added.s, added.at(b, 0))
                    pool.tensor_tensor(hb[:, s % RING, :, :], bcB[:, g % 2, :, :],
                                       bc(du[:, c, :].unsqueeze(1), [P, NG, T]), ALU.mult)\
                        .then_inc(dBu_ready.s, 1)

        @block.vector
        def _(dve):
            st = Steps(v_steps, dve)
            dve.wait_ge(s_w, 16 * 7)
            dve.wait_ge(s_zero, 6)
            dve.wait_ge(s_aneg, 1)
            dve.tensor_scalar(a_neg[:, :, :], a_neg[:, :, :], -1.0, None, ALU.mult).then_inc(s_aneg, 1)
            with dve.Fori(0, NB) as b:
                st.turn(b)
                dve.wait_ge(x_in.s, x_in.at(b, 16))
                dve.wait_ge(rstd_ready.s, rstd_ready.at(b, 0))
                for t in range(TT):
                    st.done(dve.bn_stats(stats[:, t, :], x_sb[:, t, :]))
                for t in range(TT):
                    if t == 0:
                        dve.wait_ge(st.s, st.at(TT))
                        dve.memset(tick[:, :], 0.0).then_inc(ticks.s, 1)
                    dve.bn_aggr(mv[:, t, :], stats[:, t, :]).then_inc(mv_ready.s, 1)
                dve.wait_ge(rstd_ready.s, rstd_ready.at(b, 1))
                dve.wait_ge(turned.s, turned.at(b, 0))
                for t in range(TT):
                    dve.tensor_scalar(xn[:, t, :], x_sb[:, t, :], mv[:, t, 0:1], rstd[:, t:t + 1],
                                      ALU.subtract, ALU.mult).then_inc(xn_ready.s, 1)
                dve.wait_ge(xn_ready.s, xn_ready.at(b, TT))
                fp4_steps(dve, st, xn[:, :, :].rearrange("p t d -> p (t d)"),
                          xq[:, :, :].rearrange("p t d -> p (t d)"), blk, work, P, TT * D).then_inc(xq_ready.s, 1)
                dve.wait_ge(xq_ready.s, xq_ready.at(b, 1))
                marks = [0] * IC
                for c in range(IC):
                    dve.wait_ge(xin_ready.s, xin_ready.at(b, c + 1))
                    marks[c] = st.done(dve.tensor_scalar(cv[:, c, :], xin[:, c, 0:T], conv_w[:, c, 0:1], None, ALU.mult))
                for j in range(1, 4):
                    for c in range(IC):
                        dve.wait_ge(st.s, st.at(marks[c]))
                        ins = dve.scalar_tensor_tensor(cv[:, c, :], xin[:, c, j:j + T], conv_w[:, c, j:j + 1],
                                                       cv[:, c, :], ALU.mult, ALU.add)
                        if j < 3:
                            marks[c] = st.done(ins)
                        else:
                            ins.then_inc(cv_ready.s, 1)

                def ffn_hidden(t):
                    dve.wait_ge(sg_ready.s, sg_ready.at(b, t + 1))
                    if t:
                        dve.wait_ge(hq_ready.s, hq_ready.at(b, t))
                    dve.tensor_tensor(h[:, :].rearrange("p (a n) -> p a n", a=2), ps_f[:, 2:4, 0:HALF],
                                      sg[:, :].rearrange("p (a n) -> p a n", a=2), ALU.mult).then_inc(h_ready.s, 1)
                    dve.wait_ge(h_ready.s, h_ready.at(b, t + 1))
                    if t:
                        dve.wait_ge(turned.s, turned.at(b, 4 + 2 * t))
                    fp4_steps(dve, st, h[:, :], hq[:, :], blk, work, P, I).then_inc(hq_ready.s, 1)

                ffn_hidden(0)
                for c in range(IC):
                    dve.wait_ge(sp_abs.s, sp_abs.at(b, c + 1))
                    dve.tensor_scalar(delta[:, c, :], ps_p[:, (1 + c) % 2, :], cols[:, 1, c:c + 1], 0.0,
                                      ALU.add, ALU.max).then_inc(sp_relu.s, 1)
                ffn_hidden(1)
                for c in range(IC):
                    dve.wait_ge(sp_ln.s, sp_ln.at(b, c + 1))
                    dve.wait_ge(sp_relu.s, sp_relu.at(b, c + 1))
                    dve.tensor_tensor(delta[:, c, :], delta[:, c, :], sp_t[:, c, :], ALU.add)\
                        .then_inc(delta_ready.s, 1)
                ffn_hidden(2)
                ffn_hidden(3)
                for c in range(IC):
                    dve.tensor_scalar(y[:, c, :], u[:, c, :], cols[:, 2, c:c + 1], None, ALU.mult)\
                        .then_inc(y0_ready.s, 1)
                flat = lambda ap: ap.rearrange("p n t -> p (n t)")
                for s in range(SCANS + 2):
                    if s < SCANS:
                        dve.wait_ge(dA_ready.s, dA_ready.at(b, s + 1))
                        dve.wait_ge(dBu_ready.s, dBu_ready.at(b, s + 1))
                        tile = flat(hb[:, s % RING, :, :])
                        dve.tensor_tensor_scan(tile, flat(dA[:, s % 2, :, :]), tile, 0.0, ALU.mult, ALU.add)\
                            .then_inc(scanned.s, 1)
                    if s >= 2:
                        r = s - 2
                        c = r % IC
                        dve.wait_ge(st.s, st.at(pair))
                        if r >= IC:
                            dve.wait_ge(added.s, added.at(b, r - IC + 1))
                        else:
                            dve.wait_ge(y0_ready.s, y0_ready.at(b, c + 1))
                        dve.tensor_tensor(y[:, c, :], y[:, c, :], hb[:, r % RING, 0, :], ALU.add)\
                            .then_inc(added.s, 1)
                    if 1 <= s <= SCANS:
                        r = s - 1
                        dve.wait_ge(scanned.s, scanned.at(b, r + 1))
                        tile = hb[:, r % RING, :, :]
                        dve.tensor_tensor(tile, tile, bcC[:, (r // IC) % 2, :, :], ALU.mult)\
                            .then_inc(weighed.s, 1)
                        dve.wait_ge(weighed.s, weighed.at(b, r + 1))
                        pair = st.done(dve.tensor_tensor(tile[:, 0, :], tile[:, 0, :], tile[:, 1, :], ALU.add))
                for c in range(IC):
                    dve.wait_ge(added.s, added.at(b, SCANS - IC + c + 1))
                    dve.tensor_tensor(y[:, c, :], y[:, c, :], sz[:, c, :], ALU.mult).then_inc(y_ready.s, 1)
                dve.wait_ge(out_ready.s, out_ready.at(b, 1))
                dve.tensor_tensor(x_sb[:, :, :], ps_o, x_sb[:, :, :], ALU.add).then_inc(x1_ready.s, 1)
                st.end()

        @block.scalar
        def _(act):
            act.wait_ge(s_w, 16 * 7)
            act.activation(a_neg[:, :, :], a_log[:, :, :], ACT.Exp).then_inc(s_aneg, 1)
            act.wait_ge(s_aneg, 2)
            act.wait_ge(s_zero, 6)
            with act.Fori(0, NB) as b:
                for k in range(DC):
                    act.wait_ge(turned.s, turned.at(b, k + 1))
                    act.activation(xnT[:, k, :], ps_t[:, k, :], ACT.Copy).then_inc(taken.s, 1)
                for c in range(IC):
                    act.wait_ge(proj.s, proj.at(b, c + 1))
                    if c == 0:
                        act.wait_ge(cv_ready.s, cv_ready.at(b, 0))
                    act.activation(xin[:, c, 3:], ps_p[:, c % 2, :], ACT.Copy).then_inc(xin_ready.s, 1)
                for c in range(IC):
                    act.wait_ge(proj.s, proj.at(b, IC + c + 1))
                    if c == 0:
                        act.wait_ge(y_ready.s, y_ready.at(b, 0))
                    act.activation(sz[:, c, :], ps_p[:, c % 2, :], ACT.Silu).then_inc(z_ready.s, 1)
                for k in range(DC):
                    act.wait_ge(turned.s, turned.at(b, 2 + k + 1))
                    act.activation(xqT[:, k, :], ps_t[:, k, :], ACT.Copy).then_inc(taken.s, 1)
                for c in range(IC):
                    act.wait_ge(cv_ready.s, cv_ready.at(b, c + 1))
                    if c == 0:
                        act.wait_ge(du_ready.s, du_ready.at(b, 0))
                    act.activation(u[:, c, :], cv[:, c, :], ACT.Silu, bias=cols[:, 0, c:c + 1]).then_inc(u_ready.s, 1)

                def silu_gate(t):
                    act.wait_ge(gu.s, gu.at(b, t + 1))
                    if t:
                        act.wait_ge(h_ready.s, h_ready.at(b, t))
                    act.activation(sg[:, :].rearrange("p (a n) -> p a n", a=2), ps_f[:, 0:2, 0:HALF], ACT.Silu)\
                        .then_inc(sg_ready.s, 1)

                def take_h(t):
                    act.wait_ge(turned.s, turned.at(b, 4 + 2 * t + 1))
                    act.activation(hqT[:, 0:4, t * P:(t + 1) * P], ps_t[:, 0, :].rearrange("p (k n) -> p k n", k=4),
                                   ACT.Copy).then_inc(taken.s, 1)
                    act.wait_ge(turned.s, turned.at(b, 4 + 2 * t + 2))
                    act.activation(hqT[:, 4, t * P:(t + 1) * P], ps_t[:, 1, 0:P], ACT.Copy).then_inc(taken_k4.s, 1)
                    act.activation(hqT[0:64, 5, t * P:(t + 1) * P], ps_t[0:64, 1, P:2 * P], ACT.Copy)\
                        .then_inc(taken.s, 1)

                silu_gate(0)
                act.wait_ge(proj.s, proj.at(b, 2 * IC + 1))
                act.activation(xd[0:R + 2 * NS, :], ps_p[0:R + 2 * NS, 0, :], ACT.Copy).then_inc(xd_ready.s, 1)
                for c in range(IC):
                    act.wait_ge(proj.s, proj.at(b, 2 * IC + 1 + c + 1))
                    act.activation(sp_t[:, c, :], ps_p[:, (1 + c) % 2, :], ACT.Abs, bias=cols[:, 1, c:c + 1])\
                        .then_inc(sp_abs.s, 1)
                for c in range(IC):
                    act.wait_ge(sp_abs.s, sp_abs.at(b, c + 1))
                    act.activation(sp_t[:, c, :], sp_t[:, c, :], ACT.Exp, scale=-1.0).then_inc(sp_exp.s, 1)
                for c in range(IC):
                    act.wait_ge(sp_exp.s, sp_exp.at(b, c + 1))
                    act.activation(sp_t[:, c, :], sp_t[:, c, :], ACT.Ln, bias=1.0).then_inc(sp_ln.s, 1)
                take_h(0)
                silu_gate(1)
                take_h(1)
                silu_gate(2)
                take_h(2)
                silu_gate(3)
                take_h(3)
                for s in range(SCANS):
                    g, c = divmod(s, IC)
                    act.wait_ge(delta_ready.s, delta_ready.at(b, c + 1))
                    if s >= 2:
                        act.wait_ge(scanned.s, scanned.at(b, s - 1))
                    for n in range(NG):
                        ins = act.activation(dA[:, s % 2, n, 1:], delta[:, c, 1:], ACT.Exp,
                                             scale=a_neg[:, c, g * NG + n:g * NG + n + 1])
                        ins.then_inc((dA_half if n + 1 < NG else dA_ready).s, 1)

        @block.tensor
        def _(pe):
            pe.wait_ge(s_w, 16 * 7)
            pe.wait_ge(s_zero, 6)
            with pe.Fori(0, NB) as b:
                def turn_x(src, k, n):
                    for t in range(TT):
                        last = pe.transpose(ps_t[:, k, t * P:(t + 1) * P], src[:, t, k * P:(k + 1) * P], W["ident"][:, :])
                    last.then_inc(turned.s, 1)

                pe.wait_ge(taken.s, taken.at(b, 0))
                pe.wait_ge(xn_ready.s, xn_ready.at(b, TT))
                for k in range(DC):
                    turn_x(xn, k, k)
                for c in range(2 * IC):
                    if c < DC:
                        pe.wait_ge(taken.s, taken.at(b, DC))
                    if c >= 2:
                        read = xin_ready if c - 2 < IC else z_ready
                        pe.wait_ge(read.s, read.at(b, (c - 2) % IC + 1))
                    else:
                        pe.wait_ge(sp_abs.s, sp_abs.at(b, 0))
                        pe.wait_ge(sp_relu.s, sp_relu.at(b, 0))
                    for k in range(DC):
                        last = pe.matmul(ps_p[:, c % 2, :], w_in[:, k, c * P:(c + 1) * P], xnT[:, k, :],
                                         start=(k == 0), stop=(k == DC - 1))
                    last.then_inc(proj.s, 1)
                pe.wait_ge(xq_ready.s, xq_ready.at(b, 1))
                for k in range(DC):
                    turn_x(xq, k, 2 + k)

                def gate_up(t):
                    if t == 0:
                        pe.wait_ge(taken.s, taken.at(b, 4))
                        pe.wait_ge(x1_ready.s, x1_ready.at(b, 0))
                    else:
                        pe.wait_ge(h_ready.s, h_ready.at(b, t))
                    for n in range(4):
                        w = W["gateT"] if n < 2 else W["upT"]
                        for k in range(DC):
                            last = pe.matmul(ps_f[:, n, 0:HALF], xqT[:, k, t * P:(t + 1) * P],
                                             w[:, k, (n % 2) * HALF:(n % 2 + 1) * HALF],
                                             start=(k == 0), stop=(k == DC - 1))
                    last.then_inc(gu.s, 1)

                def turn_h(t):
                    pe.wait_ge(hq_ready.s, hq_ready.at(b, t + 1))
                    pe.wait_ge(taken.s, taken.at(b, 4 + 2 * t))
                    for k in range(KC):
                        last = pe.transpose(ps_t[0:kk(k), k // 4, (k % 4) * P:(k % 4 + 1) * P],
                                            hq[:, k * P:k * P + kk(k)], W["ident"][:, :])
                        if k in (3, KC - 1):
                            last.then_inc(turned.s, 1)

                gate_up(0)
                pe.wait_ge(u_ready.s, u_ready.at(b, IC))
                pe.wait_ge(z_ready.s, z_ready.at(b, IC))
                for k in range(IC):
                    last = pe.matmul(ps_p[0:R + 2 * NS, 0, :], w_xp[:, k, :], u[:, k, :],
                                     start=(k == 0), stop=(k == IC - 1))
                last.then_inc(proj.s, 1)
                pe.wait_ge(xd_ready.s, xd_ready.at(b, 1))
                for c in range(IC):
                    if c >= 2:
                        pe.wait_ge(sp_abs.s, sp_abs.at(b, c - 1))
                        pe.wait_ge(sp_relu.s, sp_relu.at(b, c - 1))
                    pe.matmul(ps_p[:, (1 + c) % 2, :], w_dt[:, c * P:(c + 1) * P], xd[:, :],
                              start=True, stop=True).then_inc(proj.s, 1)
                turn_h(0)
                for t in range(1, TT):
                    gate_up(t)
                    turn_h(t)
                pe.wait_ge(taken.s, taken.at(b, 4 + 2 * TT))
                pe.wait_ge(y_ready.s, y_ready.at(b, IC))
                pe.wait_ge(h_ready.s, h_ready.at(b, TT))
                for t in range(TT):
                    for k in range(KC):
                        pe.matmul(ps_o[:, t, :], hqT[0:kk(k), k, t * P:(t + 1) * P], W["downT"][0:kk(k), k, :],
                                  start=(k == 0), stop=False)
                    for k in range(IC):
                        last = pe.matmul(ps_o[:, t, :], y[:, k, t * P:(t + 1) * P], w_out[:, k, :],
                                         start=False, stop=(k == IC - 1))
                last.then_inc(out_ready.s, 1)


def block_sparse_attention(nc, io, W, x1_dram, xn_dram, base_dram, NB):
    T, D, NH, HD = 512, 256, 16, 16
    TT, DC = T // P, D // P
    KEYS = [[0, 1, 2, 3], [0, 1], [0, 2], [0, 3]]
    UNIT = [(0, [h]) for h in range(NH)] + [(qt, [h, h + 1]) for qt in range(1, TT) for h in range(0, NH, 2)]
    UNITS = len(UNIT)
    LAST = [max(u for u in range(UNITS) if UNIT[u][0] == qt) for qt in range(TT)]
    TURN_LAG, PV_LAG = 3, 5
    STATS_AT, NORM_AT = 4, 10
    TURN_AT = [22, 28]

    with ExitStack() as ctx:
        sb = lambda n, s, d=F32: ctx.enter_context(nc.sbuf_tensor(n, s, d))
        sems = []

        def S(name, per):
            sems.append(Sem(ctx, nc, name, per))
            return sems[-1]

        w_qkv = sb("b_w_qkv", [P, DC, 3 * D])
        w_o = sb("b_w_o", [P, DC, D])
        qk_bias = sb("b_qk_bias", [P, 4])
        head_mask = sb("b_head_mask", [P, 4])
        v_bias = sb("b_v_bias", [P, D])
        o_bias = sb("b_o_bias", [P, D])
        mhalf = sb("b_mhalf", [P, TT])
        eps = sb("b_eps", [P, TT])
        tick = sb("b_tick", [P, 1])
        x_sb = sb("b_x", [P, TT, D])
        xb = sb("b_xb", [P, TT, D])
        res = sb("b_res", [P, TT, D])
        stats = sb("b_stats", [P, TT, 6])
        mv = sb("b_mv", [P, TT, 2])
        rstd = sb("b_rstd", [P, TT])
        veps = sb("b_veps", [P, TT])
        xn = sb("b_xn", [P, TT, D])
        xT = sb("b_xT", [P, DC, T])
        qm = sb("b_qm", [P, DC, 4, T])
        kf = sb("b_kf", [P, DC, T])
        v = sb("b_v", [P, TT, NH, HD + 1])
        negmax = sb("b_negmax", [P, UNITS, 2])
        pr = sb("b_pr", [P, 4, 512])
        pt = sb("b_pt", [P, 3, 512])
        inv = sb("b_inv", [P, NH])
        o = sb("b_o", [P, TT, D])
        oT = sb("b_oT", [P, DC, T])

        ps_s = ctx.enter_context(nc.psum_tensor("b_ps_s", [P, 4, 512], F32))
        ps_t = ctx.enter_context(nc.psum_tensor("b_ps_t", [P, 2, 512], F32))
        ps_xo = ctx.enter_context(nc.psum_tensor("b_ps_xo", [P, 2, 512], F32))
        ps_v = ps_t[:, :, :].rearrange("p a (b d) -> p (a b) d", b=2)
        ps_y = ps_xo[:, :, :].rearrange("p a (b d) -> p (a b) d", b=2)
        ps_oh = ps_xo[:, 1, 0:NH * (HD + 1)].rearrange("p (h e) -> p h e", h=NH)

        s_w = ctx.enter_context(nc.semaphore("b_weights"))
        s_const = ctx.enter_context(nc.semaphore("b_const"))
        x_in = S("b_x_in", 16)
        v_steps = S("b_v_steps", TT)
        ticks = S("b_ticks", 1)
        mv_ready = S("b_mv", TT)
        g_steps = S("b_g_steps", 1)
        rstd_ready = S("b_rstd", 1)
        xn_ready = S("b_xn", TT)
        xb_ready = S("b_xb", 1)
        xT_turned = S("b_xT_turned", DC)
        xT_ready = S("b_xT", DC)
        qk_proj = S("b_qk_proj", 4)
        q_ready = S("b_q", 8)
        k_ready = S("b_k", 2)
        v_proj = S("b_v_proj", TT)
        v_ready = S("b_v", TT)
        scores = S("b_scores", UNITS)
        max_ready = S("b_max", UNITS)
        exp_half = S("b_exp_half", UNITS - NH)
        exp_ready = S("b_exp", UNITS)
        p_turned = S("b_p_turned", UNITS)
        pt_ready = S("b_pt_ready", UNITS)
        pv_done = S("b_pv", UNITS)
        inv_ready = S("b_inv_ready", TT)
        o_ready = S("b_o_ready", TT)
        o_turned = S("b_o_turned", DC)
        oT_ready = S("b_oT_ready", DC)
        out_done = S("b_out", 1)
        res_ready = S("b_res_ready", 1)
        xn_stored = S("b_xn_stored", 16)
        stored = S("b_stored", 16)
        seed(nc, sems)
        block = ctx.enter_context(nc.Block())

        def nk(u):
            return len(KEYS[UNIT[u][0]])

        def batches(eng, first, body):
            first(0)
            if NB > 1:
                with eng.Fori(0, NB - 1) as b:
                    body(b, b + 1)
            body(NB - 1, None)

        @block.sync
        def _(sp):
            for dst, src in ((w_qkv[:, :, :], io["L1_w_qkvT"].rearrange("(c p) n -> p c n", p=P)),
                             (w_o[:, :, :], io["L1_w_outT"].rearrange("(c p) n -> p c n", p=P)),
                             (qk_bias[:, :], io["qk_bias_cols"]),
                             (head_mask[:, :], io["head_mask"]),
                             (v_bias[:, :], io["L1_attn_b_qkv"][2 * D:3 * D].unsqueeze(0).broadcast_to([P, D])),
                             (o_bias[:, :], io["L1_attn_b_out"].unsqueeze(0).broadcast_to([P, D]))):
                sp.dma_start(dst, src).then_inc(s_w, 16)
            tiles = lambda ap: ap.rearrange("(t p) d -> p t d", p=P)

            def first(n):
                sp.dma_start(x_sb[:, :, :], tiles(x1_dram[n])).then_inc(x_in.s, 16)
                sp.wait_ge(xn_ready.s, xn_ready.at(n, TT))
                sp.dma_start(tiles(xn_dram[n]), xn[:, :, :]).then_inc(xn_stored.s, 16)

            def body(b, n):
                if n is not None:
                    sp.wait_ge(xb_ready.s, xb_ready.at(b, 1))
                    first(n)
                sp.wait_ge(res_ready.s, res_ready.at(b, 1))
                sp.dma_start(tiles(base_dram[b]), res[:, :, :]).then_inc(stored.s, 16)

            batches(sp, first, body)
            sp.wait_ge(xn_stored.s, xn_stored.at(NB, 0))
            sp.wait_ge(stored.s, stored.at(NB, 0))

        @block.gpsimd
        def _(pool):
            pool.memset(mhalf[:, :], -0.5).then_inc(s_const, 1)
            pool.memset(eps[:, :], LN_EPS).then_inc(s_const, 1)
            pool.memset(v[:, :, :, HD:HD + 1], 1.0).then_inc(s_const, 1)
            pool.wait_ge(s_const, 3)
            pool.wait_ge(s_w, 16 * 6)

            def first(n):
                pool.wait_ge(mv_ready.s, mv_ready.at(n, TT))
                pool.tensor_tensor(veps[:, :], mv[:, :, 1], eps[:, :], ALU.add).then_inc(g_steps.s, 1)
                pool.wait_ge(g_steps.s, g_steps.at(n, 1))
                pool.tensor_tensor(rstd[:, :], veps[:, :], mhalf[:, :], ALU.pow).then_inc(rstd_ready.s, 1)
                pool.wait_ge(res_ready.s, res_ready.at(n, 0))
                pool.tensor_tensor(xb[:, :, :], x_sb[:, :, :], bc(o_bias[:, :].unsqueeze(1), [P, TT, D]), ALU.add)\
                    .then_inc(xb_ready.s, 1)

            def body(b, n):
                if n is not None:
                    first(n)

            batches(pool, first, body)

        @block.vector
        def _(dve):
            st = Steps(v_steps, dve)
            dve.wait_ge(s_w, 16 * 6)
            dve.wait_ge(s_const, 3)

            def statistics(n):
                st.turn(n)
                dve.wait_ge(x_in.s, x_in.at(n, 16))
                for t in range(TT):
                    st.done(dve.bn_stats(stats[:, t, :], x_sb[:, t, :]))
                dve.wait_ge(st.s, st.at(TT))
                dve.memset(tick[:, :], 0.0).then_inc(ticks.s, 1)
                for t in range(TT):
                    dve.bn_aggr(mv[:, t, :], stats[:, t, :]).then_inc(mv_ready.s, 1)
                st.end()

            def norm(n):
                dve.wait_ge(rstd_ready.s, rstd_ready.at(n, 1))
                dve.wait_ge(xn_stored.s, xn_stored.at(n, 0))
                for t in range(TT):
                    dve.tensor_scalar(xn[:, t, :], x_sb[:, t, :], mv[:, t, 0:1], rstd[:, t:t + 1],
                                      ALU.subtract, ALU.mult).then_inc(xn_ready.s, 1)

            def take_projections(n):
                for m in range(DC):
                    dve.wait_ge(qk_proj.s, qk_proj.at(n, m + 1))
                    for j in range(4):
                        dve.tensor_scalar(qm[:, m, j, :], ps_s[:, m, :], qk_bias[:, m:m + 1], head_mask[:, j:j + 1],
                                          ALU.add, ALU.mult).then_inc(q_ready.s, 1)
                for t in range(TT):
                    dve.wait_ge(v_proj.s, v_proj.at(n, 2 * (t // 2) + 2))
                    dve.tensor_tensor(v[:, t, :, 0:HD], ps_v[:, t, :].rearrange("p (h e) -> p h e", h=NH),
                                      v_bias[:, :].rearrange("p (h e) -> p h e", h=NH), ALU.add).then_inc(v_ready.s, 1)

            def normalise(b, t):
                dve.wait_ge(pv_done.s, pv_done.at(b, LAST[t] + 1))
                dve.reciprocal(inv[:, :], ps_oh[:, :, HD]).then_inc(inv_ready.s, 1)
                dve.wait_ge(inv_ready.s, inv_ready.at(b, t + 1))
                dve.tensor_tensor(o[:, t, :].rearrange("p (h e) -> p h e", h=NH), ps_oh[:, :, 0:HD],
                                  bc(inv[:, :].unsqueeze(2), [P, NH, HD]), ALU.mult).then_inc(o_ready.s, 1)

            def first(n):
                statistics(n)
                norm(n)
                take_projections(n)

            def body(b, n):
                for s in range(UNITS + TURN_LAG):
                    if s < UNITS:
                        dve.wait_ge(scores.s, scores.at(b, s + 1))
                        heads = len(UNIT[s][1])
                        dve.tensor_reduce(negmax[:, s, 0:heads],
                                          ps_s[:, s % 4, :].rearrange("p (h n) -> p h n", h=heads), AX.X, ALU.max,
                                          negate=True).then_inc(max_ready.s, 1)
                    if s >= TURN_LAG:
                        r = s - TURN_LAG
                        dve.wait_ge(p_turned.s, p_turned.at(b, r + 1))
                        if r >= 3:
                            dve.wait_ge(pv_done.s, pv_done.at(b, r - 2))
                        dve.tensor_copy(pt[:, r % 3, :], ps_t[:, r % 2, :]).then_inc(pt_ready.s, 1)
                    for t in range(TT - 1):
                        if s == LAST[t] + PV_LAG:
                            normalise(b, t)
                    if n is not None and s == STATS_AT:
                        statistics(n)
                    if n is not None and s == NORM_AT:
                        norm(n)
                normalise(b, TT - 1)
                if n is not None:
                    take_projections(n)
                dve.wait_ge(out_done.s, out_done.at(b, 1))
                dve.wait_ge(xb_ready.s, xb_ready.at(b, 1))
                dve.wait_ge(stored.s, stored.at(b, 0))
                dve.tensor_tensor(res[:, :, :], ps_y, xb[:, :, :], ALU.add).then_inc(res_ready.s, 1)

            batches(dve, first, body)

        @block.scalar
        def _(act):
            act.wait_ge(s_w, 16 * 6)

            def take_x(n, k):
                act.wait_ge(xT_turned.s, xT_turned.at(n, k + 1))
                act.activation(xT[:, k, :], ps_xo[:, 0, :], ACT.Copy).then_inc(xT_ready.s, 1)

            def take_k(n):
                for m in range(DC):
                    act.wait_ge(qk_proj.s, qk_proj.at(n, 2 + m + 1))
                    act.activation(kf[:, m, :], ps_s[:, 2 + m, :], ACT.Identity, bias=qk_bias[:, 2 + m:3 + m])\
                        .then_inc(k_ready.s, 1)

            def first(n):
                for k in range(DC):
                    take_x(n, k)
                take_k(n)

            def body(b, n):
                for u in range(UNITS):
                    act.wait_ge(max_ready.s, max_ready.at(b, u + 1))
                    if u >= 4:
                        act.wait_ge(p_turned.s, p_turned.at(b, u - 3))
                    heads = len(UNIT[u][1])
                    for i in range(heads):
                        cols = slice(i * 512 // heads, (i + 1) * 512 // heads)
                        act.activation(pr[:, u % 4, cols], ps_s[:, u % 4, cols], ACT.Exp, bias=negmax[:, u, i:i + 1])\
                            .then_inc((exp_ready if i == heads - 1 else exp_half).s, 1)
                    if n is not None and u in TURN_AT:
                        take_x(n, TURN_AT.index(u))
                if n is not None:
                    take_k(n)
                for k in range(DC):
                    act.wait_ge(o_turned.s, o_turned.at(b, k + 1))
                    act.activation(oT[:, k, :], ps_xo[:, k, :], ACT.Copy).then_inc(oT_ready.s, 1)

            batches(act, first, body)

        @block.tensor
        def _(pe):
            pe.wait_ge(s_w, 16 * 6)
            pe.wait_ge(s_const, 3)

            def turn(dst, src, k):
                for t in range(TT):
                    last = pe.transpose(dst[:, t * P:(t + 1) * P], src[:, t, k * P:(k + 1) * P], W["ident"][:, :])
                return last

            def turn_x(n, k):
                pe.wait_ge(xn_ready.s, xn_ready.at(n, TT))
                if k:
                    pe.wait_ge(xT_ready.s, xT_ready.at(n, k))
                turn(ps_xo[:, 0, :], xn, k).then_inc(xT_turned.s, 1)

            def project(n):
                pe.wait_ge(xT_ready.s, xT_ready.at(n, DC))
                for m in range(4):
                    for k in range(DC):
                        last = pe.matmul(ps_s[:, m, :], w_qkv[:, k, m * P:(m + 1) * P], xT[:, k, :],
                                         start=(k == 0), stop=(k == DC - 1))
                    last.then_inc(qk_proj.s, 1)
                pe.wait_ge(pt_ready.s, pt_ready.at(n, 0))
                for t in range(TT):
                    for k in range(DC):
                        last = pe.matmul(ps_v[:, t, :], xT[:, k, t * P:(t + 1) * P], w_qkv[:, k, 2 * D:3 * D],
                                         start=(k == 0), stop=(k == DC - 1))
                    last.then_inc(v_proj.s, 1)

            def first(n):
                for k in range(DC):
                    turn_x(n, k)
                project(n)

            def body(b, n):
                pe.wait_ge(q_ready.s, q_ready.at(b, 8))
                pe.wait_ge(k_ready.s, k_ready.at(b, 2))
                for s in range(UNITS + PV_LAG):
                    if s < UNITS:
                        qt, heads = UNIT[s]
                        if s >= 4:
                            pe.wait_ge(exp_ready.s, exp_ready.at(b, s - 3))
                        for i, h in enumerate(heads):
                            m, half, j = h // 8, h % 8 // 4, h % 4
                            rows = slice(64 * half, 64 * half + 64)
                            runs = [(0, 0, 512)] if qt == 0 else [(0, 0, 256)] if qt == 1 else \
                                [(0, 0, P), (P, qt * P, P)]
                            for at, key, w in runs:
                                at += i * 256
                                last = pe.matmul(ps_s[:, s % 4, at:at + w], qm[rows, m, j, qt * P:(qt + 1) * P],
                                                 kf[rows, m, key:key + w], start=True, stop=True)
                        last.then_inc(scores.s, 1)
                    if TURN_LAG <= s < UNITS + TURN_LAG:
                        r = s - TURN_LAG
                        pe.wait_ge(exp_ready.s, exp_ready.at(b, r + 1))
                        if r >= 2:
                            pe.wait_ge(pt_ready.s, pt_ready.at(b, r - 1))
                        else:
                            pe.wait_ge(v_ready.s, v_ready.at(b, TT))
                        for n_ in range(4):
                            last = pe.transpose(ps_t[:, r % 2, n_ * P:(n_ + 1) * P], pr[:, r % 4, n_ * P:(n_ + 1) * P],
                                                W["ident"][:, :])
                        last.then_inc(p_turned.s, 1)
                    if s >= PV_LAG:
                        r = s - PV_LAG
                        qt, heads = UNIT[r]
                        pe.wait_ge(pt_ready.s, pt_ready.at(b, r + 1))
                        if r == 0:
                            pe.wait_ge(res_ready.s, res_ready.at(b, 0))
                        elif r - 1 in LAST:
                            pe.wait_ge(o_ready.s, o_ready.at(b, qt))
                        for i, h in enumerate(heads):
                            for k, key in enumerate(KEYS[qt]):
                                at = (i * nk(r) + k) * P
                                last = pe.matmul(ps_oh[:, h, :], pt[:, r % 3, at:at + P], v[:, key, h, :],
                                                 start=(k == 0), stop=(k == nk(r) - 1))
                        last.then_inc(pv_done.s, 1)
                    if n is not None and s in TURN_AT:
                        turn_x(n, TURN_AT.index(s))
                if n is not None:
                    project(n)
                pe.wait_ge(o_ready.s, o_ready.at(b, TT))
                for k in range(DC):
                    turn(ps_xo[:, k, :], o, k).then_inc(o_turned.s, 1)
                pe.wait_ge(oT_ready.s, oT_ready.at(b, DC))
                for t in range(TT):
                    for k in range(DC):
                        last = pe.matmul(ps_y[:, t, :], oT[:, k, t * P:(t + 1) * P], w_o[:, k, :],
                                         start=(k == 0), stop=(k == DC - 1))
                last.then_inc(out_done.s, 1)

            batches(pe, first, body)


def local_attention_layers(nc, io, W, stream, NB):
    L, T, D, NH, HD, HID = 2, 512, 256, 8, 64, 682
    TT, DC, IC = T // P, D // P, NH * HD // P
    INNER = NH * HD
    JC = 6
    UNIT = [(0, [p, p + 2, p + 4, p + 6]) for p in range(2)] + \
        [(qt, [g + p, g + p + 2]) for qt in range(1, TT) for g in (0, 4) for p in range(2)]
    UNITS = len(UNIT)
    LAST = [max(u for u in range(UNITS) if UNIT[u][0] == qt and any(h // 4 == g for h in UNIT[u][1]))
            for qt in range(TT) for g in range(2)]
    HPB = 4
    TURN_LAG, PV_LAG = 3, 5
    E1 = HD + 1

    with ExitStack() as ctx:
        sb = lambda n, s, d=F32: ctx.enter_context(nc.sbuf_tensor(n, s, d))
        sems = []

        def S(name, per):
            sems.append(Sem(ctx, nc, name, per))
            return sems[-1]

        w_qkv = sb("c_w_qkv", [P, DC, 3 * INNER])
        w_o = sb("c_w_o", [P, IC, D])
        w_1 = sb("c_w_1", [P, DC, 2 * HID])
        w_2 = sb("c_w_2", [P, JC, D])
        ln_cols = sb("c_ln_cols", [P, DC, 2])
        b1_cols = sb("c_b1_cols", [P, 2, JC])
        b2_row = sb("c_b2_row", [P, D])
        qk_scale = sb("c_qk_scale", [P, 2, HD])
        rot_c0 = sb("c_rot_c0", [P, TT, 2, HD])
        rot_s0 = sb("c_rot_s0", [P, TT, 2, HD])
        rot_c = sb("c_rot_c", [P, TT, 2, HD])
        rot_s = sb("c_rot_s", [P, TT, 2, HD])
        mask32 = sb("c_mask32", [P, 2 * P])
        mask = sb("c_mask", [P, 2 * P], BF16)
        identb = sb("c_identb", [P, P], BF16)
        mhalf = sb("c_mhalf", [P, 2 * NH])
        eps = sb("c_eps", [P, TT])
        tick = sb("c_tick", [P, 1])

        x_sb = sb("c_x", [P, TT, D])
        xr = sb("c_xr", [P, TT, D])
        xT = sb("c_xT", [P, DC, T + 1])
        sq = sb("c_sq", [P, 2, INNER])
        ss = sb("c_ss", [P, 2, NH])
        ssc = sb("c_ssc", [P, 2, NH])
        rn = sb("c_rn", [P, 2, NH])
        qn = sb("c_qn", [P, 2, 2, INNER])
        q_cos = sb("c_q_cos", [P, 2, INNER])
        q_sin = sb("c_q_sin", [P, 2, 2, INNER])
        qr = sb("c_qr", [P, TT, 2, INNER])
        v = sb("c_v", [P, TT, NH, E1])
        qT = sb("c_qT", [P, IC, T])
        kT = sb("c_kT", [P, IC, T])
        negmax = sb("c_negmax", [P, UNITS, 4])
        pr = sb("c_pr", [P, 4, 512])
        pt = sb("c_pt", [P, 3, 512])
        inv = sb("c_inv", [P, 2, HPB])
        o = sb("c_o", [P, TT, INNER])
        oT = sb("c_oT", [P, IC, T])
        xa = sb("c_xa", [P, TT, D])
        xsh = sb("c_xsh", [P, TT, P])
        xa2 = sb("c_xa2", [P, TT, D])
        stats = sb("c_stats", [P, TT, 12])
        mv = sb("c_mv", [P, TT, 2])
        rstd = sb("c_rstd", [P, TT])
        veps = sb("c_veps", [P, TT])
        hn = sb("c_hn", [P, TT, D])
        hT = sb("c_hT", [P, DC, T])
        gl = sb("c_gl", [P, 2, T])
        hid = sb("c_hid", [P, JC, T])
        xo = sb("c_xo", [P, TT, D])

        ps_s = ctx.enter_context(nc.psum_tensor("c_ps_s", [P, 4, 512], F32))
        ps_t = ctx.enter_context(nc.psum_tensor("c_ps_t", [P, 2, 512], F32))
        ps_o = ctx.enter_context(nc.psum_tensor("c_ps_o", [P, 2, 512], F32))
        ps_x = ps_t[:, :, :].rearrange("p a (b d) -> p (a b) d", b=2)
        ps_y = ps_o[:, :, :].rearrange("p a (b d) -> p (a b) d", b=2)

        s_c = ctx.enter_context(nc.semaphore("c_const"))
        s_t = ctx.enter_context(nc.semaphore("c_tables"))
        w_in = S("c_w_in", 16 * 10)
        rot_ready = S("c_rot_ready", 3)
        x_in = S("c_x_in", 16)
        xr_in = S("c_xr_in", 16)
        x_turned = S("c_x_turned", DC)
        xT_ready = S("c_xT_ready", DC)
        q_proj = S("c_q_proj", TT)
        v_proj = S("c_v_proj", TT)
        sq_half = S("c_sq_half", TT)
        sq_ready = S("c_sq_ready", TT)
        v_ready = S("c_v_ready", TT)
        ss_raw = S("c_ss_raw", TT)
        ss_ready = S("c_ss", TT)
        rn_ready = S("c_rn", TT)
        qn_half = S("c_qn_half", TT)
        qn_ready = S("c_qn", TT)
        cos_half = S("c_cos_half", TT)
        cos_ready = S("c_cos", TT)
        sin_part = S("c_sin_part", 3 * TT)
        sin_ready = S("c_sin", TT)
        qr_ready = S("c_qr_ready", TT)
        q_turned = S("c_q_turned", TT)
        k_turned = S("c_k_turned", TT)
        qT_ready = S("c_qT_ready", TT)
        kT_ready = S("c_kT_ready", TT)
        scores = S("c_scores", UNITS)
        max_ready = S("c_max", UNITS)
        exp_part = S("c_exp_part", TT * NH - UNITS)
        exp_ready = S("c_exp", UNITS)
        p_turned = S("c_p_turned", UNITS)
        pt_ready = S("c_pt_ready", UNITS)
        pv_done = S("c_pv", UNITS)
        inv_ready = S("c_inv_ready", 2 * TT)
        o_ready = S("c_o_ready", 2 * TT)
        o_turned = S("c_o_turned", IC)
        oT_ready = S("c_oT_ready", IC)
        wo_done = S("c_wo_done", 1)
        xa_ready = S("c_xa", 1)
        shifted = S("c_shifted", 32)
        v_steps = S("c_v_steps", 2 * TT)
        ticks = S("c_ticks", 1)
        mv_ready = S("c_mv", TT)
        g_steps = S("c_g_steps", 1)
        rstd_ready = S("c_rstd_ready", 1)
        xa2_ready = S("c_xa2", 1)
        hn_ready = S("c_hn", 2 * TT)
        h_turned = S("c_h_turned", DC)
        hT_ready = S("c_hT_ready", DC)
        ag_proj = S("c_ag_proj", JC)
        gl_ready = S("c_gl", JC)
        hid_ready = S("c_hid", JC)
        y_done = S("c_y_done", 1)
        xo_ready = S("c_xo", 1)
        stored = S("c_stored", 16)
        seed(nc, sems)
        block = ctx.enter_context(nc.Block())

        def jj(j):
            return min(P, HID - j * P)

        def nk(u):
            return 1 if UNIT[u][0] == 0 else 2

        def pair(i):
            return 2 - 2 * (i % 2)

        def layers(eng, layer, first, body):
            with eng.Fori(0, L) as l:
                if layer:
                    layer(l)
                first(l, 0, l * NB)
                if NB > 1:
                    with eng.Fori(0, NB - 1) as b:
                        body(l, b, l * NB + b, True)
                body(l, NB - 1, l * NB + NB - 1, False)

        def halves(ap):
            return ap.rearrange("p (h d) -> p h d", h=NH)

        @block.sync
        def _(sp):
            for dst, src in ((rot_c0[:, :, :, :], io["rot_cos"].rearrange("(t p) a d -> p t a d", p=P)),
                             (rot_s0[:, :, :, :], io["rot_sin"].rearrange("(t p) a d -> p t a d", p=P)),
                             (mask32[:, :], io["window_mask"])):
                sp.dma_start(dst, src).then_inc(s_t, 16)

            def layer(l):
                sp.wait_ge(xo_ready.s, xo_ready.at(l * NB, 0))
                for dst, src in ((w_qkv[:, :, :], io["L1_ffn_wqkv"][l].rearrange("(c p) n -> p c n", p=P)),
                                 (w_o[:, :, :], io["L1_ffn_wo"][l].rearrange("(c p) n -> p c n", p=P)),
                                 (w_1[:, :, :], io["L1_ffn_w1"][l].rearrange("(c p) n -> p c n", p=P)),
                                 (w_2[:, 0:JC - 1, :], io["L1_ffn_w2"][l, 0:(JC - 1) * P, :].rearrange("(c p) n -> p c n", p=P)),
                                 (w_2[0:jj(JC - 1), JC - 1, :], io["L1_ffn_w2"][l, (JC - 1) * P:, :]),
                                 (ln_cols[:, :, :], io["ln_cols"][l]),
                                 (b1_cols[:, :, :], io["b1_cols"][l]),
                                 (b2_row[:, :], io["L1_ffn_b2"][l].unsqueeze(0).broadcast_to([P, D])),
                                 (qk_scale[:, 0, :], io["L1_ffn_q_scale"][l].unsqueeze(0).broadcast_to([P, HD])),
                                 (qk_scale[:, 1, :], io["L1_ffn_k_scale"][l].unsqueeze(0).broadcast_to([P, HD]))):
                    sp.dma_start(dst, src).then_inc(w_in.s, 16)

            tiles = lambda ap: ap.rearrange("(t p) d -> p t d", p=P)

            def first(l, b, it):
                sp.wait_ge(stored.s, stored.at(it, 0))
                sp.dma_start(x_sb[:, :, :], tiles(stream[l, b])).then_inc(x_in.s, 16)

            def body(l, b, it, more):
                sp.wait_ge(xa_ready.s, xa_ready.at(it, 0))
                sp.dma_start(xr[:, :, :], tiles(stream[l, b])).then_inc(xr_in.s, 16)
                if more:
                    sp.wait_ge(x_turned.s, x_turned.at(it, DC))
                    sp.dma_start(x_sb[:, :, :], tiles(stream[l, b + 1])).then_inc(x_in.s, 16)
                sp.wait_ge(xa_ready.s, xa_ready.at(it, 1))
                sp.dma_start(xsh[1:P, :, :], xa[0:P - 1, :, P:D]).then_inc(shifted.s, 16)
                sp.dma_start(xsh[0:1, 1:TT, :], xa[P - 1:P, 0:TT - 1, P:D]).then_inc(shifted.s, 16)
                sp.wait_ge(xo_ready.s, xo_ready.at(it, 1))
                sp.dma_start(tiles(stream[l + 1, b]), xo[:, :, :]).then_inc(stored.s, 16)

            layers(sp, layer, first, body)
            sp.wait_ge(stored.s, stored.at(L * NB, 0))

        @block.gpsimd
        def _(pool):
            pool.memset(mhalf[:, :], -0.5).then_inc(s_c, 1)
            pool.memset(eps[:, :], LN_EPS).then_inc(s_c, 1)
            pool.memset(v[:, :, :, HD:E1], 1.0).then_inc(s_c, 1)
            pool.memset(xT[:, 1, 0:1], 0.0).then_inc(s_c, 1)
            pool.memset(xsh[0:1, 0, :], 0.0).then_inc(s_c, 1)
            pool.tensor_copy(identb[:, :], W["ident"][:, :]).then_inc(s_c, 1)
            pool.wait_ge(s_t, 48)
            pool.tensor_copy(mask[:, :], mask32[:, :]).then_inc(s_c, 1)
            pool.wait_ge(s_c, 7)

            def rotate(l, n, t):
                pool.wait_ge(ss_ready.s, ss_ready.at(n, t + 1))
                pool.wait_ge(qn_ready.s, qn_ready.at(n, t))
                pool.tensor_tensor(rn[:, :, :].rearrange("p a h -> p (a h)"), ssc[:, :, :].rearrange("p a h -> p (a h)"),
                                   mhalf[:, :], ALU.pow).then_inc(rn_ready.s, 1)
                pool.wait_ge(qn_ready.s, qn_ready.at(n, t + 1))
                if t == 0:
                    pool.wait_ge(w_in.s, w_in.at(l + 1, 0))
                    pool.wait_ge(rot_ready.s, rot_ready.at(l + 1, 0))
                for a in range(2):
                    pool.tensor_tensor(halves(q_cos[:, a, :]), halves(qn[:, t % 2, a, :]),
                                       bc(rot_c[:, t, a, :].unsqueeze(1), [P, NH, HD]), ALU.mult)\
                        .then_inc((cos_ready if a else cos_half).s, 1)
                pool.wait_ge(sin_ready.s, sin_ready.at(n, t + 1))
                pool.wait_ge(cos_ready.s, cos_ready.at(n, t + 1))
                pool.wait_ge(k_turned.s, k_turned.at(n, 0))
                pool.tensor_tensor(qr[:, t, :, :], q_cos[:, :, :], q_sin[:, t % 2, :, :], ALU.add)\
                    .then_inc(qr_ready.s, 1)

            def residual(it):
                pool.wait_ge(xa_ready.s, xa_ready.at(it, 1))
                pool.wait_ge(xo_ready.s, xo_ready.at(it, 0))
                pool.tensor_tensor(xa2[:, :, :], xa[:, :, :], bc(b2_row[:, :].unsqueeze(1), [P, TT, D]), ALU.add)\
                    .then_inc(xa2_ready.s, 1)

            def root(it):
                pool.wait_ge(mv_ready.s, mv_ready.at(it, TT))
                pool.tensor_tensor(veps[:, :], mv[:, :, 1], eps[:, :], ALU.add).then_inc(g_steps.s, 1)
                pool.wait_ge(g_steps.s, g_steps.at(it, 1))
                pool.tensor_tensor(rstd[:, :], veps[:, :], mhalf[:, 0:TT], ALU.pow).then_inc(rstd_ready.s, 1)

            def first(l, b, it):
                for t in range(TT):
                    rotate(l, it, t)

            def body(l, b, it, more):
                if more:
                    rotate(l, it + 1, 0)
                root(it)
                if more:
                    rotate(l, it + 1, 1)
                    rotate(l, it + 1, 2)
                residual(it)
                if more:
                    rotate(l, it + 1, 3)

            layers(pool, None, first, body)

        @block.vector
        def _(dve):
            dve.wait_ge(s_c, 7)
            dve.wait_ge(s_t, 48)
            st = Steps(v_steps, dve)
            H2 = HD // 2

            def layer(l):
                dve.wait_ge(w_in.s, w_in.at(l + 1, 0))
                dve.wait_ge(xo_ready.s, xo_ready.at(l * NB, 0))
                every = lambda ap: bc(ap.unsqueeze(1), [P, TT, 2, ap.shape[2]])
                dve.tensor_tensor(rot_c[:, :, :, :], rot_c0[:, :, :, :], every(qk_scale[:, :, :]), ALU.mult)\
                    .then_inc(rot_ready.s, 1)
                dve.tensor_tensor(rot_s[:, :, :, 0:H2], rot_s0[:, :, :, 0:H2], every(qk_scale[:, :, H2:HD]), ALU.mult)\
                    .then_inc(rot_ready.s, 1)
                dve.tensor_tensor(rot_s[:, :, :, H2:HD], rot_s0[:, :, :, H2:HD], every(qk_scale[:, :, 0:H2]), ALU.mult)\
                    .then_inc(rot_ready.s, 1)

            def squares(n, t):
                dve.wait_ge(sq_ready.s, sq_ready.at(n, t + 1))
                dve.wait_ge(rn_ready.s, rn_ready.at(n, t))
                dve.tensor_reduce(ss[:, :, :], sq[:, :, :].rearrange("p a (h d) -> p a h d", h=NH), AX.X, ALU.add)\
                    .then_inc(ss_raw.s, 1)
                dve.wait_ge(ss_raw.s, ss_raw.at(n, t + 1))
                dve.tensor_scalar(ssc[:, :, :], ss[:, :, :], 1e-24, None, ALU.max).then_inc(ss_ready.s, 1)

            def norm_heads(l, n, t):
                dve.wait_ge(rn_ready.s, rn_ready.at(n, t + 1))
                if t >= 2:
                    dve.wait_ge(cos_ready.s, cos_ready.at(n, t - 1))
                    dve.wait_ge(qr_ready.s, qr_ready.at(n, t - 1))
                for a in range(2):
                    dve.tensor_tensor(halves(qn[:, t % 2, a, :]), halves(ps_s[:, pair(t) + a, :]),
                                      bc(rn[:, a, :].unsqueeze(2), [P, NH, HD]), ALU.mult)\
                        .then_inc((qn_ready if a else qn_half).s, 1)
                dve.wait_ge(qn_half.s, qn_half.at(n, t + 1))
                dve.wait_ge(qn_ready.s, qn_ready.at(n, t + 1))
                if t == 0:
                    dve.wait_ge(rot_ready.s, rot_ready.at(l + 1, 0))
                for i in range(2):
                    for a in range(2):
                        to, of = slice(i * H2, i * H2 + H2), slice(H2 - i * H2, HD - i * H2)
                        dve.tensor_tensor(halves(q_sin[:, t % 2, a, :])[:, :, to], halves(qn[:, t % 2, a, :])[:, :, of],
                                          bc(rot_s[:, t, a, to].unsqueeze(1), [P, NH, H2]), ALU.mult)\
                            .then_inc((sin_ready if i and a else sin_part).s, 1)

            def take_k(n, t):
                dve.wait_ge(k_turned.s, k_turned.at(n, t + 1))
                dve.tensor_copy(kT[:, :, t * P:(t + 1) * P], ps_t[:, 1, :].rearrange("p (c n) -> p c n", c=IC))\
                    .then_inc(kT_ready.s, 1)

            def normalise(it, i):
                qt, g = divmod(i, 2)
                ps = ps_o[:, g, 0:HPB * E1].rearrange("p (h e) -> p h e", h=HPB)
                dve.wait_ge(pv_done.s, pv_done.at(it, LAST[i] + 1))
                dve.reciprocal(inv[:, g, :], ps[:, :, HD]).then_inc(inv_ready.s, 1)
                dve.wait_ge(inv_ready.s, inv_ready.at(it, i + 1))
                dve.tensor_tensor(o[:, qt, g * HPB * HD:(g + 1) * HPB * HD].rearrange("p (h e) -> p h e", h=HPB),
                                  ps[:, :, 0:HD], bc(inv[:, g, :].unsqueeze(2), [P, HPB, HD]), ALU.mult)\
                    .then_inc(o_ready.s, 1)

            def first(l, b, it):
                for t in range(TT):
                    squares(it, t)
                    norm_heads(l, it, t)
                    if t:
                        take_k(it, t - 1)
                take_k(it, TT - 1)

            def body(l, b, it, more):
                n = it + 1
                for s in range(UNITS + PV_LAG + 1):
                    if s < UNITS:
                        heads = len(UNIT[s][1])
                        dve.wait_ge(scores.s, scores.at(it, s + 1))
                        dve.tensor_reduce(negmax[:, s, 0:heads], ps_s[:, s % 4, :].rearrange("p (h n) -> p h n", h=heads),
                                          AX.X, ALU.max, negate=True).then_inc(max_ready.s, 1)
                    if TURN_LAG <= s < UNITS + TURN_LAG:
                        r = s - TURN_LAG
                        dve.wait_ge(p_turned.s, p_turned.at(it, r + 1))
                        if r >= 3:
                            dve.wait_ge(pv_done.s, pv_done.at(it, r - 2))
                        dve.tensor_copy(pt[:, r % 3, :], ps_t[:, r % 2, :]).then_inc(pt_ready.s, 1)
                    for i in range(2 * TT):
                        if s == LAST[i] + PV_LAG + 1:
                            normalise(it, i)
                if more:
                    squares(n, 0)
                dve.wait_ge(wo_done.s, wo_done.at(it, 1))
                dve.wait_ge(xr_in.s, xr_in.at(it, 16))
                dve.wait_ge(xa2_ready.s, xa2_ready.at(it, 0))
                dve.wait_ge(hn_ready.s, hn_ready.at(it, 0))
                dve.tensor_tensor(xa[:, :, :], ps_x, xr[:, :, :], ALU.add).then_inc(xa_ready.s, 1)
                if more:
                    norm_heads(l, n, 0)
                st.turn(it)
                dve.wait_ge(xa_ready.s, xa_ready.at(it, 1))
                for t in range(TT):
                    st.done(dve.bn_stats(stats[:, t, 0:6], xa[:, t, 0:P]))
                dve.wait_ge(shifted.s, shifted.at(it, 32))
                for t in range(TT):
                    st.done(dve.bn_stats(stats[:, t, 6:12], xsh[:, t, :]))
                dve.wait_ge(st.s, st.at(2 * TT))
                dve.memset(tick[:, :], 0.0).then_inc(ticks.s, 1)
                for t in range(TT):
                    dve.bn_aggr(mv[:, t, :], stats[:, t, :]).then_inc(mv_ready.s, 1)
                if more:
                    squares(n, 1)
                dve.wait_ge(rstd_ready.s, rstd_ready.at(it, 1))
                for t in range(TT):
                    for half, src in enumerate((xa[:, t, 0:P], xsh[:, t, :])):
                        dve.tensor_scalar(hn[:, t, half * P:(half + 1) * P], src, mv[:, t, 0:1], rstd[:, t:t + 1],
                                          ALU.subtract, ALU.mult).then_inc(hn_ready.s, 1)
                if more:
                    norm_heads(l, n, 1)
                    for t in range(2, TT):
                        squares(n, t)
                        norm_heads(l, n, t)
                for j in range(JC):
                    m = jj(j)
                    dve.wait_ge(gl_ready.s, gl_ready.at(it, j + 1))
                    dve.scalar_tensor_tensor(hid[0:m, j, :], ps_s[0:m, pair(j), :], b1_cols[0:m, 0, j:j + 1],
                                             gl[0:m, j % 2, :], ALU.add, ALU.mult).then_inc(hid_ready.s, 1)
                    if more and j >= JC - TT:
                        take_k(n, j - JC + TT)
                dve.wait_ge(y_done.s, y_done.at(it, 1))
                dve.wait_ge(xa2_ready.s, xa2_ready.at(it, 1))
                dve.wait_ge(stored.s, stored.at(it, 0))
                dve.tensor_tensor(xo[:, :, :], ps_y, xa2[:, :, :], ALU.add).then_inc(xo_ready.s, 1)
                st.end()

            layers(dve, layer, first, body)

        @block.scalar
        def _(act):
            act.wait_ge(s_c, 7)

            def take_x(l, n):
                act.wait_ge(w_in.s, w_in.at(l + 1, 0))
                for k in range(DC):
                    act.wait_ge(x_turned.s, x_turned.at(n, k + 1))
                    act.activation(xT[:, k, k:k + T], ps_s[:, k, :], ACT.Copy).then_inc(xT_ready.s, 1)

            def square(n, t):
                act.wait_ge(q_proj.s, q_proj.at(n, t + 1))
                act.wait_ge(ss_raw.s, ss_raw.at(n, t))
                for a in range(2):
                    act.activation(sq[:, a, :], ps_s[:, pair(t) + a, :], ACT.Square)\
                        .then_inc((sq_ready if a else sq_half).s, 1)
                act.wait_ge(v_proj.s, v_proj.at(n, t + 1))
                act.activation(v[:, t, :, 0:HD], halves(ps_o[:, t % 2, :]), ACT.Copy).then_inc(v_ready.s, 1)

            def take_q(n, t):
                act.wait_ge(q_turned.s, q_turned.at(n, t + 1))
                act.activation(qT[:, :, t * P:(t + 1) * P], ps_t[:, 0, :].rearrange("p (c n) -> p c n", c=IC), ACT.Copy)\
                    .then_inc(qT_ready.s, 1)

            def first(l, b, it):
                take_x(l, it)
                for t in range(TT):
                    square(it, t)
                    if t:
                        take_q(it, t - 1)
                take_q(it, TT - 1)

            def body(l, b, it, more):
                n = it + 1
                for u in range(UNITS):
                    act.wait_ge(max_ready.s, max_ready.at(it, u + 1))
                    if u >= 4:
                        act.wait_ge(p_turned.s, p_turned.at(it, u - 3))
                    heads = len(UNIT[u][1])
                    for i in range(heads):
                        cols = slice(i * 512 // heads, (i + 1) * 512 // heads)
                        act.activation(pr[:, u % 4, cols], ps_s[:, u % 4, cols], ACT.Exp, bias=negmax[:, u, i:i + 1])\
                            .then_inc((exp_ready if i == heads - 1 else exp_part).s, 1)
                if more:
                    take_x(l, n)
                for c in range(IC):
                    act.wait_ge(o_turned.s, o_turned.at(it, c + 1))
                    act.activation(oT[:, c, :], ps_t[:, c % 2, :], ACT.Copy).then_inc(oT_ready.s, 1)
                if more:
                    for t in range(TT):
                        square(n, t)
                for k in range(DC):
                    act.wait_ge(h_turned.s, h_turned.at(it, k + 1))
                    act.activation(hT[:, k, :], ps_t[:, k, :], ACT.Identity, bias=ln_cols[:, k, 1:2],
                                   scale=ln_cols[:, k, 0:1]).then_inc(hT_ready.s, 1)
                for j in range(JC):
                    m = jj(j)
                    act.wait_ge(ag_proj.s, ag_proj.at(it, j + 1))
                    if j >= 2:
                        act.wait_ge(hid_ready.s, hid_ready.at(it, j - 1))
                    act.activation(gl[0:m, j % 2, :], ps_s[0:m, pair(j) + 1, :], ACT.Gelu, bias=b1_cols[0:m, 1, j:j + 1])\
                        .then_inc(gl_ready.s, 1)
                    if more and j >= JC - TT:
                        take_q(n, j - JC + TT)

            layers(act, None, first, body)

        @block.tensor
        def _(pe):
            pe.wait_ge(s_c, 7)

            def turn(dst, src, k):
                for t in range(TT):
                    last = pe.transpose(dst[:, t * P:(t + 1) * P], src[:, t, k * P:(k + 1) * P], W["ident"][:, :])
                return last

            def turn_x(n):
                pe.wait_ge(x_in.s, x_in.at(n, 16))
                for k in range(DC):
                    turn(ps_s[:, k, :], x_sb, k).then_inc(x_turned.s, 1)

            def project(n, t):
                if t >= 2:
                    pe.wait_ge(qn_ready.s, qn_ready.at(n, t - 1))
                    pe.wait_ge(v_ready.s, v_ready.at(n, t - 1))
                for a in range(3):
                    dst = ps_o[:, t % 2, :] if a == 2 else ps_s[:, pair(t) + a, :]
                    for k in range(DC):
                        last = pe.matmul(dst, xT[:, k, t * P:(t + 1) * P], w_qkv[:, k, a * INNER:(a + 1) * INNER],
                                         start=(k == 0), stop=(k == DC - 1))
                    if a:
                        last.then_inc((q_proj if a == 1 else v_proj).s, 1)

            def turn_qk(n, t):
                pe.wait_ge(qr_ready.s, qr_ready.at(n, t + 1))
                if t:
                    pe.wait_ge(qT_ready.s, qT_ready.at(n, t))
                    pe.wait_ge(kT_ready.s, kT_ready.at(n, t))
                for a in range(2):
                    for c in range(IC):
                        last = pe.transpose(ps_t[:, a, c * P:(c + 1) * P], qr[:, t, a, c * P:(c + 1) * P],
                                            W["ident"][:, :])
                    last.then_inc((k_turned if a else q_turned).s, 1)

            def first(l, b, it):
                pe.wait_ge(w_in.s, w_in.at(l + 1, 0))
                pe.wait_ge(xo_ready.s, xo_ready.at(it, 0))
                turn_x(it)
                pe.wait_ge(xT_ready.s, xT_ready.at(it, DC))
                for t in range(TT + 1):
                    if t < TT:
                        project(it, t)
                    if t:
                        turn_qk(it, t - 1)

            def body(l, b, it, more):
                n = it + 1
                pe.wait_ge(qT_ready.s, qT_ready.at(it, TT))
                pe.wait_ge(kT_ready.s, kT_ready.at(it, TT))
                for s in range(UNITS + PV_LAG):
                    if s < UNITS:
                        qt, heads = UNIT[s]
                        if s >= 4:
                            pe.wait_ge(exp_ready.s, exp_ready.at(it, s - 3))
                        w = P * nk(s)
                        for i, h in enumerate(heads):
                            rows = slice(64 * (h % 2), 64 * (h % 2) + 64)
                            dst = ps_s[:, s % 4, i * w:(i + 1) * w]
                            pe.matmul(dst, identb[:, :], mask[:, 2 * P - w:2 * P], start=True, stop=False)
                            last = pe.matmul(dst, qT[rows, h // 2, qt * P:(qt + 1) * P],
                                             kT[rows, h // 2, (qt + 1) * P - w:(qt + 1) * P], start=False, stop=True)
                        last.then_inc(scores.s, 1)
                    if TURN_LAG <= s < UNITS + TURN_LAG:
                        r = s - TURN_LAG
                        pe.wait_ge(exp_ready.s, exp_ready.at(it, r + 1))
                        if r >= 2:
                            pe.wait_ge(pt_ready.s, pt_ready.at(it, r - 1))
                        for i in range(4):
                            last = pe.transpose(ps_t[:, r % 2, i * P:(i + 1) * P], pr[:, r % 4, i * P:(i + 1) * P],
                                                W["ident"][:, :])
                        last.then_inc(p_turned.s, 1)
                    if s >= PV_LAG:
                        r = s - PV_LAG
                        qt, heads = UNIT[r]
                        pe.wait_ge(pt_ready.s, pt_ready.at(it, r + 1))
                        if r == 0:
                            pe.wait_ge(v_ready.s, v_ready.at(it, TT))
                            pe.wait_ge(xo_ready.s, xo_ready.at(it, 0))
                        elif qt:
                            pe.wait_ge(o_ready.s, o_ready.at(it, 2 * (qt - 1) + heads[0] // 4 + 1))
                        for i, h in enumerate(heads):
                            for k in range(nk(r)):
                                at = (i * nk(r) + k) * P
                                last = pe.matmul(ps_o[:, h // 4, h % 4 * E1:(h % 4 + 1) * E1], pt[:, r % 3, at:at + P],
                                                 v[:, qt - nk(r) + 1 + k, h, :], start=(k == 0), stop=(k == nk(r) - 1))
                        last.then_inc(pv_done.s, 1)
                if more:
                    turn_x(n)
                pe.wait_ge(o_ready.s, o_ready.at(it, 2 * TT))
                for c in range(IC):
                    pe.wait_ge(pt_ready.s, pt_ready.at(it, UNITS))
                    if c >= 2:
                        pe.wait_ge(oT_ready.s, oT_ready.at(it, c - 1))
                    turn(ps_t[:, c % 2, :], o, c).then_inc(o_turned.s, 1)
                if more:
                    pe.wait_ge(xT_ready.s, xT_ready.at(n, DC))
                    project(n, 0)
                pe.wait_ge(oT_ready.s, oT_ready.at(it, IC))
                for t in range(TT):
                    for c in range(IC):
                        last = pe.matmul(ps_x[:, t, :], oT[:, c, t * P:(t + 1) * P], w_o[:, c, :],
                                         start=(c == 0), stop=(c == IC - 1))
                last.then_inc(wo_done.s, 1)
                if more:
                    for t in range(1, TT):
                        project(n, t)
                pe.wait_ge(hn_ready.s, hn_ready.at(it, 2 * TT))
                pe.wait_ge(xa_ready.s, xa_ready.at(it, 1))
                for k in range(DC):
                    turn(ps_t[:, k, :], hn, k).then_inc(h_turned.s, 1)
                pe.wait_ge(hT_ready.s, hT_ready.at(it, DC))
                for j in range(JC):
                    m = jj(j)
                    if j >= 2:
                        pe.wait_ge(hid_ready.s, hid_ready.at(it, j - 1))
                    elif more:
                        pe.wait_ge(qn_ready.s, qn_ready.at(n, TT - 1 + j))
                    for a in range(2):
                        for k in range(DC):
                            last = pe.matmul(ps_s[0:m, pair(j) + a, :], w_1[:, k, a * HID + j * P:a * HID + j * P + m],
                                             hT[:, k, :], start=(k == 0), stop=(k == DC - 1))
                    last.then_inc(ag_proj.s, 1)
                    if more and j >= JC - TT:
                        turn_qk(n, j - JC + TT)
                pe.wait_ge(hid_ready.s, hid_ready.at(it, JC))
                if more:
                    pe.wait_ge(v_ready.s, v_ready.at(n, TT))
                for t in range(TT):
                    for j in range(JC):
                        m = jj(j)
                        last = pe.matmul(ps_y[:, t, :], hid[0:m, j, t * P:(t + 1) * P], w_2[0:m, j, :],
                                         start=(j == 0), stop=(j == JC - 1))
                last.then_inc(y_done.s, 1)

            layers(pe, None, first, body)


def add_streams(nc, base_dram, last_dram, out, NB):
    T, D = 512, 256
    TT = T // P
    with ExitStack() as ctx:
        sems = []

        def S(name, per):
            sems.append(Sem(ctx, nc, name, per))
            return sems[-1]

        one = ctx.enter_context(nc.sbuf_tensor("d_one", [P, 2, TT, D], F32))
        two = ctx.enter_context(nc.sbuf_tensor("d_two", [P, 2, TT, D], F32))
        loaded = [S(f"d_loaded{i}", 32) for i in range(2)]
        added = [S(f"d_added{i}", 1) for i in range(2)]
        stored = [S(f"d_stored{i}", 16) for i in range(2)]
        seed(nc, sems)
        tiles = lambda ap: ap.rearrange("(t p) d -> p t d", p=P)
        with nc.Block() as block:
            @block.sync
            def _(sp):
                with sp.Fori(0, NB // 2) as n:
                    for i in range(2):
                        sp.wait_ge(stored[i].s, stored[i].at(n, 0))
                        sp.dma_start(one[:, i, :, :], tiles(base_dram[n * 2 + i])).then_inc(loaded[i].s, 16)
                        sp.dma_start(two[:, i, :, :], tiles(last_dram[n * 2 + i])).then_inc(loaded[i].s, 16)

            @block.vector
            def _(dve):
                with dve.Fori(0, NB // 2) as n:
                    for i in range(2):
                        dve.wait_ge(loaded[i].s, loaded[i].at(n, 32))
                        dve.tensor_tensor(one[:, i, :, :], one[:, i, :, :], two[:, i, :, :], ALU.add).then_inc(added[i].s, 1)

            @block.scalar
            def _(act):
                with act.Fori(0, NB // 2) as n:
                    for i in range(2):
                        act.wait_ge(added[i].s, added[i].at(n, 1))
                        act.dma_start(tiles(out[n * 2 + i]), one[:, i, :, :]).then_inc(stored[i].s, 16)
                for i in range(2):
                    act.wait_ge(stored[i].s, stored[i].at(NB // 2, 0))


def build(nc, io, out, NB):
    x1_dram = nc.dram_tensor("x1_scratch", [NB, 512, 256], F32).ap()
    bc_dram = nc.dram_tensor("bc_scratch", [NB, 32, 512], F32).ap()
    base_dram = nc.dram_tensor("base_scratch", [NB, 512, 256], F32).ap()
    stream = nc.dram_tensor("stream_scratch", [3, NB, 512, 256], F32).ap()
    with ExitStack() as ctx:
        W = {"ident": ctx.enter_context(nc.sbuf_tensor("ident", [P, P], F32))}
        with ExitStack() as first:
            for name, shape in (("gateT", [P, 2, 704]), ("upT", [P, 2, 704]), ("downT", [P, 6, 256])):
                W[name] = first.enter_context(nc.sbuf_tensor(name, shape, F32))
            prepare_fp4_weights(nc, io, W)
            mamba_and_fp4_ffn(nc, io, W, x1_dram, bc_dram, NB)
        block_sparse_attention(nc, io, W, x1_dram, stream[0], base_dram, NB)
        local_attention_layers(nc, io, W, stream, NB)
        add_streams(nc, base_dram, stream[2], out, NB)


_PLAIN = ['L0_attn_conv_w', 'L0_attn_A_log', 'L0_ffn_w_gate', 'L0_ffn_w_up', 'L0_ffn_w_down',
          'L1_attn_b_qkv', 'L1_attn_b_out', 'L1_ffn_wqkv', 'L1_ffn_wo', 'L1_ffn_w1', 'L1_ffn_w2',
          'L1_ffn_q_scale', 'L1_ffn_k_scale', 'L1_ffn_b2']
_TURNED = {'W_inT': 'L0_attn_W_in', 'W_xprojT': 'L0_attn_W_xproj', 'W_dtT': 'L0_attn_W_dt', 'W_outT': 'L0_attn_W_out',
           'L1_w_qkvT': 'L1_attn_w_qkv', 'L1_w_outT': 'L1_attn_w_out'}


def _columns(v):
    return np.asarray(v).reshape(-1, P).T


def _layouts(inputs):
    a = {name: np.asarray(inputs[name]) for name in _PLAIN}
    a.update({name: np.asarray(inputs[src]).T for name, src in _TURNED.items()})
    a["mamba_cols"] = np.stack([_columns(inputs[n]) for n in ('L0_attn_conv_b', 'L0_attn_b_dt', 'L0_attn_D_param')],
                               axis=1)
    a["qk_bias_cols"] = _columns(np.asarray(inputs["L1_attn_b_qkv"])[:512])
    a["head_mask"] = np.where(np.arange(P)[:, None] % 64 // 16 == np.arange(4)[None, :], 0.25, 0.0).astype(np.float32)
    a["ln_cols"] = np.stack([np.stack([_columns(v) for v in np.asarray(inputs[n])])
                             for n in ('L1_ffn_ln_g', 'L1_ffn_ln_b')], axis=3)
    b1 = np.zeros((2, 2, 768), np.float32)
    b1[:, :, :682] = np.asarray(inputs['L1_ffn_b1']).reshape(2, 2, 682)
    a["b1_cols"] = b1.reshape(2, 2, 6, P).transpose(0, 3, 1, 2)
    a.update(_rotary_tables())
    return a


def _rotary_tables():
    n, d, window = 512, 64, 128
    f = np.float32
    half = np.arange(0, d, 2, dtype=f)
    freqs = np.arange(n, dtype=f)[:, None] * (f(1.0) / f(10000.0) ** (half / f(d)))[None, :]
    base = (half + f(0.4 * d)) / f(1.4 * d)
    scale = base[None, :] ** ((np.arange(n, dtype=f) - n // 2) / f(window // 2))[:, None]
    freqs, scale = (np.concatenate([t, t], axis=1).astype(f) for t in (freqs, scale))
    cos, sin = np.cos(freqs), np.sin(freqs)
    sin[:, :d // 2] *= -1
    qk = lambda t: np.stack([t * scale * f(8.0), t / scale], axis=1).astype(f)
    i, j = np.arange(P)[:, None], np.arange(P)[None, :]
    mask = np.concatenate([np.where(j >= i, 0.0, -1e30), np.where(j <= i, 0.0, -1e30)], axis=1).astype(f)
    return {"rot_cos": qk(cos), "rot_sin": qk(sin), "window_mask": mask}


def kernel(**inputs):
    import numpy as _np
    import concourse.bacc as _bacc
    from concourse import mybir as _mybir
    from concourse.bass_utils import run_bass_kernel_spmd as _run

    nc = _bacc.Bacc("TRN2", target_bir_lowering=False, num_devices=1)
    arrays, io = {}, {}
    named = _layouts(inputs)
    named["x"] = _np.asarray(inputs["L0_attn_x"])
    for name, a in named.items():
        a = _np.ascontiguousarray(a)
        arrays[f"in_{name}_dram"] = a
        io[name] = nc.dram_tensor(f"in_{name}_dram", a.shape, _mybir.dt.from_np(a.dtype), kind="ExternalInput").ap()
    NB = io["x"].shape[0]
    out = nc.dram_tensor("out_0_dram", (NB, 512, 256), F32, kind="ExternalOutput").ap()
    build(nc, io, out, NB)
    r = _run(nc, [arrays], core_ids=[0])
    return r.results[0]["out_0_dram"]
```
